# Optimizing a Trainium2 kernel written in Bass

```python
import numpy as np
import jax
import jax.numpy as jnp

def _softmax(x, axis=-1):
    return jax.nn.softmax(x, axis=axis)

def _gelu(x):
    return jax.nn.gelu(x, approximate=True)

def _silu(x):
    return jax.nn.silu(x)

def _sigmoid(x):
    return jax.nn.sigmoid(x)

def _layernorm(x, axis=-1, eps=1e-05):
    m = jnp.mean(x, axis=axis, keepdims=True)
    v = jnp.var(x, axis=axis, keepdims=True)
    return (x - m) / jnp.sqrt(v + eps)

def _scatter_add(tgt, idx, src, axis=0):
    return tgt.at[idx].add(src)

def _segment_sum(src, seg, n):
    return jax.ops.segment_sum(src, seg, n)
kernel_name = 'mk_flamingo_gated_d4_seqx_r8_a2549f'

def setup_inputs(seed: int=0):
    np.random.seed(seed)
    _w = jnp.asarray

    def _rec_inputs():
        import jax
        import jax.numpy as jnp
        _rk = jax.random.key(seed)
        x = -0.0002928 + 1 * jax.random.normal(jax.random.fold_in(_rk, 1), (16, 128, 256), jnp.float32)
        _lenS = 128 - jax.random.randint(jax.random.fold_in(_rk, 7), (16,), 0, max(1, 128 // 4) + 1, jnp.int32)
        _lenS2 = 128 - jax.random.randint(jax.random.fold_in(_rk, 8), (16,), 0, max(1, 128 // 4) + 1, jnp.int32)
        _ctx_2048P = jax.random.normal(jax.random.fold_in(_rk, 11), (16, 16, 256), jnp.float32)
        _ctx_2048c = jax.random.dirichlet(jax.random.fold_in(_rk, 511), 0.3 * jnp.ones((16,), jnp.float32), (16, 128))
        _ctx_2048t = jnp.einsum('bsk,bkd->bsd', _ctx_2048c, _ctx_2048P)
        _ctx_2048t = _ctx_2048t * jax.lax.rsqrt(jnp.mean(jnp.square(_ctx_2048t)) + 1e-12) * 0.953939
        ctx_2048 = -1.39393e-06 + 0.999914 * (_ctx_2048t + 0.3 * jax.random.normal(jax.random.fold_in(_rk, 611), (16, 128, 256), jnp.float32))
        _validS = jnp.arange(128)[None, :] < _lenS[:, None]
        _validS2 = jnp.arange(128)[None, :] < _lenS2[:, None]
        _causal = jnp.tril(jnp.ones((128, 128), dtype=bool))
        mask_BxSxS2_ff0 = jnp.where(jnp.ones((16, 128, 128), dtype=bool), 0.0, -1000000000.0).astype(jnp.float32)
        _g = jax.random.normal(jax.random.fold_in(_rk, 9001), (2, 4), jnp.float32)
        _g = jnp.sign(_g) * jnp.maximum(jnp.abs(_g), 1.0) + (_g == 0) * 1.0
        g_xattn = _g[0]
        g_ffn = _g[1]
        return (x, ctx_2048, mask_BxSxS2_ff0, g_xattn, g_ffn)
    x, ctx_2048, mask_BxSxS2_ff0, g_xattn, g_ffn = _rec_inputs()

    def _L0_xattn_setup():
        import jax, jax.numpy as jnp
        import numpy as np
        HID = 256
        H = 32
        HK = 8
        G = H // HK
        D = HID // H
        T = 128
        W_ATT = 32
        W_SSM = 64

        def _heads(x, n):
            B, Tt, _ = x.shape
            return x.reshape(B, Tt, n, D).transpose(0, 2, 1, 3)

        def _attend(q, k, v):
            pos = jnp.arange(T)
            rel = pos[None, :] - pos[:, None]
            slopes = jnp.power(2.0, -8.0 * jnp.arange(H, dtype=jnp.float32) / H)
            alibi = slopes[:, None, None] * rel.astype(jnp.float32)
            bias = jnp.concatenate([alibi, alibi], axis=-1)
            delta = -rel
            ssm_mask = (delta >= 0) & (delta < W_SSM)
            att_mask = (delta >= 0) & (delta < W_ATT)
            mask = jnp.concatenate([ssm_mask, att_mask], axis=-1)
            scores = jnp.einsum('bhqd,bhkd->bhqk', q, k) / np.sqrt(D).astype(np.float32)
            scores = scores + bias[None]
            scores = jnp.where(mask[None, None], scores, -jnp.inf)
            wei = jax.nn.softmax(scores, axis=-1)
            return jnp.einsum('bhqk,bhkd->bhqd', wei, v)
        key = jax.random.key(seed)
        ks = jax.random.split(key, 8)
        s = lambda fan_in: 1.0 / np.sqrt(fan_in)
        return {'hidden_states': jax.random.normal(ks[0], (2, T, HID), jnp.float32), 'ssm_states': jax.random.normal(ks[1], (2, T, HID), jnp.float32), 'Wq': jax.random.normal(ks[2], (2 * HID, HID), jnp.float32) * s(2 * HID), 'Wk': jax.random.normal(ks[3], (HID, HK * D), jnp.float32) * s(HID), 'Wv': jax.random.normal(ks[4], (HID, HK * D), jnp.float32) * s(HID), 'Wsk': jax.random.normal(ks[5], (HID, HK * D), jnp.float32) * s(HID), 'Wsv': jax.random.normal(ks[6], (HID, HK * D), jnp.float32) * s(HID), 'Wo': jax.random.normal(ks[7], (HID, HID), jnp.float32) * s(HID)}
    _L0_xattn_all = _L0_xattn_setup()
    _L0_xattn_in = {k: v for k, v in _L0_xattn_all.items() if k in ('Wq', 'Wk', 'Wv', 'Wsk', 'Wsv', 'Wo')}
    del _L0_xattn_all

    def _L0_ffn_setup():
        import jax, jax.numpy as jnp
        import numpy as np
        N_EXPERTS = 8
        TOP_K = 2
        D_MODEL = 256
        D_FF = 128
        BATCH, SEQ = (2, 256)

        def _trunc_normal(key, shape, fan_in):
            std = jnp.sqrt(1.0 / 3.0) / jnp.sqrt(float(fan_in))
            return jax.random.truncated_normal(key, -2.0, 2.0, shape, dtype=jnp.float32) * std
        key = jax.random.key(seed)
        kx, kr, k1, k2, k3 = jax.random.split(key, 5)
        x = jax.random.normal(kx, (BATCH, SEQ, D_MODEL), dtype=jnp.float32)
        router_w = jax.random.uniform(kr, (N_EXPERTS, D_MODEL), dtype=jnp.float32, minval=-1.0, maxval=1.0) / jnp.sqrt(float(D_MODEL))
        w1 = _trunc_normal(k1, (N_EXPERTS, D_MODEL, D_FF), D_MODEL)
        w2 = _trunc_normal(k2, (N_EXPERTS, D_MODEL, D_FF), D_MODEL)
        w3 = _trunc_normal(k3, (N_EXPERTS, D_FF, D_MODEL), D_FF)
        return {'x': x, 'router_w': router_w, 'w1': w1, 'w2': w2, 'w3': w3}
    _L0_ffn_all = _L0_ffn_setup()
    _L0_ffn_in = {k: v for k, v in _L0_ffn_all.items() if k in ('router_w', 'w1', 'w2', 'w3')}
    del _L0_ffn_all

    def _L1_xattn_setup():
        import jax, jax.numpy as jnp
        import numpy as np
        N_HEAD = 8
        key = jax.random.key(seed)
        k1, k2, k3 = jax.random.split(key, 3)
        B, D, L = (4, 128, 256)
        q = jax.random.normal(k1, (B, D, L), dtype=jnp.float32)
        k = jax.random.normal(k2, (B, D, L), dtype=jnp.float32)
        v = jax.random.normal(k3, (B, D, L), dtype=jnp.float32)
        gamma = jnp.ones((), dtype=jnp.float32)
        return {'q': q, 'k': k, 'v': v, 'gamma': gamma}
    _L1_xattn_all = _L1_xattn_setup()
    _L1_xattn_in = {k: v for k, v in _L1_xattn_all.items() if k in ('gamma',)}
    del _L1_xattn_all

    def _L1_ffn_setup():
        import jax, jax.numpy as jnp
        import numpy as np
        NUM_EXPERTS_PER_TOK = 2
        key = jax.random.key(seed)
        k1, k2, k3, k4 = jax.random.split(key, 4)
        B, S, D, O, E = (2, 512, 256, 256, 8)
        x = jax.random.normal(k1, (B, S, D), dtype=jnp.float32)
        gate_w = jax.random.normal(k2, (E, D), dtype=jnp.float32) * 0.02
        expert_w = jax.random.normal(k3, (E, O, D), dtype=jnp.float32) * 0.02
        expert_b = jax.random.normal(k4, (E, O), dtype=jnp.float32) * 0.02
        return {'x': x, 'gate_w': gate_w, 'expert_w': expert_w, 'expert_b': expert_b}
    _L1_ffn_all = _L1_ffn_setup()
    _L1_ffn_in = {k: v for k, v in _L1_ffn_all.items() if k in ('gate_w', 'expert_w', 'expert_b')}
    del _L1_ffn_all

    def _L2_xattn_setup():
        import jax, jax.numpy as jnp
        import numpy as np
        NUM_HEADS = 16
        EPS = 1e-08

        def _dyn_quant(x):
            s = jnp.maximum(jnp.max(jnp.abs(x), axis=-1, keepdims=True) / 127.0, EPS)
            q = jnp.clip(jnp.round(x / s), -127.0, 127.0)
            return (q, s)

        def _quant_weight(w):
            s = jnp.maximum(jnp.max(jnp.abs(w), axis=1, keepdims=True) / 127.0, EPS)
            q = jnp.clip(jnp.round(w / s), -127.0, 127.0)
            return (q, s)

        def _w8a8_linear(x, w, b):
            qx, sx = _dyn_quant(x)
            qw, sw = _quant_weight(w)
            y = jnp.einsum('bnc,oc->bno', qx, qw) * (sx * sw[:, 0])
            return y + b
        key = jax.random.key(seed)
        ks = jax.random.split(key, 9)
        B, N, L, C = (2, 512, 64, 256)
        sc = 0.02
        return {'x': jax.random.normal(ks[0], (B, N, C), jnp.float32), 'cond': jax.random.normal(ks[1], (B, L, C), jnp.float32), 'mask': jnp.zeros((B, N, L), jnp.float32), 'wq': jax.random.normal(ks[2], (C, C), jnp.float32) * sc, 'bq': jnp.zeros((C,), jnp.float32), 'wk': jax.random.normal(ks[3], (C, C), jnp.float32) * sc, 'bk': jnp.zeros((C,), jnp.float32), 'wv': jax.random.normal(ks[4], (C, C), jnp.float32) * sc, 'bv': jnp.zeros((C,), jnp.float32), 'wo': jax.random.normal(ks[5], (C, C), jnp.float32) * sc, 'bo': jnp.zeros((C,), jnp.float32)}
    _L2_xattn_all = _L2_xattn_setup()
    _L2_xattn_in = {k: v for k, v in _L2_xattn_all.items() if k in ('wq', 'bq', 'wk', 'bk', 'wv', 'bv', 'wo', 'bo')}
    del _L2_xattn_all

    def _L2_ffn_setup():
        import math
        import jax, jax.numpy as jnp
        import numpy as np
        DIM = 256
        RANK = 8
        B, T = (4, 512)

        def _orthogonal(key, n):
            a = jax.random.normal(key, (n, n), dtype=jnp.float32)
            q, r = jnp.linalg.qr(a)
            q = q * jnp.sign(jnp.diagonal(r))[None, :]
            return q
        key = jax.random.key(seed)
        kx, kf = jax.random.split(key)
        x = jax.random.normal(kx, (B, T, DIM), dtype=jnp.float32)
        fkeys = jax.random.split(kf, RANK)
        factors = jnp.stack([_orthogonal(fkeys[r], DIM) * (r + 1) ** (-0.5) for r in range(RANK)])
        bias = jnp.zeros((DIM,), dtype=jnp.float32)
        return {'x': x, 'factors': factors, 'bias': bias}
    _L2_ffn_all = _L2_ffn_setup()
    _L2_ffn_in = {k: v for k, v in _L2_ffn_all.items() if k in ('factors', 'bias')}
    del _L2_ffn_all

    def _L3_xattn_setup():
        import jax, jax.numpy as jnp
        import numpy as np
        from math import sqrt
        key = jax.random.key(seed)
        kq, kk, kv = jax.random.split(key, 3)
        B, D, N = (8, 128, 256)
        Q = jax.random.normal(kq, (B, D, N), dtype=jnp.float32)
        K = jax.random.normal(kk, (B, D, N), dtype=jnp.float32)
        V = jax.random.normal(kv, (B, D, N), dtype=jnp.float32)
        return {'Q': Q, 'K': K, 'V': V}
    _L3_xattn_all = _L3_xattn_setup()
    _L3_xattn_in = {k: v for k, v in _L3_xattn_all.items() if k in ()}
    del _L3_xattn_all

    def _L3_ffn_setup():
        import jax, jax.numpy as jnp
        import numpy as np
        B, S, D = (2, 256, 256)
        E = 8
        TOPK = 2
        H_SHARED = 1024
        H_ROUTED = 128
        STD = 0.02
        key = jax.random.key(seed)
        ks = jax.random.split(key, 7)
        return {'x': jax.random.normal(ks[0], (B, S, D), jnp.float32), 'w12': jax.random.normal(ks[1], (E, 2 * H_ROUTED, D), jnp.float32) * STD, 'w3': jax.random.normal(ks[2], (E, D, H_ROUTED), jnp.float32) * STD, 'router_w': jax.random.normal(ks[3], (E, D), jnp.float32) * STD, 'expert_bias': jnp.zeros((E,), jnp.float32), 'sw1': jax.random.normal(ks[4], (H_SHARED, D), jnp.float32) * STD, 'sw2': jax.random.normal(ks[5], (H_SHARED, D), jnp.float32) * STD, 'sw3': jax.random.normal(ks[6], (D, H_SHARED), jnp.float32) * STD}
    _L3_ffn_all = _L3_ffn_setup()
    _L3_ffn_in = {k: v for k, v in _L3_ffn_all.items() if k in ('w12', 'w3', 'router_w', 'expert_bias', 'sw1', 'sw2', 'sw3')}
    del _L3_ffn_all
    return {'x': x, 'ctx_2048': ctx_2048, 'mask_BxSxS2_ff0': mask_BxSxS2_ff0, 'g_xattn': g_xattn, 'g_ffn': g_ffn, 'L0_xattn_Wq': _L0_xattn_in['Wq'], 'L0_xattn_Wk': _L0_xattn_in['Wk'], 'L0_xattn_Wv': _L0_xattn_in['Wv'], 'L0_xattn_Wsk': _L0_xattn_in['Wsk'], 'L0_xattn_Wsv': _L0_xattn_in['Wsv'], 'L0_xattn_Wo': _L0_xattn_in['Wo'], 'L0_ffn_router_w': _L0_ffn_in['router_w'], 'L0_ffn_w1': _L0_ffn_in['w1'], 'L0_ffn_w2': _L0_ffn_in['w2'], 'L0_ffn_w3': _L0_ffn_in['w3'], 'L1_xattn_gamma': _L1_xattn_in['gamma'], 'L1_ffn_gate_w': _L1_ffn_in['gate_w'], 'L1_ffn_expert_w': _L1_ffn_in['expert_w'], 'L1_ffn_expert_b': _L1_ffn_in['expert_b'], 'L2_xattn_wq': _L2_xattn_in['wq'], 'L2_xattn_bq': _L2_xattn_in['bq'], 'L2_xattn_wk': _L2_xattn_in['wk'], 'L2_xattn_bk': _L2_xattn_in['bk'], 'L2_xattn_wv': _L2_xattn_in['wv'], 'L2_xattn_bv': _L2_xattn_in['bv'], 'L2_xattn_wo': _L2_xattn_in['wo'], 'L2_xattn_bo': _L2_xattn_in['bo'], 'L2_ffn_factors': _L2_ffn_in['factors'], 'L2_ffn_bias': _L2_ffn_in['bias'], 'L3_ffn_w12': _L3_ffn_in['w12'], 'L3_ffn_w3': _L3_ffn_in['w3'], 'L3_ffn_router_w': _L3_ffn_in['router_w'], 'L3_ffn_expert_bias': _L3_ffn_in['expert_bias'], 'L3_ffn_sw1': _L3_ffn_in['sw1'], 'L3_ffn_sw2': _L3_ffn_in['sw2'], 'L3_ffn_sw3': _L3_ffn_in['sw3']}

def reference(x, ctx_2048, mask_BxSxS2_ff0, g_xattn, g_ffn, L0_xattn_Wq, L0_xattn_Wk, L0_xattn_Wv, L0_xattn_Wsk, L0_xattn_Wsv, L0_xattn_Wo, L0_ffn_router_w, L0_ffn_w1, L0_ffn_w2, L0_ffn_w3, L1_xattn_gamma, L1_ffn_gate_w, L1_ffn_expert_w, L1_ffn_expert_b, L2_xattn_wq, L2_xattn_bq, L2_xattn_wk, L2_xattn_bk, L2_xattn_wv, L2_xattn_bv, L2_xattn_wo, L2_xattn_bo, L2_ffn_factors, L2_ffn_bias, L3_ffn_w12, L3_ffn_w3, L3_ffn_router_w, L3_ffn_expert_bias, L3_ffn_sw1, L3_ffn_sw2, L3_ffn_sw3):
    import jax
    import jax.numpy as jnp

    def _L0_xattn_ref(hidden_states, ssm_states, Wq, Wk, Wv, Wsk, Wsv, Wo):
        import jax, jax.numpy as jnp
        import numpy as np
        HID = 256
        H = 32
        HK = 8
        G = H // HK
        D = HID // H
        T = 128
        W_ATT = 32
        W_SSM = 64

        def _heads(x, n):
            B, Tt, _ = x.shape
            return x.reshape(B, Tt, n, D).transpose(0, 2, 1, 3)

        def _attend(q, k, v):
            pos = jnp.arange(T)
            rel = pos[None, :] - pos[:, None]
            slopes = jnp.power(2.0, -8.0 * jnp.arange(H, dtype=jnp.float32) / H)
            alibi = slopes[:, None, None] * rel.astype(jnp.float32)
            bias = jnp.concatenate([alibi, alibi], axis=-1)
            delta = -rel
            ssm_mask = (delta >= 0) & (delta < W_SSM)
            att_mask = (delta >= 0) & (delta < W_ATT)
            mask = jnp.concatenate([ssm_mask, att_mask], axis=-1)
            scores = jnp.einsum('bhqd,bhkd->bhqk', q, k) / np.sqrt(D).astype(np.float32)
            scores = scores + bias[None]
            scores = jnp.where(mask[None, None], scores, -jnp.inf)
            wei = jax.nn.softmax(scores, axis=-1)
            return jnp.einsum('bhqk,bhkd->bhqd', wei, v)
        B = hidden_states.shape[0]
        q = _heads(jnp.concatenate([ssm_states, hidden_states], axis=-1) @ Wq, H)
        k = _heads(hidden_states @ Wk, HK)
        v = _heads(hidden_states @ Wv, HK)
        ssm_k = _heads(ssm_states @ Wsk, HK)
        ssm_v = _heads(ssm_states @ Wsv, HK)
        rep = lambda x: jnp.repeat(x, G, axis=1)
        kcat = jnp.concatenate([rep(ssm_k), rep(k)], axis=2)
        vcat = jnp.concatenate([rep(ssm_v), rep(v)], axis=2)
        o = _attend(q, kcat, vcat)
        o = o.transpose(0, 2, 1, 3).reshape(B, T, HID)
        return o @ Wo

    def _L0_ffn_ref(x, router_w, w1, w2, w3):
        import jax, jax.numpy as jnp
        import numpy as np
        N_EXPERTS = 8
        TOP_K = 2
        D_MODEL = 256
        D_FF = 128
        BATCH, SEQ = (2, 256)

        def _trunc_normal(key, shape, fan_in):
            std = jnp.sqrt(1.0 / 3.0) / jnp.sqrt(float(fan_in))
            return jax.random.truncated_normal(key, -2.0, 2.0, shape, dtype=jnp.float32) * std
        B, S, D = x.shape
        xf = x.reshape(-1, D)
        n_tokens = xf.shape[0]
        logits = xf @ router_w.T
        topk_vals, topk_idx = jax.lax.top_k(logits, TOP_K)
        topk_weights = jax.nn.softmax(topk_vals, axis=-1)
        gate = jax.nn.silu(jnp.einsum('nd,edf->enf', xf, w1))
        value = jnp.einsum('nd,edf->enf', xf, w2)
        expert_out = jnp.einsum('enf,efd->end', gate * value, w3)
        tok = jnp.arange(n_tokens)[:, None]
        selected = expert_out[topk_idx, tok]
        out = jnp.sum(selected * topk_weights[..., None], axis=1)
        return out.reshape(B, S, D)

    def _L1_xattn_ref(q, k, v, gamma):
        import jax, jax.numpy as jnp
        import numpy as np
        N_HEAD = 8
        B, Dq, Lq = q.shape
        Dv, Lk = (v.shape[-2], v.shape[-1])
        h = N_HEAD
        dq = Dq // h
        dv = Dv // h
        qh = q.reshape(B, h, dq, Lq)
        kh = k.reshape(B, h, dq, Lk)
        vh = v.reshape(B, h, dv, Lk)
        scale = 1.0 / jnp.sqrt(jnp.asarray(dq, dtype=q.dtype))
        qk = jnp.einsum('bhdq,bhdl->bhql', qh, kh) * scale
        sm = jax.nn.softmax(qk, axis=-1)
        ret = jnp.einsum('bhql,bhdl->bhdq', sm, vh)
        ret = ret.reshape(B, Dv, Lq)
        return gamma * ret

    def _L1_ffn_ref(x, gate_w, expert_w, expert_b):
        import jax, jax.numpy as jnp
        import numpy as np
        NUM_EXPERTS_PER_TOK = 2
        E = gate_w.shape[0]
        O = expert_w.shape[1]
        gate_logits = jnp.einsum('bsd,ed->bse', x, gate_w)
        topk_vals, topk_idx = jax.lax.top_k(gate_logits, NUM_EXPERTS_PER_TOK)
        weights = jax.nn.softmax(topk_vals.astype(jnp.float32), axis=-1).astype(x.dtype)
        dense_w = jnp.sum(jax.nn.one_hot(topk_idx, E, dtype=x.dtype) * weights[..., None], axis=2)
        out = jnp.zeros(x.shape[:2] + (O,), dtype=x.dtype)
        for e in range(E):
            y_e = jnp.einsum('bsd,od->bso', x, expert_w[e]) + expert_b[e]
            out = out + dense_w[..., e:e + 1] * y_e
        return out

    def _L2_xattn_ref(x, cond, mask, wq, bq, wk, bk, wv, bv, wo, bo):
        import jax, jax.numpy as jnp
        import numpy as np
        NUM_HEADS = 16
        EPS = 1e-08

        def _dyn_quant(x):
            s = jnp.maximum(jnp.max(jnp.abs(x), axis=-1, keepdims=True) / 127.0, EPS)
            q = jnp.clip(jnp.round(x / s), -127.0, 127.0)
            return (q, s)

        def _quant_weight(w):
            s = jnp.maximum(jnp.max(jnp.abs(w), axis=1, keepdims=True) / 127.0, EPS)
            q = jnp.clip(jnp.round(w / s), -127.0, 127.0)
            return (q, s)

        def _w8a8_linear(x, w, b):
            qx, sx = _dyn_quant(x)
            qw, sw = _quant_weight(w)
            y = jnp.einsum('bnc,oc->bno', qx, qw) * (sx * sw[:, 0])
            return y + b
        B, N, C = x.shape
        L = cond.shape[1]
        H = NUM_HEADS
        D = C // H
        inv_sqrt_d = np.float32(1.0 / np.sqrt(D))
        q = _w8a8_linear(x, wq, bq).reshape(B, N, H, D).transpose(0, 2, 1, 3)
        k = (cond @ wk.T + bk).reshape(B, L, H, D).transpose(0, 2, 1, 3)
        v = (cond @ wv.T + bv).reshape(B, L, H, D).transpose(0, 2, 1, 3)
        scores = jnp.einsum('bhnd,bhld->bhnl', q, k) * inv_sqrt_d + mask[:, None]
        attn = jax.nn.softmax(scores, axis=-1)
        o = jnp.einsum('bhnl,bhld->bhnd', attn, v)
        o = o.transpose(0, 2, 1, 3).reshape(B, N, C)
        return _w8a8_linear(o, wo, bo)

    def _L2_ffn_ref(x, factors, bias):
        import math
        import jax, jax.numpy as jnp
        import numpy as np
        DIM = 256
        RANK = 8
        B, T = (4, 512)

        def _orthogonal(key, n):
            a = jax.random.normal(key, (n, n), dtype=jnp.float32)
            q, r = jnp.linalg.qr(a)
            q = q * jnp.sign(jnp.diagonal(r))[None, :]
            return q
        rank = factors.shape[0]
        mixed = jnp.einsum('btd,rde->bte', x, factors)
        mixed = mixed / math.sqrt(rank) + bias
        return mixed

    def _L3_xattn_ref(Q, K, V):
        import jax, jax.numpy as jnp
        import numpy as np
        from math import sqrt
        dk = Q.shape[1]
        x = jnp.einsum('bdn,bdm->bnm', Q, K) / sqrt(dk)
        score = jax.nn.sigmoid(x)
        out = jnp.einsum('bvn,bnm->bvm', V, score)
        return out

    def _L3_ffn_ref(x, w12, w3, router_w, expert_bias, sw1, sw2, sw3):
        import jax, jax.numpy as jnp
        import numpy as np
        B, S, D = (2, 256, 256)
        E = 8
        TOPK = 2
        H_SHARED = 1024
        H_ROUTED = 128
        STD = 0.02
        b, s, d = x.shape
        g = x @ sw1.T
        u = x @ sw2.T
        shared_out = jax.nn.silu(g) * u @ sw3.T
        scores = jax.nn.sigmoid(x @ router_w.T)
        selection_scores = scores + expert_bias
        _, top_idx = jax.lax.top_k(selection_scores, TOPK)
        top_scores = jnp.take_along_axis(scores, top_idx, axis=-1)
        top_scores = top_scores / (top_scores.sum(-1, keepdims=True) + 1e-09)
        flat_x = x.reshape(-1, d)
        T = flat_x.shape[0]
        flat_idx = top_idx.reshape(T, TOPK)
        flat_sc = top_scores.reshape(T, TOPK)
        combine = jnp.zeros((T, E), x.dtype).at[jnp.arange(T)[:, None], flat_idx].add(flat_sc)
        h12 = jnp.einsum('td,ehd->teh', flat_x, w12)
        h1, h2 = jnp.split(h12, 2, axis=-1)
        h = jax.nn.silu(h1) * h2
        out_e = jnp.einsum('teh,edh->ted', h, w3)
        routed_out = jnp.einsum('ted,te->td', out_e, combine).reshape(b, s, d)
        return shared_out + routed_out
    x = x + jnp.tanh(g_xattn[0]) * _L0_xattn_ref(_layernorm(x, axis=-1), ctx_2048, L0_xattn_Wq, L0_xattn_Wk, L0_xattn_Wv, L0_xattn_Wsk, L0_xattn_Wsv, L0_xattn_Wo)
    x = x + jnp.tanh(g_ffn[0]) * _L0_ffn_ref(_layernorm(x, axis=-1), L0_ffn_router_w, L0_ffn_w1, L0_ffn_w2, L0_ffn_w3)
    x = x + jnp.tanh(g_xattn[1]) * _L1_xattn_ref(_layernorm(x, axis=-1), ctx_2048, ctx_2048, L1_xattn_gamma)
    x = x + jnp.tanh(g_ffn[1]) * _L1_ffn_ref(_layernorm(x, axis=-1), L1_ffn_gate_w, L1_ffn_expert_w, L1_ffn_expert_b)
    x = x + jnp.tanh(g_xattn[2]) * _L2_xattn_ref(_layernorm(x, axis=-1), ctx_2048, mask_BxSxS2_ff0, L2_xattn_wq, L2_xattn_bq, L2_xattn_wk, L2_xattn_bk, L2_xattn_wv, L2_xattn_bv, L2_xattn_wo, L2_xattn_bo)
    x = x + jnp.tanh(g_ffn[2]) * _L2_ffn_ref(_layernorm(x, axis=-1), L2_ffn_factors, L2_ffn_bias)
    x = x + jnp.tanh(g_xattn[3]) * _L3_xattn_ref(_layernorm(x, axis=-1), ctx_2048, ctx_2048)
    x = x + jnp.tanh(g_ffn[3]) * _L3_ffn_ref(_layernorm(x, axis=-1), L3_ffn_w12, L3_ffn_w3, L3_ffn_router_w, L3_ffn_expert_bias, L3_ffn_sw1, L3_ffn_sw2, L3_ffn_sw3)
    return x

_drawn_inputs = setup_inputs


def setup_inputs(seed=0):
    import zlib

    import numpy as np

    out = dict(_drawn_inputs(seed))
    spreads = {'L2_xattn_bq': (0.0, 0.8),
     'L2_xattn_bk': (0.0, 0.8),
     'L2_xattn_bv': (0.0, 0.1),
     'L2_xattn_bo': (0.0, 0.1),
     'L2_ffn_bias': (0.0, 0.1),
     'L3_ffn_expert_bias': (0.0, 0.8)}
    factors = {'g_ffn': 8.0,
     'L0_ffn_router_w': 3.088,
     'L0_ffn_w1': 2.801,
     'L0_ffn_w2': 2.872,
     'L0_ffn_w3': 2.831,
     'L1_ffn_expert_b': 3.415,
     'L2_xattn_wq': 8.0,
     'L2_xattn_wk': 8.0,
     'L3_ffn_w12': 8.0,
     'L3_ffn_w3': 8.0,
     'L3_ffn_router_w': 8.0,
     'L3_ffn_sw1': 8.0,
     'L3_ffn_sw2': 8.0,
     'L3_ffn_sw3': 8.0}
    for name, (base, spread) in spreads.items():
        noise = np.random.default_rng([zlib.crc32(name.encode()), seed]).standard_normal(out[name].shape)
        drawn = base * np.exp(spread * noise) if base else spread * noise
        out[name] = jnp.asarray(drawn.astype(out[name].dtype))
    for name, factor in factors.items():
        out[name] = (out[name] * factor).astype(out[name].dtype)
    return out
```

```python
import numpy as np
from contextlib import ExitStack

import concourse.bass as bass
from concourse import mybir

F32 = mybir.dt.float32
BF16 = mybir.dt.bfloat16
U32 = mybir.dt.uint32
ALU = mybir.AluOpType
ACT = mybir.ActivationFunctionType
AX = mybir.AxisListType

NB = 16
T = 128
C = 256
NC = C // 128
EPS_LN = 1e-5

H0, HK0, D0 = 32, 8, 8
G0 = H0 // HK0
QB = 32
NQB = T // QB
W_SSM, W_ATT = 64, 32
R0 = 64
MASKED = -1e30
KEYS_T = [64, 64, 128, 128]
KEYS_Q = [(0, 32), (0, 64), (0, 96), (32, 96)]
FILLS_Q = [(0, 0, 4), (1, 0, 4), (2, 0, 2), (2, 2, 2), (3, 0, 2), (3, 2, 2)]
FILLS_T = [(0, 2), (1, 2), (2, 0), (2, 1), (3, 0), (3, 1)]

TOP_E = 8


class Flag:

    def __init__(self, sem, per, credit=0, base=0):
        self.sem, self.per, self.credit = sem, per, base + credit
        self.given = credit

    def at(self, item, k):
        return item * self.per + (k + self.credit)


def bass_program(nc, a, out, n_stages=8):
    ctx = ExitStack()
    with ctx:
        def sb(name, shape, dt=F32):
            return ctx.enter_context(nc.sbuf_tensor(name, shape, dt))

        def sem(name):
            return ctx.enter_context(nc.semaphore(name))

        def flag(name, per, credit=0):
            return Flag(sem(name), per, credit)

        psum = ctx.enter_context(nc.psum_tensor("psum", [128, 8 * 512], F32))

        def bank(n, k=1):
            return psum[:, 512 * n:512 * (n + k)]

        x = sb("x", [128, NB, C])
        ident = sb("ident", [128, 128])
        identb = sb("identb", [128, 128], BF16)
        gates = sb("gates", [128, 9])
        loaded_x = sem("loaded_x")
        loaded_c = sem("loaded_c")
        gates_ready = sem("gates_ready")
        x_done = Flag(sem("x_done"), 1)
        stats = sb("stats", [128, 4, 6])
        mv = sb("mv", [128, 4, 2])
        veps = sb("veps", [128, 4, 1])
        rstd = sb("rstd", [128, 4, 1])
        minus_half = sb("minus_half", [128, 1])
        xn = sb("xn", [128, 2, 2, C])
        xnT = sb("xnT", [128, 2, NC, 2 * T])
        zero_ready = sem("zero_ready")
        waited = sem("waited")

        w_attn = sb("w_attn", [128, 2560])
        w0x = w_attn[:, 0:768].rearrange("p (c n) -> p c n", c=NC)
        w0c = w_attn[:, 768:1536].rearrange("p (c n) -> p c n", c=NC)
        w0o = w_attn[0:64, 1536:2560].rearrange("p (g n) -> p g n", g=G0)
        ext0 = sb("ext0", [128, HK0 * sum(2 * k for k in KEYS_T)], BF16)
        mxq0 = sb("mxq0", [128, 128], BF16)
        ohq0 = sb("ohq0", [128, 128], BF16)
        ctxT = sb("ctxT", [128, 2, NC, T])
        q_f = sb("q_f", [128, 2, C])
        kv_f = sb("kv_f", [128, 2, 2, 128])
        q_r = sb("q_r", [128, C])
        k_r = sb("k_r", [128, 128])
        q_parts = sb("q_parts", [128, 2, H0, R0], BF16)
        k_parts = sb("k_parts", [128, 2, 2, HK0, R0], BF16)
        qT0 = sb("qT0", [128, HK0 // 2, NQB, G0, QB], BF16)
        kT0 = sb("kT0", [128, HK0 // 2, 2, T], BF16)
        v0 = sb("v0", [128, 2, 3, HK0, D0 + 1])
        mx0 = sb("mx0", [128, NQB, HK0 // 2, 2])
        mxr0 = sb("mxr0", [128, 32])
        mxp0 = sb("mxp0", [128, 3, 32], BF16)
        PT = sb("PT", [128, 12 * 512])
        rden = sb("rden", [128, 32])
        o_n = sb("o_n", [128, NQB, 64])
        oT0 = sb("oT0", [64, G0, T])

        arena = sb("arena", [128, 12288])
        w1a = arena[:, 0:4096].rearrange("p (e c v m) -> p e c v m", e=TOP_E, c=NC, v=2)
        w1b = arena[:, 4096:6144].rearrange("p (e n) -> p e n", e=TOP_E)
        w3e = arena[:, 6144:10240].rearrange("p (c n) -> p c n", c=NC)
        w7a = arena[:, 0:8192].rearrange("p (e c v m) -> p e c v m", e=16, c=NC, v=2)
        w7b = arena[:, 8192:12288].rearrange("p (e n) -> p e n", e=16)
        wr = sb("wr", [128, 3, NC, TOP_E])
        iota8 = sb("iota8", [128, TOP_E])
        ebias = sb("ebias", [96, TOP_E * C], BF16)
        ones96 = sb("ones96", [96, 128], BF16)
        sbias = sb("sbias", [128, TOP_E])
        staging = PT[:, 0:4096]
        half = sb("half", [128, 2, 9])
        lg = sb("lg", [128, 2, TOP_E])
        sg8 = sb("sg8", [128, 2, TOP_E])
        sel8 = sb("sel8", [128, 2, TOP_E])
        v8 = sb("v8", [128, 2, 8])
        i8 = sb("i8", [128, 2, 8], U32)
        idf = sb("idf", [128, 2, 2])
        dl = sb("dl", [128, 2, 1])
        th = sb("th", [128, 2, 8])
        wk = sb("wk", [128, 2, 2])
        den = sb("den", [128, 2, 1])
        oh = sb("oh", [128, 2, 2, TOP_E])
        ohs = sb("ohs", [128, 2, 2, TOP_E])
        cw = sb("cw", [128, 2, TOP_E])
        sil = sb("sil", [128, 2, 2 * T])
        hT = sb("hT", [128, 2, 2 * T])
        qop = ext0[0:96, 0:4096].rearrange("p (s h n) -> p s h n", s=2, h=8)
        kop = q_parts[:].rearrange("p s h r -> p (s h r)")[0:96].rearrange("p (s h n) -> p s h n", s=2, h=8)
        xparts = sb("xparts", [128, 2, 3, C], BF16)
        xres = sb("xres", [128, C])
        vT2 = sb("vT2", [128, 2, 2, 8, 17])
        sel2 = sb("sel2", [96, 8, 128], BF16)
        mxq2 = sb("mxq2", [96, C], BF16)
        mx2 = sb("mx2", [128, 2, 8])
        mxr2 = sb("mxr2", [128, 2, 8])
        mxp2 = sb("mxp2", [128, 2, 3, 8], BF16)
        gg = sb("gg", [128, 1])
        cnat = sb("cnat", [128, 2, C])
        cparts = sb("cparts", [128, 2, 3, C], BF16)
        cres = sb("cres", [128, C])
        wkT = w_attn[:, 0:1024].rearrange("p (c g m) -> p c g m", c=NC, g=4)
        wvT = w_attn[:, 1024:1536].rearrange("p (c n) -> p c n", c=NC)
        sel4 = w_attn[0:96, 1536:2560].bitcast(BF16).rearrange("p (h m) -> p h m", h=16)
        bkc = sb("bkc", [128, 4])
        rows4 = sb("rows4", [128, 5, C])
        qwT = sb("qwT", [128, 2, NC, C], BF16)
        qw = sb("qw", [128, 2, 2, C], BF16)
        wsc = sb("wsc", [128, 4, 2, 2])
        diag = staging[:, 1024:1536].rearrange("p (n m) -> p n m", n=4)
        onesf = sb("onesf", [128, 128])
        qsc = sb("qsc", [128, 2, 4])
        qt_f = sb("qt_f", [128, C])
        qx = sb("qx", [128, C], BF16)
        qxT = sb("qxT", [128, NC, T], BF16)
        q_tmp = sb("q_tmp", [128, C])
        qpad = sb("qpad", [128, 16, 32])
        qT4 = qT0[:].rearrange("p j b g q -> p (j b g q)").bitcast(F32).rearrange("p (s g t) -> p s g t", s=2, g=4)
        kT4 = sb("kT4", [128, 2, 4, T])
        v4 = sb("v4", [128, 2, 16, 17])
        mskq = sb("mskq", [128, 2, T])
        mskT = sb("mskT", [128, 2, T])
        mxq4 = sb("mxq4", [96, 128], BF16)
        mx4 = sb("mx4", [128, 16])
        mxr4 = sb("mxr4", [128, 16])
        mxp4 = sb("mxp4", [128, 3, 16], BF16)
        osc = sb("osc", [128, 4])
        fsum = sb("fsum", [128, NC, C])
        fb = sb("fb", [128, C])
        gs5 = sb("gs5", [128, 1])

        qo = sb("qo", [128, C], BF16)
        qoT = sb("qoT", [128, NC, T], BF16)
        eb_f = PT[0:96, 0:2048]
        eb_r = PT[0:96, 2048:4096]
        eb_b = PT[0:96, 4096:5120].bitcast(BF16)

        kscr = nc.dram_tensor("kscr", (NB, 3, 128, C), BF16, kind="Internal").ap()
        qscr = nc.dram_tensor("qscr", (2, 3, 128, C), BF16, kind="Internal").ap()
        ends = {}
        w_loaded = [sem(f"w_loaded{k}") for k in range(8)]
        prep_w = Flag(sem("prep_w"), 0)

        f = {}
        shared = {}

        def stage_flags(s, names, n_items=NB):
            for n, per, credit in names:
                count = NB // 2 if n[-1] in "01" else NB if (n, per, credit) in LN else n_items
                if (n, credit) not in shared:
                    shared[n, credit] = [sem(n + (f"_{credit}" if credit else "")), 0]
                entry = shared[n, credit]
                f[s, n] = Flag(entry[0], per, credit, entry[1])
                entry[1] += per * count

        given = set()

        def give(eng, keys):
            for key in keys:
                fl = f.get(key)
                if fl and fl.given and (key[1], fl.given) not in given:
                    given.add((key[1], fl.given))
                    eng.sem_inc(fl.sem, fl.given)

        LN = [("stats", 1, 0), ("mv", 1, 0), ("veps", 1, 0), ("rstd", 1, 0), ("xn", 1, 0)]

        stage_flags(0, [
            ("ctx_loaded0", 16, 0), ("ctx_loaded1", 16, 0),
            ("stats", 1, 0), ("mv", 1, 0), ("veps", 1, 0), ("rstd", 1, 0), ("xn", 1, 0), ("xnT_psum", 1, 0), ("xnT", 1, 0),
            ("qkv_psum", 1, 0), ("qkv", 2, 0), ("parts", 8, 0), ("kT_psum", 1, 0), ("qT_psum", 2, 0), ("qkT", 3, 0),
            ("v", 2, 0), ("sq", 6, 0), ("mx", 6, 0), ("mparts", 4, 0), ("mxT_psum", 1, 0), ("mxT", 1, 0),
            ("st", 6, 0), ("p", 6, 2), ("pv", 1, 0), ("rden", 1, 0), ("on", 1, 0), ("oT_psum", 1, 0), ("oT", 1, 0), ("y", 1, 0)])


        def ff_flags(s):
            n = {1: 8, 3: 4, 5: 1, 7: 16}[s]
            names = LN + [("xnT_psum", 1, 0), ("xnT", 1, 0), ("y", n, 2 if s in (1, 7) else 0),
                          ("acc", {1: 8, 3: 16, 5: 1, 7: 9}[s], {1: 2, 3: 8, 5: 2, 7: 2}[s])]
            if s == 5:
                names += [("bias", 1, 0)]
            else:
                names += [("lg_psum", 1, 0), ("lg", 1, 1), ("route", {1: 10, 3: 10, 7: 16}[s], 0), ("tanh", 1, 0)]
            if s in (1, 7):
                names += [("up", n, 0), ("silu", n, 0), ("h", n, 2)]
            stage_flags(s, names, NB // 2)

        ff_flags(1)
        stage_flags(2, LN + [("parts", 5, 0), ("q_stored0", 16, 0), ("q_stored1", 16, 0), ("q_loaded0", 96, 0), ("q_loaded1", 96, 0),
                             ("k_loaded0", 112, 0), ("k_loaded1", 112, 0),
                             ("sq", 4, 0), ("mx", 4, 0), ("mparts", 4, 0), ("mxT_psum", 1, 0), ("mxT", 1, 0), ("st", 4, 0), ("p", 4, 2),
                             ("pv", 1, 0), ("rden", 1, 0), ("on", 1, 0), ("y", 1, 0)])
        ff_flags(3)
        stage_flags(4, LN + [("ctx_loaded0", 48, 0), ("ctx_loaded1", 48, 0), ("quant", 6, 0), ("xT_psum", 1, 0), ("xT", 1, 0), ("q_psum", 1, 0), ("k_psum", 1, 0),
                             ("qdve", 3, 0), ("k", 4, 0), ("qT_psum", 1, 0), ("qT", 1, 0), ("sq", 2, 0), ("mx", 2, 0), ("mparts", 4, 0),
                             ("mxT_psum", 1, 0), ("mxT", 1, 0), ("st", 2, 0), ("p", 2, 2), ("pv", 1, 0), ("rden", 1, 0), ("on", 1, 0),
                             ("oquant", 6, 0), ("oT_psum", 1, 0), ("oT", 1, 0), ("y", 1, 0), ("fin", 2, 0)])
        ff_flags(5)
        stage_flags(6, LN + [("ctx_loaded0", 32, 0), ("ctx_loaded1", 32, 0), ("s_psum", 1, 0), ("s", 1, 0), ("y", 1, 0)])
        ff_flags(7)
        ends[0] = (x_done.sem, NB)
        for s in (1, 3, 5, 7):
            fl = f[s, "acc"]
            ends[s] = (fl.sem, fl.at(NB // 2, 0))
        for n, s in enumerate((2, 4, 6)):
            ends[s] = (x_done.sem, NB * (n + 2))

        block = ctx.enter_context(nc.Block())

        def items(eng, front, back, n=NB, unroll=2):
            front(0, 0, 0)
            with eng.Fori(0, n // unroll - 1) as i:
                for u in range(unroll):
                    back(i * unroll + u, u % 2, lambda v=u: front(i * unroll + (v + 1), (v + 1) % 2, i + (v + 1) // 2))
            for b in range(n - unroll, n):
                nxt = (lambda v=b: front(v + 1, (v + 1) % 2, (v + 1) // 2)) if b + 1 < n else (lambda: None)
                back(b, b % 2, nxt)

        def plain(eng):
            eng.sem_inc(waited, 1)

        def s0_sp(sp):
            F = lambda n: f[0, n]
            def load(b, s):
                sp.dma_start(ctxT[:, s], a["ctxT"][:, b]).then_inc(F(f"ctx_loaded{s}").sem, 16)
            load(0, 0)
            load(1, 1)
            with sp.Fori(0, NB // 2 - 1) as i:
                for u in range(2):
                    sp.wait_ge(F("qkv_psum").sem, F("qkv_psum").at(i * 2 + u, 1))
                    load(i * 2 + (u + 2), u)

        def ln_stats(s, dve, b, slot, i4):
            F = lambda n: f[s, n]
            nc.vector.bn_stats(stats[:, i4], x[:, b]).then_inc(F("stats").sem, 1)
            dve.wait_ge(F("stats").sem, F("stats").at(b, 1))
            plain(dve)
            nc.vector.bn_aggr(mv[:, i4], stats[:, i4]).then_inc(F("mv").sem, 1)

        def ln_apply(s, dve, b, i4, out_):
            F = lambda n: f[s, n]
            dve.wait_ge(F("rstd").sem, F("rstd").at(b, 1))
            nc.vector.tensor_scalar(out_, x[:, b], mv[:, i4, 0:1], rstd[:, i4], ALU.subtract, ALU.mult).then_inc(F("xn").sem, 1)

        def rstd_step(st, pool):
            F = lambda n: f[st, n]

            def rs(b, s):
                pool.wait_ge(F("mv").sem, F("mv").at(b, 1))
                plain(pool)
                nc.gpsimd.tensor_scalar(veps[:, s], mv[:, s, 1:2], EPS_LN, None, ALU.add).then_inc(F("veps").sem, 1)
                pool.wait_ge(F("veps").sem, F("veps").at(b, 1))
                nc.gpsimd.tensor_tensor(rstd[:, s], veps[:, s], minus_half[:], ALU.pow).then_inc(F("rstd").sem, 1)
            return rs

        def pool_stage(st, pool):
            rs = rstd_step(st, pool)
            step = 4 if st % 2 else 2
            with pool.Fori(0, NB // step) as i:
                for u in range(step):
                    rs(i * step + u, u)

        def s0_dve(dve):
            F = lambda n: f[0, n]
            V = nc.vector

            def wait(n, b, k):
                dve.wait_ge(F(n).sem, F(n).at(b, k))

            def front(b, s, turn):
                ln_stats(0, dve, b, s, s)

            def front2(b, s):
                wait("rstd", b, 1)
                V.tensor_scalar(xn[:, s, 0], x[:, b], mv[:, s, 0:1], rstd[:, s], ALU.subtract, ALU.mult).then_inc(F("xn").sem, 1)

            def start(b, s, turn):
                front(b, s, turn)
                front2(b, s)

            def back(b, s, nxt):
                P = F("parts")
                qv = q_f[:, s].rearrange("p (h d) -> p h d", d=D0)
                rv = q_r[:].rearrange("p (h d) -> p h d", d=D0)
                qp = lambda n, k, step=2: q_parts[:, s, :, 0:48].rearrange("p h (r d) -> p h r d", d=D0)[:, :, n:n + step * (k - 1) + 1:step]
                wait("qkv", b, 2)
                V.tensor_copy(qp(0, 3), qv.unsqueeze(2).to_broadcast([128, H0, 3, D0])).then_inc(P.sem, 1)
                kf = kv_f[:, s, :, 0:64].rearrange("p c (h d) -> p c h d", d=D0)
                kr = k_r[:].rearrange("p (c h d) -> p c h d", c=2, d=D0)
                kp = lambda n: k_parts[:, s, :, :, 8 * n:8 * n + 8]
                V.tensor_copy(kp(0), kf).then_inc(P.sem, 1)
                V.tensor_copy(kp(1), kf)
                V.tensor_copy(kp(5), kf)
                dve.wait_ge(P.sem, P.at(b, 1))
                V.tensor_tensor(rv, qv, qp(0, 1).rearrange("p h o d -> p h (o d)"), ALU.subtract).then_inc(P.sem, 1)
                dve.wait_ge(P.sem, P.at(b, 2))
                V.tensor_tensor(kr, kf, kp(0), ALU.subtract).then_inc(P.sem, 1)
                dve.wait_ge(P.sem, P.at(b, 3))
                V.tensor_copy(qp(1, 2), rv.unsqueeze(2).to_broadcast([128, H0, 2, D0])).then_inc(P.sem, 1)
                dve.wait_ge(P.sem, P.at(b, 4))
                V.tensor_copy(kp(2), kr)
                V.tensor_copy(kp(3), kr).then_inc(P.sem, 1)
                dve.wait_ge(P.sem, P.at(b, 5))
                V.tensor_tensor(qp(5, 1).rearrange("p h o d -> p h (o d)"), rv, qp(1, 1).rearrange("p h o d -> p h (o d)"), ALU.subtract)
                dve.wait_ge(P.sem, P.at(b, 6))
                V.tensor_tensor(kp(4), kr, kp(3), ALU.subtract).then_inc(P.sem, 1)
                vv = v0[:, s, :, :, 0:D0]
                kvv = kv_f[:, s, :, 64:128].rearrange("p c (h d) -> p c h d", d=D0)
                V.tensor_copy(vv[0:64, 2], kvv[0:64, 0])
                V.tensor_copy(vv[64:128, 2], kvv[0:64, 1])
                V.tensor_copy(vv[:, 0:2], kvv).then_inc(P.sem, 1)
                nxt()
                for k, (qb, j, n) in enumerate(FILLS_Q):
                    w = 2 * KEYS_Q[qb][1]
                    wait("sq", b, k + 1)
                    src = bank(4 + 2 * (k % 2), 2).rearrange("p (e c) -> p e c", e=2)[:, :, 0:n * w].rearrange("p e (j w) -> p e j w", w=w)
                    V.tensor_reduce(mx0[:, qb, j:j + n].rearrange("p j e -> p e j"), src, axis=AX.X, op=ALU.max, negate=True).then_inc(F("mx").sem, 1)
                M = F("mparts")
                m = mx0[:].rearrange("p q j e -> p (q j e)")
                wait("mx", b, 6)
                V.tensor_copy(mxp0[:, 0], m).then_inc(M.sem, 1)
                dve.wait_ge(M.sem, M.at(b, 1))
                V.tensor_tensor(mxr0[:], m, mxp0[:, 0], ALU.subtract).then_inc(M.sem, 1)
                dve.wait_ge(M.sem, M.at(b, 2))
                V.tensor_copy(mxp0[:, 1], mxr0[:]).then_inc(M.sem, 1)
                dve.wait_ge(M.sem, M.at(b, 3))
                V.tensor_tensor(mxp0[:, 2], mxr0[:], mxp0[:, 1], ALU.subtract).then_inc(M.sem, 1)
                wait("mxT_psum", b, 1)
                V.tensor_copy(mxq0[0:96, :], bank(2).bitcast(BF16)[0:96, 0:128]).then_inc(F("mxT").sem, 1)
                wait("pv", b, 1)
                pv = bank(3)[:, 0:288].rearrange("p (r d) -> p r d", d=D0 + 1)
                V.reciprocal(rden[:], pv[:, :, D0]).then_inc(F("rden").sem, 1)
                wait("rden", b, 1)
                V.tensor_tensor(o_n[:].rearrange("p q (h d) -> p (q h) d", d=D0), pv[:, :, 0:D0],
                                rden[:].unsqueeze(2).to_broadcast([128, 32, D0]), ALU.mult).then_inc(F("on").sem, 1)
                wait("y", b, 1)
                V.scalar_tensor_tensor(x[:, b], bank(1)[:, 0:C], gates[:, 0:1], x[:, b], ALU.mult, ALU.add).then_inc(x_done.sem, 1)

            def back_(b, s, nxt):
                def mid():
                    nxt()
                back(b, s, mid)

            items(dve, start, back_)

        def s0_act(act):
            F = lambda n: f[0, n]
            A = nc.scalar

            def wait(n, b, k):
                act.wait_ge(F(n).sem, F(n).at(b, k))

            def front(b, s, turn):
                wait("xnT_psum", b, 1)
                A.copy(xnT[:, s, :, 0:T], bank(0)[:, 0:C].rearrange("p (c t) -> p c t", c=NC)).then_inc(F("xnT").sem, 1)
                wait("qkv_psum", b, 1)
                A.activation(q_f[:, s], bank(0)[:, 128:384], ACT.Copy, scale=float(D0) ** -0.5).then_inc(F("qkv").sem, 1)
                A.copy(kv_f[:, s], bank(0).rearrange("p (c k) -> p c k", c=4)[:, 0:4:3, :]).then_inc(F("qkv").sem, 1)

            def back(b, s, nxt):
                wait("kT_psum", b, 1)
                A.copy(kT0[:], bank(1).bitcast(BF16).rearrange("p (j c t) -> p j c t", j=4, c=2)).then_inc(F("qkT").sem, 1)
                for k in range(2):
                    wait("qT_psum", b, k + 1)
                    src = bank(1 + (k + 1) % 2).bitcast(BF16).rearrange("p (j g b q) -> p j b g q", j=2, g=G0, b=NQB)
                    A.copy(qT0[:, 2 * k], src[:, 0])
                    A.copy(qT0[:, 2 * k + 1], src[:, 1]).then_inc(F("qkT").sem, 1)
                nxt()
                for k in range(6):
                    wait("st", b, k + 1)
                    A.activation(PT[:, 1024 * k:1024 * (k + 1)], bank(4 + 2 * (k % 2), 2), ACT.Exp).then_inc(F("p").sem, 1)
                wait("oT_psum", b, 1)
                A.copy(oT0[:].rearrange("p g (b q) -> p b g q", b=NQB), bank(2)[0:64].rearrange("p (b g q) -> p b g q", b=NQB, g=G0)).then_inc(F("oT").sem, 1)

            items(act, front, back)

        def s0_pe(pe):
            F = lambda n: f[0, n]
            MM = nc.tensor.matmul

            def wait(n, b, k):
                pe.wait_ge(F(n).sem, F(n).at(b, k))

            def front(b, s, turn):
                wait("xn", b, 1)
                for c in range(NC):
                    t = nc.tensor.transpose(bank(0)[:, 128 * c:128 * (c + 1)], xn[:, s, 0, 128 * c:128 * (c + 1)], ident[:])
                t.then_inc(F("xnT_psum").sem, 1)
                wait(f"ctx_loaded{s}", turn, 16)
                wait("xnT", b, 1)
                for c in range(NC):
                    MM(bank(0)[:, 128:512], xnT[:, s, c, 0:T], w0x[:, c], start=(c == 0), stop=False, skip_group_check=True)
                for c in range(NC):
                    t = MM(bank(0)[:, 0:384], ctxT[:, s, c], w0c[:, c], start=False, stop=(c == NC - 1), skip_group_check=True)
                t.then_inc(F("qkv_psum").sem, 1)

            def back(b, s, nxt):
                P = F("parts")
                kb, qa = bank(1).bitcast(BF16), bank(2).bitcast(BF16)
                pe.wait_ge(P.sem, P.at(b, 7))
                for j in range(4):
                    for c in range(2):
                        o = (j * 2 + c) * 128
                        t = nc.tensor.transpose(kb[:, o:o + 128], k_parts[:, s, c, 2 * j:2 * j + 2, :].rearrange("p h r -> p (h r)"), identb[:])
                t.then_inc(F("kT_psum").sem, 1)
                for k in range(2):
                    if k == 1:
                        wait("qkT", b, 1)
                    for j in range(2):
                        for g in range(G0):
                            o = (j * 4 + g) * 128
                            hk = 2 * (2 * k + j)
                            t = nc.tensor.transpose((qa if k == 0 else kb)[:, o:o + 128], q_parts[:, s, HK0 * g + hk:HK0 * g + hk + 2, :].rearrange("p h r -> p (h r)"), identb[:])
                    t.then_inc(F("qT_psum").sem, 1)
                nxt()
                wait("qkT", b, 3)

                def q_op(hk, qb):
                    r = 64 * (hk % 2)
                    return qT0[r:r + 64, hk // 2, qb].rearrange("p g q -> p (g q)")

                def k_op(hk, c, k0, n):
                    r = 64 * (hk % 2)
                    return kT0[r:r + 64, hk // 2, c, k0:k0 + n]

                base = [0, 128, 256, 512]

                def ext(hk, qb, c, k0, n):
                    o = 768 * hk + base[qb] + c * KEYS_T[qb] + k0
                    return ext0[:, o:o + n]

                for k, (qb, j0, n) in enumerate(FILLS_Q):
                    k0, w = KEYS_Q[qb]
                    if k < 2:
                        pe.wait_ge(F("p").sem, F("p").at(b, 0) - 1 + k)
                    else:
                        wait("mx", b, k - 1)
                    for e in range(2):
                        o = bank(4 + 2 * (k % 2) + e)
                        for j in range(n):
                            mk = ext0[:, base[qb]:base[qb] + 2 * KEYS_T[qb]].rearrange("p (c m) -> p c m", c=2)[:, :, k0:k0 + w]
                            MM(o[:, 2 * w * j:2 * w * (j + 1)], ohq0[:], mk, start=(j == 0), stop=False, skip_group_check=True)
                    for e in range(2):
                        o = bank(4 + 2 * (k % 2) + e)
                        for j in range(n):
                            hk = 2 * (j0 + j) + e
                            r = 64 * e
                            t = MM(o[:, 2 * w * j:2 * w * (j + 1)], q_op(hk, qb), kT0[r:r + 64, hk // 2, :, k0:k0 + w],
                                   start=False, stop=True, skip_group_check=True)
                    t.then_inc(F("sq").sem, 1)
                M = F("mparts")
                pe.wait_ge(M.sem, M.at(b, 4))
                nc.tensor.transpose(bank(2).bitcast(BF16)[0:96, 0:128], mxp0[:].rearrange("p a r -> p (a r)"), identb[:]).then_inc(F("mxT_psum").sem, 1)
                wait("mxT", b, 1)
                for k, (qb, c) in enumerate(FILLS_T):
                    if k < 2:
                        wait("mx", b, 5 + k)
                    else:
                        pe.wait_ge(F("p").sem, F("p").at(b, k - 1))
                    parts = ((0, 0, 64), (1, 64, 64)) if c == 2 else ((c, 0, 128),)
                    for e in range(2):
                        o = bank(4 + 2 * (k % 2) + e)
                        for j in range(4):
                            for cc, r0, m in parts:
                                MM(o[r0:r0 + m, 128 * j:128 * (j + 1)], ext(2 * j + e, qb, cc, 0, m), mxq0[:],
                                   start=(j == 0), stop=False, skip_group_check=True)
                    for e in range(2):
                        o = bank(4 + 2 * (k % 2) + e)
                        for j in range(4):
                            for cc, r0, m in parts:
                                t = MM(o[r0:r0 + m, 128 * j:128 * (j + 1)], k_op(2 * j + e, cc, 0, m), q_op(2 * j + e, qb),
                                       start=False, stop=True, skip_group_check=True)
                    t.then_inc(F("st").sem, 1)
                pvo = bank(3)[:, 0:288].rearrange("p (q h d) -> p q h d", q=NQB, h=HK0)
                ptv = PT[:].rearrange("p (k e j r) -> p k e j r", k=6, e=2, j=4)
                for qb in range(NQB):
                    ks = [qb] if qb < 2 else [2 * qb - 2, 2 * qb - 1]
                    pe.wait_ge(F("p").sem, F("p").at(b, ks[-1] + 1))
                    for hk in range(HK0):
                        for n, k in enumerate(ks):
                            t = MM(pvo[:, qb, hk], ptv[:, k, hk % 2, hk // 2], v0[:, s, FILLS_T[k][1], hk], start=(n == 0), stop=(n == len(ks) - 1))
                t.then_inc(F("pv").sem, 1)
                wait("on", b, 1)
                plain(pe)
                for qb in range(NQB):
                    t = nc.tensor.transpose(bank(2)[0:64, 128 * qb:128 * (qb + 1)], o_n[:, qb], ident[:])
                t.then_inc(F("oT_psum").sem, 1)
                wait("oT", b, 1)
                for g in range(G0):
                    t = MM(bank(1)[:, 0:C], oT0[:, g], w0o[:, g], start=(g == 0), stop=(g == G0 - 1))
                t.then_inc(F("y").sem, 1)

            items(pe, front, back)

        def stage_over(eng, s):
            if s > 0:
                eng.wait_ge(*ends[s - 1])

        def ff_front_dve(st, dve, p, s):
            for u in range(2):
                ln_stats(st, dve, 2 * p + u, None, 2 * s + u)
            for u in range(2):
                ln_apply(st, dve, 2 * p + u, 2 * s + u, xn[:, s, u])

        def ff_front_pe(st, pe, p, s):
            F = lambda n: f[st, n]
            pe.wait_ge(F("xn").sem, F("xn").at(2 * p + 1, 1))
            for c in range(NC):
                for u in range(2):
                    t = nc.tensor.transpose(bank(0)[:, 256 * c + 128 * u:256 * c + 128 * (u + 1)], xn[:, s, u, 128 * c:128 * (c + 1)], ident[:])
            t.then_inc(F("xnT_psum").sem, 1)

        def ff_front_act(st, act, p, s):
            F = lambda n: f[st, n]
            act.wait_ge(F("xnT_psum").sem, F("xnT_psum").at(p, 1))
            nc.scalar.copy(xnT[:, s], bank(0).rearrange("p (c t) -> p c t", c=NC)).then_inc(F("xnT").sem, 1)

        def router_pe(st, pe, p, s):
            F = lambda n: f[st, n]
            pe.wait_ge(F("xnT").sem, F("xnT").at(p, 1))
            pe.wait_ge(F("lg").sem, F("lg").at(p, 0))
            for u in range(2):
                for c in range(NC):
                    t = nc.tensor.matmul(bank(1)[:, 8 * u:8 * u + 8], xnT[:, s, c, T * u:T * (u + 1)], wr[:, {1: 0, 3: 1, 7: 2}[st], c],
                                         start=(c == 0), stop=(c == NC - 1))
            t.then_inc(F("lg_psum").sem, 1)

        def bc(ap, shape):
            return ap.to_broadcast(shape)

        def router_dve(st, dve, p):
            F = lambda n: f[st, n]
            V = nc.vector
            R = F("route")
            gate = {1: 4, 3: 5, 7: 7}[st]
            k = [0]

            def step(ins):
                k[0] += 1
                ins.then_inc(R.sem, 1)

            def settle(back=0):
                dve.wait_ge(R.sem, R.at(p, k[0] - back))

            dve.wait_ge(F("lg_psum").sem, F("lg_psum").at(p, 1))
            V.tensor_copy(lg[:], bank(1)[:, 0:16].rearrange("p (u e) -> p u e", u=2)).then_inc(F("lg").sem, 1)
            src = lg
            dve.wait_ge(F("lg").sem, F("lg").at(p, 1))
            if st == 7:
                dve.wait_ge(F("tanh").sem, F("tanh").at(p, 1))
                step(V.tensor_scalar(sg8[:], th[:], 0.5, 0.5, ALU.mult, ALU.add))
                settle()
                step(V.tensor_tensor(sel8[:], sg8[:], bc(sbias[:].unsqueeze(1), [128, 2, TOP_E]), ALU.add))
                settle()
                src = sel8
            plain(dve)
            for u in range(2):
                step(V.max(v8[:, u], src[:, u]))
            settle()
            plain(dve)
            for u in range(2):
                step(V.max_index(i8[:, u], v8[:, u], src[:, u]))
            if st != 7:
                step(V.tensor_tensor(dl[:], v8[:, :, 1:2], v8[:, :, 0:1], ALU.subtract))
            settle()
            step(V.tensor_copy(idf[:], i8[:, :, 0:2]))
            settle()
            step(V.tensor_tensor(oh[:], bc(iota8[:].unsqueeze(1).unsqueeze(1), [128, 2, 2, TOP_E]), bc(idf[:].unsqueeze(3), [128, 2, 2, TOP_E]), ALU.is_equal))
            if st != 7:
                dve.wait_ge(F("tanh").sem, F("tanh").at(p, 1))
                V.tensor_scalar(wk[:, :, 0:1], th[:, :, 0:1], half[:, 1, gate:gate + 1], half[:, 0, gate:gate + 1], ALU.mult, ALU.add)
                step(V.tensor_scalar(wk[:, :, 1:2], th[:, :, 0:1], half[:, 0, gate:gate + 1], half[:, 0, gate:gate + 1], ALU.mult, ALU.add))
            else:
                settle()
                step(V.tensor_tensor(ohs[:], oh[:], bc(sg8[:].unsqueeze(2), [128, 2, 2, TOP_E]), ALU.mult))
                settle()
                step(V.tensor_reduce(wk[:], ohs[:], axis=AX.X, op=ALU.add))
                settle()
                step(V.tensor_tensor(den[:], wk[:, :, 0:1], wk[:, :, 1:2], ALU.add))
                settle()
                step(V.tensor_scalar(den[:], den[:], 1e-9, None, ALU.add))
                settle()
                step(V.reciprocal(den[:], den[:]))
                settle()
                step(V.scalar_tensor_tensor(wk[:], wk[:], gates[:, gate:gate + 1], bc(den[:], [128, 2, 2]), ALU.mult, ALU.mult))
            settle()
            step(V.tensor_tensor(ohs[:], oh[:], bc(wk[:].unsqueeze(3), [128, 2, 2, TOP_E]), ALU.mult))
            settle()
            step(V.tensor_tensor(cw[:], ohs[:, :, 0], ohs[:, :, 1], ALU.add))
            assert k[0] == R.per, k
            settle()

        def router_act(st, act, p):
            F = lambda n: f[st, n]
            if st == 7:
                act.wait_ge(F("lg").sem, F("lg").at(p, 1))
                nc.scalar.activation(th[:], lg[:], ACT.Tanh, scale=0.5).then_inc(F("tanh").sem, 1)
            else:
                act.wait_ge(F("route").sem, F("route").at(p, 5))
                nc.scalar.activation(th[:, :, 0:1], dl[:], ACT.Tanh, scale=0.5).then_inc(F("tanh").sem, 1)

        def glu_pe(st, pe):
            F = lambda n: f[st, n]
            MM = nc.tensor.matmul
            wa, wb, n = (w1a, w1b, 8) if st == 1 else (w7a, w7b, 16)

            def front(p, s, turn):
                ff_front_pe(st, pe, p, s)

            def back(p, s, nxt):
                router_pe(st, pe, p, s)
                for j in range(n + 1):
                    if j < n:
                        pe.wait_ge(F("h").sem, F("h").at(p, j - 1))
                        for v in range(2):
                            for c in range(NC):
                                t = MM(bank(2 + j % 2)[:, 256 * v:256 * (v + 1)], wa[:, j, c, v], xnT[:, s, c], start=(c == 0), stop=(c == NC - 1))
                        t.then_inc(F("up").sem, 1)
                    if j == n // 2:
                        nxt()
                    if j > 0:
                        i = j - 1
                        pe.wait_ge(F("h").sem, F("h").at(p, i + 1))
                        if i < 8:
                            pe.wait_ge(F("acc").sem, F("acc").at(p, i - 1 if (st == 1 or i >= 2) else -1))
                        elif i == 8:
                            pe.wait_ge(F("acc").sem, F("acc").at(p, 0))
                        for u in range(2):
                            o = bank(4 + i % 2 if i < 8 else 6)[:, C * u:C * (u + 1)]
                            if i < 8:
                                t = MM(o, hT[:, i % 2, T * u:T * (u + 1)], wb[:, i], start=True, stop=True)
                            else:
                                t = MM(o, hT[:, i % 2, T * u:T * (u + 1)], wb[:, i], start=(i == 8 and u == 0), stop=(i == n - 1), skip_group_check=True)
                        t.then_inc(F("y").sem, 1)

            items(pe, front, back, n=NB // 2)

        def glu_act(st, act):
            F = lambda n: f[st, n]
            n = 8 if st == 1 else 16

            def front(p, s, turn):
                ff_front_act(st, act, p, s)

            def back(p, s, nxt):
                for j in range(n):
                    if j == 1:
                        router_act(st, act, p)
                    act.wait_ge(F("up").sem, F("up").at(p, j + 1))
                    act.wait_ge(F("h").sem, F("h").at(p, j - 1))
                    nc.scalar.activation(sil[:, j % 2], bank(2 + j % 2)[:, 0:256], ACT.Silu).then_inc(F("silu").sem, 1)
                    if j == n // 2:
                        nxt()

            items(act, front, back, n=NB // 2)

        def glu_dve(st, dve):
            F = lambda n: f[st, n]
            V = nc.vector
            n = 8 if st == 1 else 16

            def front(p, s, turn):
                ff_front_dve(st, dve, p, s)

            def back(p, s, nxt):
                acc = F("acc")
                if st == 1:
                    nxt()
                router_dve(st, dve, p)
                if st == 7:
                    nxt()
                for j in range(n + 1):
                    if j < n:
                        dve.wait_ge(F("silu").sem, F("silu").at(p, j + 1))
                        dve.wait_ge(F("y").sem, F("y").at(p, j - 1))
                        V.tensor_tensor(hT[:, j % 2], sil[:, j % 2], bank(2 + j % 2)[:, 256:512], ALU.mult).then_inc(F("h").sem, 1)
                    if 0 < j <= 8:
                        i = j - 1
                        dve.wait_ge(F("y").sem, F("y").at(p, i + 1))
                        if i > 0:
                            dve.wait_ge(acc.sem, acc.at(p, i))
                        for u in range(2):
                            t = V.scalar_tensor_tensor(x[:, 2 * p + u], bank(4 + i % 2)[:, C * u:C * (u + 1)], cw[:, u, i:i + 1], x[:, 2 * p + u], ALU.mult, ALU.add)
                        t.then_inc(acc.sem, 1)
                if st == 7:
                    dve.wait_ge(F("y").sem, F("y").at(p, 16))
                    dve.wait_ge(acc.sem, acc.at(p, 8))
                    V.scalar_tensor_tensor(x[:, bass.ds(2 * p, 2)], bank(6).rearrange("p (u c) -> p u c", u=2), gates[:, 7:8], x[:, bass.ds(2 * p, 2)],
                                           ALU.mult, ALU.add).then_inc(acc.sem, 1)

            items(dve, front, back, n=NB // 2)

        def s3_pe(pe):
            F = lambda n: f[3, n]
            MM = nc.tensor.matmul

            def front(p, s, turn):
                ff_front_pe(3, pe, p, s)

            def back(p, s, nxt):
                router_pe(3, pe, p, s)
                for j in range(4):
                    if j == 2:
                        nxt()
                    pe.wait_ge(F("acc").sem, F("acc").at(p, 4 * j - 4))
                    for u in range(2):
                        o = bank(2 + 2 * (j % 2) + u)
                        for c in range(NC):
                            MM(o, xnT[:, s, c, T * u:T * (u + 1)], w3e[:, c, 512 * j:512 * (j + 1)], start=(c == 0), stop=False)
                        t = MM(o, ones96[:], ebias[:, 512 * j:512 * (j + 1)], start=False, stop=True)
                    t.then_inc(F("y").sem, 1)

            items(pe, front, back, n=NB // 2)

        def s3_act(act):
            def front(p, s, turn):
                ff_front_act(3, act, p, s)

            def back(p, s, nxt):
                router_act(3, act, p)
                nxt()

            items(act, front, back, n=NB // 2)

        def s3_dve(dve):
            F = lambda n: f[3, n]

            def front(p, s, turn):
                ff_front_dve(3, dve, p, s)

            def back(p, s, nxt):
                acc = F("acc")
                nxt()
                router_dve(3, dve, p)
                for j in range(4):
                    dve.wait_ge(F("y").sem, F("y").at(p, j + 1))
                    for e in range(2):
                        for u in range(2):
                            k = 4 * j + 2 * e + u
                            if k >= 2:
                                dve.wait_ge(acc.sem, acc.at(p, k - 1))
                            nc.vector.scalar_tensor_tensor(x[:, 2 * p + u], bank(2 + 2 * (j % 2) + u)[:, C * e:C * (e + 1)], cw[:, u, 2 * j + e:2 * j + e + 1],
                                                           x[:, 2 * p + u], ALU.mult, ALU.add).then_inc(acc.sem, 1)

            items(dve, front, back, n=NB // 2)

        def s5_pe(pe):
            F = lambda n: f[5, n]

            def front(p, s, turn):
                ff_front_pe(5, pe, p, s)

            def back(p, s, nxt):
                pe.wait_ge(F("xnT").sem, F("xnT").at(p, 1))
                nxt()
                pe.wait_ge(F("acc").sem, F("acc").at(p, -1))
                for u in range(2):
                    for c in range(NC):
                        t = nc.tensor.matmul(bank(2 + s)[:, C * u:C * (u + 1)], xnT[:, s, c, T * u:T * (u + 1)], fsum[:, c], start=(c == 0), stop=(c == NC - 1))
                t.then_inc(F("y").sem, 1)

            items(pe, front, back, n=NB // 2)

        def s5_act(act):
            def front(p, s, turn):
                ff_front_act(5, act, p, s)

            def back(p, s, nxt):
                nxt()

            items(act, front, back, n=NB // 2)

        def s5_dve(dve):
            F = lambda n: f[5, n]
            V = nc.vector

            def front(p, s, turn):
                ff_front_dve(5, dve, p, s)

            def back(p, s, nxt):
                nxt()
                xs = x[:, bass.ds(2 * p, 2)]
                V.tensor_tensor(xs, xs, fb[:].unsqueeze(1).to_broadcast([128, 2, C]), ALU.add).then_inc(F("bias").sem, 1)
                dve.wait_ge(F("bias").sem, F("bias").at(p, 1))
                dve.wait_ge(F("y").sem, F("y").at(p, 1))
                V.scalar_tensor_tensor(xs, bank(2 + s).rearrange("p (u c) -> p u c", u=2), gs5[:], xs, ALU.mult, ALU.add).then_inc(F("acc").sem, 1)

            items(dve, front, back, n=NB // 2)

        POS_Q, POS_K = (0, 1, 0, 1, 0, 2), (0, 0, 1, 1, 2, 0)

        def s2_sp(sp):
            F = lambda n: f[2, n]

            def load_k(b, s):
                for r in range(6):
                    sp.dma_start(kop[16 * r:16 * (r + 1), s], kscr[b, POS_K[r]].rearrange("(h d) n -> d h n", d=16)).then_inc(F(f"k_loaded{s}").sem, 16)
                sp.dma_start(vT2[:, s], a["ctxT17"][:, b]).then_inc(F(f"k_loaded{s}").sem, 16)

            def q(b, s, turn):
                sp.wait_ge(F("parts").sem, F("parts").at(b, 5))
                sp.dma_start(qscr[s].rearrange("r p n -> p r n"), xparts[:, s]).then_inc(F(f"q_stored{s}").sem, 16)
                sp.wait_ge(F(f"q_stored{s}").sem, F(f"q_stored{s}").at(turn, 16))
                for r in range(6):
                    sp.dma_start(qop[16 * r:16 * (r + 1), s], qscr[s, POS_Q[r]].rearrange("(h d) n -> d h n", d=16)).then_inc(F(f"q_loaded{s}").sem, 16)

            for u in range(2):
                sp.wait_ge(c_out[u], 16 * (NB // 2))
            for b in range(2):
                load_k(b, b)
                q(b, b, 0)
            with sp.Fori(0, NB // 2 - 1) as i:
                for u in range(2):
                    sp.wait_ge(F("pv").sem, F("pv").at(i * 2 + u, 1))
                    load_k(i * 2 + (u + 2), u)
                    q(i * 2 + (u + 2), u, i + 1)

        def split3(V, eng, src, dst, res, fl, item, k0=0):
            if V is nc.gpsimd:
                plain(eng)
            V.tensor_copy(dst(0), src).then_inc(fl.sem, 1)
            eng.wait_ge(fl.sem, fl.at(item, k0 + 1))
            V.tensor_tensor(res, src, dst(0), ALU.subtract).then_inc(fl.sem, 1)
            eng.wait_ge(fl.sem, fl.at(item, k0 + 2))
            if V is nc.gpsimd:
                plain(eng)
            V.tensor_copy(dst(1), res).then_inc(fl.sem, 1)
            eng.wait_ge(fl.sem, fl.at(item, k0 + 3))
            V.tensor_tensor(dst(2), res, dst(1), ALU.subtract).then_inc(fl.sem, 1)

        def s2_dve(dve):
            F = lambda n: f[2, n]
            V = nc.vector

            def wait(n, b, k):
                dve.wait_ge(F(n).sem, F(n).at(b, k))

            def front(b, s, turn):
                ln_stats(2, dve, b, None, s)
                ln_apply(2, dve, b, s, xn[:, s, 0])
                P = F("parts")
                dve.wait_ge(F("xn").sem, F("xn").at(b, 1))
                split3(V, dve, xn[:, s, 0], lambda n: xparts[:, s, n], xres[:], P, b)
                V.tensor_copy(dl[:, 0, 0:1], dl[:, 0, 0:1]).then_inc(P.sem, 1)

            def back(b, s, nxt):
                nxt()
                for k in range(4):
                    wait("sq", b, k + 1)
                    V.tensor_reduce(mx2[:, k // 2, 4 * (k % 2):4 * (k % 2) + 4], bank(4 + 2 * (k % 2), 2).rearrange("p (h l) -> p h l", h=4),
                                    axis=AX.X, op=ALU.max, negate=True).then_inc(F("mx").sem, 1)
                wait("mx", b, 4)
                split3(V, dve, mx2[:], lambda n: mxp2[:, :, n], mxr2[:], F("mparts"), b)
                wait("mxT_psum", b, 1)
                V.tensor_copy(mxq2[0:24, :], bank(2).bitcast(BF16)[0:24, 0:256]).then_inc(F("mxT").sem, 1)
                wait("pv", b, 1)
                pv = bank(3)[:, 0:272].rearrange("p (r d) -> p r d", d=17)
                V.reciprocal(rden[:, 0:16], pv[:, :, 16]).then_inc(F("rden").sem, 1)
                wait("rden", b, 1)
                V.tensor_tensor(o_n[:].rearrange("p q (h d) -> p (q h) d", d=16), pv[:, :, 0:16], rden[:, 0:16].unsqueeze(2).to_broadcast([128, 16, 16]),
                                ALU.mult).then_inc(F("on").sem, 1)
                wait("y", b, 1)
                V.scalar_tensor_tensor(x[:, b], bank(2)[:, 0:C], gg[:], x[:, b], ALU.mult, ALU.add).then_inc(x_done.sem, 1)

            items(dve, front, back)

        def s2_act(act):
            F = lambda n: f[2, n]

            def front(b, s, turn):
                pass

            def back(b, s, nxt):
                for k in range(4):
                    act.wait_ge(F("st").sem, F("st").at(b, k + 1))
                    nc.scalar.activation(PT[:, 1024 * k:1024 * (k + 1)], bank(4 + 2 * (k % 2), 2), ACT.Exp, scale=0.25).then_inc(F("p").sem, 1)

            items(act, front, back)

        def s2_pe(pe):
            F = lambda n: f[2, n]
            MM = nc.tensor.matmul

            def wait(n, b, k):
                pe.wait_ge(F(n).sem, F(n).at(b, k))

            def front(b, s, turn):
                pass

            def back(b, s, nxt, turn):
                wait(f"q_loaded{s}", turn, 96)
                wait(f"k_loaded{s}", turn, 112)
                for k in range(4):
                    if k < 2:
                        wait("p", b, k - 1)
                    else:
                        wait("mx", b, k - 1)
                    qt, h0 = k // 2, 4 * (k % 2)
                    for h in range(4):
                        t = MM(bank(4 + 2 * (k % 2), 2)[:, 256 * h:256 * (h + 1)], qop[:, s, h0 + h, 128 * qt:128 * (qt + 1)], kop[:, s, h0 + h], start=True, stop=True)
                    t.then_inc(F("sq").sem, 1)
                wait("mparts", b, 4)
                plain(pe)
                for qt in range(2):
                    t = nc.tensor.transpose(bank(2).bitcast(BF16)[0:24, 128 * qt:128 * (qt + 1)], mxp2[:, qt].rearrange("p r h -> p (r h)"), identb[:])
                t.then_inc(F("mxT_psum").sem, 1)
                wait("mxT", b, 1)
                for k in range(4):
                    if k < 2:
                        wait("mx", b, 3 + k)
                    else:
                        wait("p", b, k - 1)
                    for j in range(2):
                        h = 2 * k + j
                        for lt in range(2):
                            o = bank(4 + 2 * (k % 2) + j)[:, 256 * lt:256 * (lt + 1)]
                            MM(o, sel2[:, h], mxq2[:], start=True, stop=False)
                            t = MM(o, kop[:, s, h, 128 * lt:128 * (lt + 1)], qop[:, s, h], start=False, stop=True)
                    t.then_inc(F("st").sem, 1)
                ptv = PT[:, 0:4096].rearrange("p (h l q) -> p h l q", h=8, l=2)
                pvo = bank(3)[:, 0:272].rearrange("p (q h d) -> p q h d", q=2, h=8)
                for h in range(8):
                    wait("p", b, h // 2 + 1)
                    for qt in range(2):
                        for lt in range(2):
                            t = MM(pvo[:, qt, h], ptv[:, h, lt, 128 * qt:128 * (qt + 1)], vT2[:, s, lt, h], start=(lt == 0), stop=(lt == 1))
                t.then_inc(F("pv").sem, 1)
                wait("on", b, 1)
                ov = o_n[:].rearrange("p q h -> p (q h)")
                for qt in range(2):
                    t = nc.tensor.transpose(bank(2)[:, 128 * qt:128 * (qt + 1)], ov[:, 128 * qt:128 * (qt + 1)], ident[:])
                t.then_inc(F("y").sem, 1)

            with pe.Fori(0, NB // 2) as i:
                for u in range(2):
                    back(i * 2 + u, u, None, i)

        MAGIC = 1.5 * 2 ** 23

        def quant(dve, src, dst, sc, tmp, fl, item, k0, amax_done=False):
            V = nc.vector

            def settle(k):
                dve.wait_ge(fl.sem, fl.at(item, k0 + k))
            V.tensor_reduce(sc[:, 0:1], src, axis=AX.X, op=ALU.max, apply_absolute_value=True).then_inc(fl.sem, 1)
            settle(1)
            V.tensor_scalar(sc[:, 1:2], sc[:, 0:1], 1.0 / 127.0, 1e-8, ALU.mult, ALU.max).then_inc(fl.sem, 1)
            settle(2)
            V.reciprocal(sc[:, 2:3], sc[:, 1:2]).then_inc(fl.sem, 1)
            settle(3)
            V.tensor_scalar(tmp, src, sc[:, 2:3], 127.0, ALU.mult, ALU.min).then_inc(fl.sem, 1)
            settle(4)
            V.tensor_scalar(tmp, tmp, -127.0, MAGIC, ALU.max, ALU.add).then_inc(fl.sem, 1)
            settle(5)
            V.tensor_scalar(dst, tmp, MAGIC, None, ALU.subtract).then_inc(fl.sem, 1)

        wq_n = staging[:, 0:1024].rearrange("p (w o c) -> p w o c", w=2, o=2)
        wprep = Flag(sem("wprep"), 0)
        wprep_pe = sem("wprep_pe")

        def s4_weights_dve(dve):
            k = 0
            for w in range(2):
                for o in range(2):
                    n = 2 * w + o
                    if k:
                        dve.wait_ge(wprep.sem, k)
                    quant(dve, wq_n[:, w, o], qw[:, w, o], wsc[:, n].rearrange("p a b -> p (a b)"), qt_f[:], wprep, 0, k)
                    k += 6
                    V = nc.vector
                    V.tensor_scalar(diag[:, n], ident[:], wsc[:, n].rearrange("p a b -> p (a b)")[:, 1:2], None, ALU.mult).then_inc(wprep.sem, 1)
                    k += 1
            dve.wait_ge(wprep_pe, 1)
            V.tensor_scalar(rows4[:, 3], bank(1)[:, 0:256], 0.25, None, ALU.mult)
            V.tensor_scalar(rows4[:, 4], bank(1)[:, 256:512], gates[:, 2:3], None, ALU.mult)
            V.tensor_scalar(rows4[:, 0], rows4[:, 0], 0.25, None, ALU.mult)
            V.tensor_scalar(rows4[:, 2], rows4[:, 2], gates[:, 2:3], None, ALU.mult)
            for w in range(2):
                t = V.tensor_copy(qwT[:, w], bank(2 + w).bitcast(BF16)[:, 0:512].rearrange("p (c o) -> p c o", c=2))
            t.then_inc(wprep.sem, 1)
            k += 1
            dve.wait_ge(wprep.sem, k)
            return k

        def s4_weights_pe(pe):
            pe.wait_ge(wprep.sem, 28)
            for w in range(2):
                for o in range(2):
                    nc.tensor.matmul(bank(1)[:, 256 * w + 128 * o:256 * w + 128 * (o + 1)], onesf[:], diag[:, 2 * w + o], start=True, stop=True)
                    for c in range(2):
                        t = nc.tensor.transpose(bank(2 + w).bitcast(BF16)[:, 256 * c + 128 * o:256 * c + 128 * (o + 1)], qw[:, w, o, 128 * c:128 * (c + 1)], identb[:])
            t.then_inc(wprep_pe, 1)
            pe.wait_ge(wprep.sem, 29)

        def s4_sp(sp):
            F = lambda n: f[4, n]

            def load(b, s):
                sp.dma_start(ctxT[:, s], a["ctxT"][:, b]).then_inc(F(f"ctx_loaded{s}").sem, 16)
                sp.dma_start(mskq[:, s], a["mask"][:, b]).then_inc(F(f"ctx_loaded{s}").sem, 16)
                sp.dma_start(mskT[:, s], a["maskT"][:, b]).then_inc(F(f"ctx_loaded{s}").sem, 16)
            load(0, 0)
            load(1, 1)
            with sp.Fori(0, NB // 2 - 1) as i:
                for u in range(2):
                    sp.wait_ge(F("pv").sem, F("pv").at(i * 2 + u, 1))
                    load(i * 2 + (u + 2), u)

        def s4_dve(dve):
            F = lambda n: f[4, n]
            V = nc.vector

            def wait(n, b, k):
                dve.wait_ge(F(n).sem, F(n).at(b, k))

            def front(b, s, turn):
                ln_stats(4, dve, b, None, s)
                ln_apply(4, dve, b, s, xn[:, s, 0])
                wait("xn", b, 1)
                quant(dve, xn[:, s, 0], qx[:], qsc[:, s], qt_f[:], F("quant"), b, 0)
                wait("q_psum", b, 1)
                D = F("qdve")
                V.scalar_tensor_tensor(q_tmp[:], bank(1)[:, 0:C], qsc[:, s, 1:2], rows4[:, 3], ALU.mult, ALU.mult).then_inc(D.sem, 1)
                V.tensor_tensor(v4[:, s, :, 0:16], bank(1)[:, C:2 * C].rearrange("p (h d) -> p h d", d=16), rows4[:, 1].rearrange("p (h d) -> p h d", d=16), ALU.add).then_inc(D.sem, 1)
                dve.wait_ge(D.sem, D.at(b, 1))
                V.tensor_tensor(qpad[:, :, 0:16], q_tmp[:].rearrange("p (h d) -> p h d", d=16), rows4[:, 0].rearrange("p (h d) -> p h d", d=16), ALU.add).then_inc(D.sem, 1)

            def back(b, s, nxt):
                for k in range(2):
                    wait("sq", b, k + 1)
                    V.tensor_reduce(mx4[:, 8 * k:8 * k + 8], bank(4 + 2 * k, 2).rearrange("p (h l) -> p h l", h=8), axis=AX.X, op=ALU.max, negate=True).then_inc(F("mx").sem, 1)
                wait("mx", b, 2)
                split3(V, dve, mx4[:], lambda n: mxp4[:, n], mxr4[:], F("mparts"), b)
                wait("mxT_psum", b, 1)
                V.tensor_copy(mxq4[0:48, :], bank(3).bitcast(BF16)[0:48, 0:128]).then_inc(F("mxT").sem, 1)
                nxt()
                wait("pv", b, 1)
                pv = bank(3)[:, 0:272].rearrange("p (r d) -> p r d", d=17)
                V.reciprocal(rden[:, 0:16], pv[:, :, 16]).then_inc(F("rden").sem, 1)
                wait("rden", b, 1)
                ov = o_n[:].rearrange("p q h -> p (q h)")
                V.tensor_tensor(ov.rearrange("p (h d) -> p h d", d=16), pv[:, :, 0:16], rden[:, 0:16].unsqueeze(2).to_broadcast([128, 16, 16]), ALU.mult).then_inc(F("on").sem, 1)
                wait("on", b, 1)
                if b is not None:
                    quant(dve, ov, qo[:], osc[:], qt_f[:], F("oquant"), b, 0)
                wait("y", b, 1)
                fin = F("fin")
                V.scalar_tensor_tensor(q_tmp[:], bank(3)[:, 0:C], osc[:, 1:2], rows4[:, 4], ALU.mult, ALU.mult).then_inc(fin.sem, 1)
                wait("fin", b, 1)
                V.tensor_tensor(q_tmp[:], q_tmp[:], rows4[:, 2], ALU.add).then_inc(fin.sem, 1)
                wait("fin", b, 2)
                V.tensor_tensor(x[:, b], x[:, b], q_tmp[:], ALU.add).then_inc(x_done.sem, 1)

            items(dve, front, back)

        def s4_act(act):
            F = lambda n: f[4, n]
            A = nc.scalar

            def wait(n, b, k):
                act.wait_ge(F(n).sem, F(n).at(b, k))

            def front(b, s, turn):
                wait("xT_psum", b, 1)
                A.copy(qxT[:], bank(0).bitcast(BF16)[:, 0:256].rearrange("p (c t) -> p c t", c=2)).then_inc(F("xT").sem, 1)
                wait("k_psum", b, 1)
                for g in range(4):
                    A.activation(kT4[:, s, g], bank(2)[:, 128 * g:128 * (g + 1)], ACT.Identity, bias=bkc[:, g:g + 1]).then_inc(F("k").sem, 1)
                wait("qT_psum", b, 1)
                A.copy(qT4[:, s], bank(0).rearrange("p (g t) -> p g t", g=4)).then_inc(F("qT").sem, 1)

            def back(b, s, nxt):
                nxt()
                for k in range(2):
                    wait("st", b, k + 1)
                    A.activation(PT[:, 1024 * k:1024 * (k + 1)], bank(4 + 2 * k, 2), ACT.Exp).then_inc(F("p").sem, 1)
                wait("oT_psum", b, 1)
                A.copy(qoT[:], bank(3).bitcast(BF16)[:, 512:768].rearrange("p (c t) -> p c t", c=2)).then_inc(F("oT").sem, 1)

            items(act, front, back)

        def s4_pe(pe):
            F = lambda n: f[4, n]
            MM = nc.tensor.matmul

            def wait(n, b, k):
                pe.wait_ge(F(n).sem, F(n).at(b, k))

            def front(b, s, turn):
                wait("quant", b, 6)
                for c in range(2):
                    t = nc.tensor.transpose(bank(0).bitcast(BF16)[:, 128 * c:128 * (c + 1)], qx[:, 128 * c:128 * (c + 1)], identb[:])
                t.then_inc(F("xT_psum").sem, 1)
                wait(f"ctx_loaded{s}", turn, 48)
                for g in range(4):
                    for c in range(2):
                        t = MM(bank(2)[:, 128 * g:128 * (g + 1)], wkT[:, c, g], ctxT[:, s, c], start=(c == 0), stop=(c == 1))
                t.then_inc(F("k_psum").sem, 1)
                for c in range(2):
                    MM(bank(1)[:, C:2 * C], ctxT[:, s, c], wvT[:, c], start=(c == 0), stop=(c == 1))
                wait("xT", b, 1)
                for c in range(2):
                    t = MM(bank(1)[:, 0:C], qxT[:, c], qwT[:, 0, c], start=(c == 0), stop=(c == 1))
                t.then_inc(F("q_psum").sem, 1)
                wait("qdve", b, 3)
                qv = qpad[:].rearrange("p h d -> p (h d)")
                for g in range(4):
                    t = nc.tensor.transpose(bank(0)[:, 128 * g:128 * (g + 1)], qv[:, 128 * g:128 * (g + 1)], ident[:])
                t.then_inc(F("qT_psum").sem, 1)

            def back(b, s, nxt):
                wait("qT", b, 1)
                wait("k", b, 4)
                for k in range(2):
                    wait("p", b, k - 1)
                    for r in (2 * k, 2 * k + 1):
                        MM(bank(4 + r), ident[:], mskq[:, s].unsqueeze(1).to_broadcast([128, 4, T]), start=True, stop=False, skip_group_check=True)
                    for g in range(4):
                        for r in (2 * k, 2 * k + 1):
                            t = MM(bank(4 + r)[:, 128 * g:128 * (g + 1)], qT4[32 * r:32 * r + 16, s, g], kT4[32 * r:32 * r + 16, s, g], start=False, stop=True, skip_group_check=True)
                    t.then_inc(F("sq").sem, 1)
                wait("mparts", b, 4)
                plain(pe)
                nc.tensor.transpose(bank(3).bitcast(BF16)[0:48, 0:128], mxp4[:].rearrange("p r h -> p (r h)"), identb[:]).then_inc(F("mxT_psum").sem, 1)
                wait("mxT", b, 1)
                for k in range(2):
                    wait("mx", b, k + 1)
                    for r in (2 * k, 2 * k + 1):
                        MM(bank(4 + r), ident[:], mskT[:, s].unsqueeze(1).to_broadcast([128, 4, T]), start=True, stop=False, skip_group_check=True)
                        for g in range(4):
                            MM(bank(4 + r)[:, 128 * g:128 * (g + 1)], sel4[:, 4 * r + g], mxq4[:], start=False, stop=False, skip_group_check=True)
                    for g in range(4):
                        for r in (2 * k, 2 * k + 1):
                            t = MM(bank(4 + r)[:, 128 * g:128 * (g + 1)], kT4[32 * r:32 * r + 16, s, g], qT4[32 * r:32 * r + 16, s, g], start=False, stop=True, skip_group_check=True)
                    t.then_inc(F("st").sem, 1)
                nxt()
                ptv = PT[:, 0:2048].rearrange("p (r g q) -> p r g q", r=4, g=4)
                pvo = bank(3)[:, 0:272].rearrange("p (h d) -> p h d", d=17)
                for k in range(2):
                    wait("p", b, k + 1)
                    for r in (2 * k, 2 * k + 1):
                        for g in range(4):
                            t = MM(pvo[:, 4 * g + r], ptv[:, r, g], v4[:, s, 4 * g + r], start=True, stop=True)
                t.then_inc(F("pv").sem, 1)
                wait("oquant", b, 6)
                for c in range(2):
                    t = nc.tensor.transpose(bank(3).bitcast(BF16)[:, 512 + 128 * c:512 + 128 * (c + 1)], qo[:, 128 * c:128 * (c + 1)], identb[:])
                t.then_inc(F("oT_psum").sem, 1)
                wait("oT", b, 1)
                for c in range(2):
                    t = MM(bank(3)[:, 0:C], qoT[:, c], qwT[:, 1, c], start=(c == 0), stop=(c == 1))
                t.then_inc(F("y").sem, 1)

            items(pe, front, back)

        def s6_sp(sp):
            F = lambda n: f[6, n]

            def load(b, s):
                sp.dma_start(ctxT[:, s], a["ctxT"][:, b]).then_inc(F(f"ctx_loaded{s}").sem, 16)
                sp.dma_start(cnat[:, s], a["ctx"][:, b]).then_inc(F(f"ctx_loaded{s}").sem, 16)
            load(0, 0)
            load(1, 1)
            with sp.Fori(0, NB // 2 - 1) as i:
                for u in range(2):
                    sp.wait_ge(F("y").sem, F("y").at(i * 2 + u, 1))
                    load(i * 2 + (u + 2), u)

        sgm = PT[:, 0:1024].rearrange("p (s n m) -> p s n m", s=2, n=2)

        def s6_dve(dve):
            F = lambda n: f[6, n]

            def front(b, s, turn):
                ln_stats(6, dve, b, None, s)
                ln_apply(6, dve, b, s, xn[:, s, 0])

            def back(b, s, nxt):
                nxt()
                dve.wait_ge(F("y").sem, F("y").at(b, 1))
                nc.vector.scalar_tensor_tensor(x[:, b], bank(4 + s)[:, 0:C], gates[:, 3:4], x[:, b], ALU.mult, ALU.add).then_inc(x_done.sem, 1)

            items(dve, front, back)

        def s6_act(act):
            F = lambda n: f[6, n]

            def front(b, s, turn):
                act.wait_ge(F("s_psum").sem, F("s_psum").at(b, 1))
                nc.scalar.activation(sgm[:, s], bank(2 + s).rearrange("p (n m) -> p n m", n=2), ACT.Sigmoid, scale=float(T) ** -0.5).then_inc(F("s").sem, 1)

            def back(b, s, nxt):
                nxt()

            items(act, front, back)

        def s6_pe(pe):
            F = lambda n: f[6, n]
            MM = nc.tensor.matmul

            def front(b, s, turn):
                pe.wait_ge(F("xn").sem, F("xn").at(b, 1))
                pe.wait_ge(F(f"ctx_loaded{s}").sem, F(f"ctx_loaded{s}").at(turn, 32))
                for n in range(2):
                    t = MM(bank(2 + s)[:, C * n:C * (n + 1)], xn[:, s, 0, 128 * n:128 * (n + 1)], cnat[:, s], start=True, stop=True)
                t.then_inc(F("s_psum").sem, 1)

            def back(b, s, nxt):
                nxt()
                pe.wait_ge(F("s").sem, F("s").at(b, 1))
                pe.wait_ge(x_done.sem, b + (3 * NB - 1))
                for n in range(2):
                    t = MM(bank(4 + s)[:, 0:C], ctxT[:, s, n], sgm[:, s, n], start=(n == 0), stop=(n == 1))
                t.then_inc(F("y").sem, 1)

            items(pe, front, back)

        c_in = [sem("c_in0"), sem("c_in1")]
        c_parts = Flag(sem("c_parts"), 4)
        c_out = [sem("c_out0"), sem("c_out1")]

        def ctx_pipeline(pool, fetch):
            rs = rstd_step(0, pool)

            def one(b, u, turn, first, last):
                rs(b, u)
                pool.wait_ge(c_in[u], turn * 16 + 16)
                plain(pool)
                if not first:
                    pool.wait_ge(c_out[u], turn * 16)
                split3(nc.gpsimd, pool, cnat[:, u], lambda n: cparts[:, u, n], cres[:], c_parts, b)
                pool.wait_ge(c_parts.sem, c_parts.at(b, 4))
                pool.dma_start(kscr[b].rearrange("r p n -> p r n"), cparts[:, u]).then_inc(c_out[u], 16)
                if not last:
                    fetch(b + 2, u)
            for u in range(2):
                one(u, u, 0, True, False)
            with pool.Fori(1, NB // 2 - 1) as i:
                for u in range(2):
                    one(i * 2 + u, u, i, False, False)
            for u in range(2):
                one(NB - 2 + u, u, NB // 2 - 1, False, True)


        @block.sync
        def _(sp):
            for q in range(4):
                sp.dma_start(x[:, 4 * q:4 * q + 4], a["x"][:, 4 * q:4 * q + 4]).then_inc(loaded_x, 16)
            sp.dma_start(arena[:, 0:10240], a["w13"]).then_inc(w_loaded[1], 16)
            s0_sp(sp)
            if n_stages > 2:
                stage_over(sp, 2)
                s2_sp(sp)
                sp.dma_start(wkT, a["wkT"]).then_inc(w_loaded[3], 16)
                sp.dma_start(wvT, a["wvT"]).then_inc(w_loaded[3], 16)
                sp.dma_start(sel4, a["sel4"].bitcast(BF16)).then_inc(w_loaded[3], 16)
            if n_stages > 3:
                stage_over(sp, 3)
                sp.dma_start(staging[:, 0:1024], a["w4n"]).then_inc(w_loaded[4], 16)
            if n_stages > 4:
                stage_over(sp, 4)
                for t, name in ((arena[:], "w7"),):
                    sp.dma_start(t, a[name]).then_inc(w_loaded[7], 16)
                s4_sp(sp)
                stage_over(sp, 5)
                sp.dma_start(staging, a["w5"]).then_inc(w_loaded[5], 16)
            if n_stages > 6:
                stage_over(sp, 6)
                s6_sp(sp)
            sp.wait_ge(*ends[n_stages - 1])
            done = sem("stored")
            sp.dma_start(out, x[:]).then_inc(done, 16)
            sp.wait_ge(done, 16)

        @block.scalar
        def _(act):
            n = 0
            for t, name in ((ident, "ident"), (gates, "gates"), (w0x, "w0x"), (w0c, "w0c"), (w0o, "w0o"), (wr, "wr"), (iota8, "iota8"),
                            (sbias, "sbias"), (bkc, "bkc"), (fb, "fb")):
                act.dma_start(t[:], a[name]).then_inc(loaded_c, 16)
            act.dma_start(rows4[:, 0:3], a["rows4"]).then_inc(loaded_c, 16)
            for t, name in ((ext0, "ext0"), (mxq0, "mxq0"), (ohq0, "ohq0"), (sel2, "sel2")):
                act.dma_start(t[:], a[name].bitcast(BF16)).then_inc(loaded_c, 16)
            for s in range(2):
                act.dma_start(q_parts[:, s], a["q_const"].bitcast(BF16)).then_inc(loaded_c, 16)
                act.dma_start(k_parts[:, s], a["k_const"].bitcast(BF16)).then_inc(loaded_c, 16)
            act.dma_start(eb_f, a["eb"]).then_inc(loaded_c, 16)
            act.wait_ge(loaded_c, LOADS_0)
            A = nc.scalar
            A.activation(gates[:, 0:8], gates[:, 0:8], ACT.Tanh).then_inc(gates_ready, 1)
            give(act, [(0, "p")])
            s0_act(act)
            for s, prog in enumerate((None, lambda: glu_act(1, act), lambda: s2_act(act), lambda: s3_act(act), lambda: s4_act(act),
                                      lambda: s5_act(act), lambda: s6_act(act), lambda: glu_act(7, act))):
                if 0 < s < n_stages:
                    stage_over(act, s)
                    prog()

        @block.vector
        def _(dve):
            V = nc.vector
            dve.wait_ge(loaded_c, LOADS_0)
            dve.wait_ge(loaded_x, 64)
            V.memset(minus_half[:], -0.5)
            V.memset(v0[:], 1.0)
            V.memset(v4[:], 1.0)
            V.memset(qpad[:], 0.0)
            V.memset(onesf[:], 1.0)
            V.memset(ones96[:], 1.0)
            V.memset(mxq2[:], 0.0)
            V.memset(mxq4[:], 0.0)
            V.memset(dl[:], 0.0)
            V.memset(th[:], 0.0)
            V.tensor_copy(identb[:], ident[:]).then_inc(zero_ready, 1)
            dve.wait_ge(zero_ready, 1)
            give(dve, [(s, n) for s in (1, 3, 5, 7) for n in ("h", "acc", "lg")])
            G = prep_w
            V.tensor_copy(eb_b, eb_f).then_inc(G.sem, 1)
            dve.wait_ge(G.sem, 1)
            V.tensor_copy(ebias[0:32], eb_b[0:32])
            V.tensor_tensor(eb_r, eb_f, eb_b, ALU.subtract).then_inc(G.sem, 1)
            dve.wait_ge(G.sem, 2)
            V.tensor_copy(eb_b, eb_r).then_inc(G.sem, 1)
            dve.wait_ge(G.sem, 3)
            V.tensor_copy(ebias[32:64], eb_b[32:64])
            V.tensor_tensor(ebias[64:96], eb_r[64:96], eb_b[64:96], ALU.subtract).then_inc(G.sem, 1)
            dve.wait_ge(G.sem, 4)
            dve.wait_ge(gates_ready, 1)
            V.tensor_scalar(half[:, 0], gates[:], 0.5, None, ALU.mult)
            V.tensor_scalar(half[:, 1], gates[:], -0.5, None, ALU.mult)
            V.tensor_scalar(gs5[:], gates[:, 6:7], float(8.0 ** -0.5), None, ALU.mult)
            V.tensor_scalar(fb[:], fb[:], gates[:, 6:7], None, ALU.mult)
            V.tensor_tensor(gg[:], gates[:, 1:2], gates[:, 8:9], ALU.mult).then_inc(G.sem, 1)
            dve.wait_ge(G.sem, 5)
            s0_dve(dve)
            if n_stages > 1:
                stage_over(dve, 1)
                glu_dve(1, dve)
            if n_stages > 2:
                stage_over(dve, 2)
                s2_dve(dve)
            if n_stages > 3:
                stage_over(dve, 3)
                s3_dve(dve)
            if n_stages > 4:
                stage_over(dve, 4)
                dve.wait_ge(w_loaded[4], 16)
                s4_weights_dve(dve)
                s4_dve(dve)
            if n_stages > 5:
                stage_over(dve, 5)
                dve.wait_ge(w_loaded[5], 16)
                V.tensor_reduce(fsum[:].rearrange("p c n -> p (c n)"), staging.rearrange("p (r m) -> p m r", r=8), axis=AX.X, op=ALU.add).then_inc(G.sem, 1)
                s5_dve(dve)
            if n_stages > 6:
                stage_over(dve, 6)
                s6_dve(dve)
            if n_stages > 7:
                stage_over(dve, 7)
                glu_dve(7, dve)

        @block.gpsimd
        def _(pool):
            pool.wait_ge(zero_ready, 1)
            if n_stages > 2:
                def fetch(b, u):
                    pool.dma_start(cnat[:, u], a["ctx"][:, b]).then_inc(c_in[u], 16)
                fetch(0, 0)
                fetch(1, 1)
                ctx_pipeline(pool, fetch)
            for s in range(1 if n_stages > 2 else 0, n_stages):
                stage_over(pool, s)
                pool_stage(s, pool)

        @block.tensor
        def _(pe):
            pe.wait_ge(loaded_c, LOADS_0)
            pe.wait_ge(prep_w.sem, 5)
            give(pe, [(1, "y")])
            s0_pe(pe)
            for s, prog in enumerate((None, lambda: glu_pe(1, pe), lambda: s2_pe(pe), lambda: s3_pe(pe), lambda: (s4_weights_pe(pe), s4_pe(pe)),
                                      lambda: s5_pe(pe), lambda: s6_pe(pe), lambda: glu_pe(7, pe))):
                if 0 < s < n_stages:
                    stage_over(pe, s)
                    if s in (1, 3):
                        pe.wait_ge(w_loaded[1], 16)
                    if s == 4:
                        pe.wait_ge(w_loaded[3], 48)
                    if s == 5:
                        pe.wait_ge(prep_w.sem, 6)
                    if s == 7:
                        pe.wait_ge(w_loaded[7], 16)
                    prog()


LOADS_0 = 16 * (10 + 1 + 4 + 4 + 1)


def layouts(inp):
    def bf16(v):
        u = np.ascontiguousarray(v, np.float32).view(np.uint32).astype(np.uint64)
        return ((u + 0x7FFF + ((u >> 16) & 1)) >> 16).astype(np.uint16)

    def back(bits):
        return (bits.astype(np.uint32) << 16).view(np.float32)

    def chunks(w):
        return np.ascontiguousarray(w.reshape(NC, 128, -1).transpose(1, 0, 2))

    d = {}
    d["x"] = np.ascontiguousarray(inp["x"].transpose(1, 0, 2))
    d["ctxT"] = np.ascontiguousarray(inp["ctx_2048"].reshape(NB, T, NC, 128).transpose(3, 0, 2, 1))
    d["ident"] = np.eye(128, dtype=np.float32)
    g = np.concatenate([inp["g_xattn"], inp["g_ffn"], inp["L1_xattn_gamma"].reshape(1)])
    d["gates"] = np.ascontiguousarray(np.broadcast_to(g, (128, 9)))
    wq = inp["L0_xattn_Wq"].reshape(2 * C, HK0, G0, D0).transpose(0, 2, 1, 3).reshape(2 * C, C)
    d["w0x"] = chunks(np.concatenate([wq[C:], inp["L0_xattn_Wk"], inp["L0_xattn_Wv"]], 1))
    d["w0c"] = chunks(np.concatenate([inp["L0_xattn_Wsk"], inp["L0_xattn_Wsv"], wq[:C]], 1))
    d["w0o"] = np.ascontiguousarray(inp["L0_xattn_Wo"].reshape(HK0, G0, D0, C).transpose(0, 2, 1, 3).reshape(64, G0, C))
    ext = np.zeros((128, HK0, sum(2 * k for k in KEYS_T)), np.float32)
    o = 0
    for qb in range(NQB):
        for c, win in ((0, W_SSM), (1, W_ATT)):
            m = KEYS_T[qb]
            for hk in range(HK0):
                for part in range(3):
                    ext[32 * part + 8 * qb + hk, hk, o:o + m] = 1.0
            delta = (QB * qb + np.arange(QB))[:, None] - np.arange(m)[None, :]
            ext[96:128, :, o:o + m] = np.where((delta >= 0) & (delta < win), 0.0, MASKED)[:, None, :]
            o += m
    d["ext0"] = bf16(ext.reshape(128, -1))
    oh = np.zeros((128, 128), np.float32)
    oh[96:128] = np.tile(np.eye(QB), (1, G0))
    d["mxq0"] = bf16(oh)
    d["ohq0"] = bf16(oh)
    slopes = np.power(np.float32(2.0), -8.0 * np.arange(H0, dtype=np.float32) / H0).astype(np.float32)
    qc = np.zeros((128, H0, R0), np.float32)
    rest = slopes.copy()
    for part in range(3):
        p = back(bf16(rest))
        qc[:, :, 48 + part] = p.reshape(HK0, G0).T.reshape(-1)
        rest = rest - p
    kc = np.zeros((128, 2, HK0, R0), np.float32)
    kc[:, :, :, 48:51] = (np.arange(T) - 64)[:, None, None, None]
    d["q_const"], d["k_const"] = bf16(qc), bf16(kc)
    def units(gate, value, down):
        up = np.stack([gate, value], 2).reshape(-1, NC, 128, 2, 128).transpose(2, 0, 1, 3, 4)
        return up.reshape(128, -1), down.transpose(1, 0, 2).reshape(128, -1)

    up, down = units(inp["L0_ffn_w1"], inp["L0_ffn_w2"], inp["L0_ffn_w3"])
    d["w13"] = np.ascontiguousarray(np.concatenate([up, down, chunks(inp["L1_ffn_expert_w"].transpose(2, 0, 1).reshape(C, -1)).reshape(128, -1)], 1))
    w12 = inp["L3_ffn_w12"].transpose(0, 2, 1)
    s1, s2 = (inp[n].reshape(8, 128, C).transpose(0, 2, 1) for n in ("L3_ffn_sw1", "L3_ffn_sw2"))
    down = np.concatenate([inp["L3_ffn_w3"].transpose(0, 2, 1), inp["L3_ffn_sw3"].T.reshape(8, 128, C)])
    d["w7"] = np.ascontiguousarray(np.concatenate(units(np.concatenate([w12[:, :, :128], s1]), np.concatenate([w12[:, :, 128:], s2]), down), 1))
    d["wr"] = np.ascontiguousarray(np.stack([chunks(inp[n].T) for n in ("L0_ffn_router_w", "L1_ffn_gate_w", "L3_ffn_router_w")], 1))
    d["iota8"] = np.ascontiguousarray(np.broadcast_to(np.arange(8, dtype=np.float32), (128, 8)))
    d["sbias"] = np.ascontiguousarray(np.broadcast_to(inp["L3_ffn_expert_bias"], (128, 8)))
    eb = np.zeros((96, TOP_E * C), np.float32)
    eb[0:96:32] = inp["L1_ffn_expert_b"].reshape(-1)
    d["eb"] = eb
    d["ctx"] = np.ascontiguousarray(inp["ctx_2048"].transpose(1, 0, 2))
    v = np.ones((128, NB, 2, 8, 17), np.float32)
    v[..., :16] = inp["ctx_2048"].reshape(NB, 8, 16, 2, 128).transpose(4, 0, 3, 1, 2)
    d["ctxT17"] = v
    sel = np.zeros((96, 8, 128), np.float32)
    for h in range(8):
        sel[h:24:8, h] = 1.0
    d["sel2"] = bf16(sel)
    wk = np.zeros((C, 4, 4, 32), np.float32)
    wk[..., :16] = inp["L2_xattn_wk"].T.reshape(C, 4, 4, 16)
    d["wkT"] = np.ascontiguousarray(chunks(wk.reshape(C, -1)).reshape(128, NC, 4, 128))
    bk = np.zeros((4, 4, 32), np.float32)
    bk[..., :16] = inp["L2_xattn_bk"].reshape(4, 4, 16)
    d["bkc"] = np.ascontiguousarray(bk.reshape(4, 128).T)
    d["wvT"] = chunks(inp["L2_xattn_wv"].T)
    d["rows4"] = np.ascontiguousarray(np.broadcast_to(np.stack([inp["L2_xattn_bq"], inp["L2_xattn_bv"], inp["L2_xattn_bo"]]), (128, 3, C)))
    d["w4n"] = np.ascontiguousarray(np.stack([inp[n].reshape(2, 128, C).transpose(1, 0, 2) for n in ("L2_xattn_wq", "L2_xattn_wo")], 1).reshape(128, -1))
    d["mask"] = np.ascontiguousarray(inp["mask_BxSxS2_ff0"].transpose(1, 0, 2))
    d["maskT"] = np.ascontiguousarray(inp["mask_BxSxS2_ff0"].transpose(2, 0, 1))
    sel = np.zeros((96, 16, 128), np.float32)
    for h in range(16):
        sel[h:48:16, h] = 1.0
    d["sel4"] = bf16(sel)
    d["w5"] = np.ascontiguousarray(inp["L2_ffn_factors"].reshape(8, NC, 128, C).transpose(2, 0, 1, 3).reshape(128, -1))
    d["fb"] = np.ascontiguousarray(np.broadcast_to(inp["L2_ffn_bias"], (128, C)))
    return d


def kernel(**inputs):
    import numpy as _np
    import concourse.bacc as _bacc
    from concourse import mybir as _mybir
    from concourse.bass_utils import run_bass_kernel_spmd as _run

    nc = _bacc.Bacc("TRN2", target_bir_lowering=False, num_devices=1)
    arrays, a = {}, {}
    for name, v in layouts(inputs).items():
        arrays["in_" + name] = v
        a[name] = nc.dram_tensor("in_" + name, v.shape, _mybir.dt.from_np(v.dtype), kind="ExternalInput").ap()
    out = nc.dram_tensor("out", (T, NB, C), F32, kind="ExternalOutput").ap()
    bass_program(nc, a, out)
    r = _run(nc, [arrays], core_ids=[0])
    return _np.ascontiguousarray(r.results[0]["out"].transpose(1, 0, 2))
```

```python
import numpy as np
from contextlib import ExitStack

import concourse.bass as bass
from concourse import mybir

F32 = mybir.dt.float32
BF16 = mybir.dt.bfloat16
F32R = mybir.dt.float32r
U32 = mybir.dt.uint32
ALU = mybir.AluOpType
ACT = mybir.ActivationFunctionType
AX = mybir.AxisListType

NB = 16
T = 128
C = 256
NC = C // 128
EPS_LN = 1e-5

H0, HK0, D0 = 32, 8, 8
G0 = H0 // HK0
QB = 32
NQB = T // QB
W_SSM, W_ATT = 64, 32
R0 = 64
MASKED = -1e30
KEYS_T = [64, 64, 128, 128]
KEYS_Q = [(0, 32), (0, 64), (0, 96), (32, 96)]
FILLS_Q = [(0, 0, 4), (1, 0, 4), (2, 0, 2), (2, 2, 2), (3, 0, 2), (3, 2, 2)]
FILLS_T = [(0, 2), (1, 2), (2, 0), (2, 1), (3, 0), (3, 1)]

TOP_E = 8


class Flag:

    def __init__(self, sem, per, credit=0, base=0):
        self.sem, self.per, self.credit = sem, per, base + credit
        self.given = credit

    def at(self, item, k):
        return item * self.per + (k + self.credit)


def bass_program(nc, a, out, n_stages=8):
    ctx = ExitStack()
    with ctx:
        def sb(name, shape, dt=F32):
            return ctx.enter_context(nc.sbuf_tensor(name, shape, dt))

        def sem(name):
            return ctx.enter_context(nc.semaphore(name))

        def flag(name, per, credit=0):
            return Flag(sem(name), per, credit)

        psum = ctx.enter_context(nc.psum_tensor("psum", [128, 8 * 512], F32))

        def bank(n, k=1):
            return psum[:, 512 * n:512 * (n + k)]

        x = sb("x", [128, NB, C])
        ident = sb("ident", [128, 128])
        identb = sb("identb", [128, 128], BF16)
        gates = sb("gates", [128, 9])
        loaded_x = sem("loaded_x")
        loaded_c = sem("loaded_c")
        gates_ready = sem("gates_ready")
        x_done = Flag(sem("x_done"), 1)
        stats = sb("stats", [128, 4, 6])
        mv = sb("mv", [128, 4, 2])
        veps = sb("veps", [128, 4, 1])
        rstd = sb("rstd", [128, 4, 1])
        minus_half = sb("minus_half", [128, 1])
        xn = sb("xn", [128, 2, 2, C])
        xnT = sb("xnT", [128, 2, NC, 2 * T])
        zero_ready = sem("zero_ready")
        waited = sem("waited")

        w_attn = sb("w_attn", [128, 2560])
        w0x = w_attn[:, 0:768].rearrange("p (c n) -> p c n", c=NC)
        w0c = w_attn[:, 768:1536].rearrange("p (c n) -> p c n", c=NC)
        w0o = w_attn[0:64, 1536:2560].rearrange("p (g n) -> p g n", g=G0)
        ext0 = sb("ext0", [128, HK0 * sum(2 * k for k in KEYS_T)], BF16)
        mxq0 = sb("mxq0", [128, 128], BF16)
        ohq0 = sb("ohq0", [128, 128], BF16)
        ctxT = sb("ctxT", [128, 2, NC, T])
        q_f = sb("q_f", [128, 2, C])
        kv_f = sb("kv_f", [128, 2, 2, 128])
        q_r = sb("q_r", [128, C])
        k_r = sb("k_r", [128, 128])
        k_parts = sb("k_parts", [128, 2, 2, HK0, R0], BF16)
        qT0 = sb("qT0", [128, HK0 // 2, NQB, G0, QB], BF16)
        kT0 = sb("kT0", [128, HK0 // 2, 2, T], BF16)
        mx0 = sb("mx0", [128, NQB, HK0 // 2, 2])
        mxr0 = sb("mxr0", [128, 32])
        mxp0 = sb("mxp0", [128, 3, 32], BF16)
        PT = sb("PT", [128, 12 * 512])
        rden = sb("rden", [128, 512])
        bc_sb = sb("bc_sb", [128, 512])
        sel0 = sb("sel0", [128, 64])
        o_n = sb("o_n", [128, NQB, 64])
        oT0 = sb("oT0", [64, G0, T])

        arena = sb("arena", [128, 10240 + 3904])
        tail = arena[:, 10240:]
        v0 = arena[:, 10240:14080].rearrange("p (s c w) -> p s c w", s=2, c=3)
        w1a = arena[:, 0:4096].rearrange("p (e c v m) -> p e c v m", e=TOP_E, c=NC, v=2)
        w1b = arena[:, 4096:6144].rearrange("p (e n) -> p e n", e=TOP_E)
        w3e = arena[:, 6144:10240].rearrange("p (c n) -> p c n", c=NC)
        w7a = arena[:, 0:8192].rearrange("p (e c v m) -> p e c v m", e=16, c=NC, v=2)
        w7b = arena[:, 8192:12288].rearrange("p (e n) -> p e n", e=16)
        wr = sb("wr", [128, 3, NC, TOP_E])
        iota8 = sb("iota8", [128, TOP_E])
        ebias = sb("ebias", [96, TOP_E * C], BF16)
        ones96 = sb("ones96", [96, 128], BF16)
        sbias = sb("sbias", [128, TOP_E])
        staging = PT[:, 0:4096]
        half = sb("half", [128, 2, 9])
        lg = sb("lg", [128, 2, TOP_E])
        sg8 = sb("sg8", [128, 2, TOP_E])
        sel8 = sb("sel8", [128, 2, TOP_E])
        v8 = sb("v8", [128, 2, 8])
        i8 = sb("i8", [128, 2, 8], U32)
        idf = sb("idf", [128, 2, 2])
        dl = sb("dl", [128, 2, 1])
        th = sb("th", [128, 2, 8])
        wk = sb("wk", [128, 2, 2])
        den = sb("den", [128, 2, 1])
        oh = sb("oh", [128, 2, 2, TOP_E])
        ohs = sb("ohs", [128, 2, 2, TOP_E])
        cw = sb("cw", [128, 2, TOP_E])
        sil = sb("sil", [128, 2, 2 * T])
        hT = sb("hT", [128, 2, 2 * T])
        qop = ext0[0:96, 0:4096].rearrange("p (s h n) -> p s h n", s=2, h=8)
        xparts = sb("xparts", [128, 2, 3, C], BF16)
        xres = sb("xres", [128, C])
        v_raw = sb("v_raw", [128, 2, 2 * 128])
        v2a = tail[:, 0:1344].rearrange("p (s l w) -> p s l w", s=2, l=2)
        v2b = tail[:, 1344:3904].rearrange("p (s l w) -> p s l w", s=2, l=2)
        rd2 = sb("rd2", [68, C])
        sel2s = sb("sel2s", [68, 128])
        v2_ready = sem("v2_ready")
        sel2 = sb("sel2", [96, 8, 128], BF16)
        mxq2 = sb("mxq2", [96, C], BF16)
        mx2 = sb("mx2", [128, 2, 8])
        mxr2 = sb("mxr2", [128, 2, 8])
        mxp2 = sb("mxp2", [128, 2, 3, 8], BF16)
        gg = sb("gg", [128, 1])
        cnat = sb("cnat", [128, 2, C])
        cparts = sb("cparts", [128, 2, 3, C], BF16)
        cres = sb("cres", [128, C])
        wkT = w_attn[:, 0:1024].rearrange("p (c g m) -> p c g m", c=NC, g=4)
        wvT = w_attn[:, 1024:1536].rearrange("p (c n) -> p c n", c=NC)
        sel4 = w_attn[0:96, 1536:2560].bitcast(BF16).rearrange("p (h m) -> p h m", h=16)
        bkc = sb("bkc", [128, 4])
        rows4 = sb("rows4", [128, 5, C])
        qwT = sb("qwT", [128, 2, NC, C], BF16)
        qw = sb("qw", [128, 2, 2, C], BF16)
        wsc = sb("wsc", [128, 4, 2, 2])
        diag = staging[:, 1024:1536].rearrange("p (n m) -> p n m", n=4)
        onesf = sb("onesf", [128, 128])
        qsc = sb("qsc", [128, 2, 4])
        qt_f = sb("qt_f", [128, C])
        qx = sb("qx", [128, C], BF16)
        qxT = sb("qxT", [128, NC, T], BF16)
        q_tmp = sb("q_tmp", [128, C])
        qpad = sb("qpad", [128, 16, 32])
        qT4 = qT0[:].rearrange("p j b g q -> p (j b g q)").bitcast(F32).rearrange("p (s g t) -> p s g t", s=2, g=4)
        kT4 = k_parts[:].rearrange("p s c h r -> p (s c h r)").bitcast(F32).rearrange("p (s g t) -> p s g t", s=2, g=4)
        v4 = tail[:, 0:2688].rearrange("p (s r w) -> p s r w", s=2, r=4)
        v4_ready = sem("v4_ready")
        msk = q_f[:].rearrange("p s (w t) -> p s w t", w=2)
        mxq4 = sb("mxq4", [96, 128], BF16)
        mx4 = sb("mx4", [128, 16])
        mxr4 = sb("mxr4", [128, 16])
        mxp4 = sb("mxp4", [128, 3, 16], BF16)
        osc = sb("osc", [128, 4])
        fsum = kv_f[:].rearrange("p s c k -> p (s c k)").rearrange("p (c n) -> p c n", c=NC)
        fb = sb("fb", [128, C])
        gs5 = sb("gs5", [128, 1])

        qo = sb("qo", [128, C], BF16)
        qoT = sb("qoT", [128, NC, T], BF16)
        with nc.sbuf_tensor("q_parts", [128, 2, H0, R0], BF16) as q_parts:
            kop = q_parts[:].rearrange("p s h r -> p (s h r)")[0:96].rearrange("p (s h n) -> p s h n", s=2, h=8)
        mskp = sb("mskp", [128, 2, 2, 2, T], F32R)
        ident_r = sb("ident_r", [128, 128], F32R)
        eb_f = PT[0:96, 0:2048]
        eb_r = PT[0:96, 2048:4096]
        eb_b = PT[0:96, 4096:5120].bitcast(BF16)

        kscr = nc.dram_tensor("kscr", (NB, 3, 128, C), BF16, kind="Internal").ap()
        qscr = nc.dram_tensor("qscr", (2, 3, 128, C), BF16, kind="Internal").ap()
        ends = {}
        w_loaded = [sem(f"w_loaded{k}") for k in range(8)]
        prep_w = Flag(sem("prep_w"), 0)

        f = {}
        shared = {}

        def stage_flags(s, names, n_items=NB):
            for n, per, credit in names:
                count = NB // 2 if n[-1] in "01" else NB if (n, per, credit) in LN else n_items
                if (n, credit) not in shared:
                    shared[n, credit] = [sem(n + (f"_{credit}" if credit else "")), 0]
                entry = shared[n, credit]
                f[s, n] = Flag(entry[0], per, credit, entry[1])
                entry[1] += per * count

        given = set()

        def give(eng, keys):
            for key in keys:
                fl = f.get(key)
                if fl and fl.given and (key[1], fl.given) not in given:
                    given.add((key[1], fl.given))
                    eng.sem_inc(fl.sem, fl.given)

        LN = [("stats", 1, 0), ("mv", 1, 0), ("veps", 1, 0), ("rstd", 1, 0), ("xn", 1, 0)]

        stage_flags(0, [
            ("ctx_loaded0", 16, 0), ("ctx_loaded1", 16, 0),
            ("stats", 1, 0), ("mv", 1, 0), ("veps", 1, 0), ("rstd", 1, 0), ("xn", 1, 0), ("xnT_psum", 1, 0), ("xnT", 1, 0),
            ("qkv_psum", 1, 0), ("qkv", 2, 0), ("parts", 8, 0), ("kT_psum", 1, 0), ("qT_psum", 2, 0), ("qkT", 3, 0),
            ("sq", 6, 0), ("mx", 6, 0), ("mparts", 4, 0), ("mxT_psum", 1, 0), ("mxT", 1, 0),
            ("st", 6, 0), ("p", 6, 2), ("pv", 1, 0), ("rden", 1, 0), ("bc_psum", 1, 0), ("bc", 1, 0), ("oT", 1, 0), ("y", 1, 0)])


        def ff_flags(s):
            n = {1: 8, 3: 4, 5: 1, 7: 16}[s]
            names = LN + [("xnT_psum", 1, 0), ("xnT", 1, 0), ("y", n, 2 if s in (1, 7) else 0),
                          ("acc", {1: 8, 3: 16, 5: 1, 7: 9}[s], {1: 2, 3: 8, 5: 2, 7: 2}[s])]
            if s == 5:
                names += [("bias", 1, 0)]
            else:
                names += [("lg_psum", 1, 0), ("lg", 1, 1), ("route", {1: 10, 3: 10, 7: 16}[s], 0), ("tanh", 1, 0)]
            if s in (1, 7):
                names += [("up", n, 0), ("silu", n, 0), ("h", n, 2)]
            stage_flags(s, names, NB // 2)

        ff_flags(1)
        stage_flags(2, LN + [("parts", 5, 0), ("q_stored0", 16, 0), ("q_stored1", 16, 0), ("q_loaded0", 96, 0), ("q_loaded1", 96, 0),
                             ("k_loaded0", 96, 0), ("k_loaded1", 96, 0), ("v_loaded0", 16, 0), ("v_loaded1", 16, 0), ("v", 1, 0),
                             ("sq", 4, 0), ("mx", 4, 0), ("mparts", 4, 0), ("mxT_psum", 1, 0), ("mxT", 1, 0), ("st", 4, 0), ("p", 4, 2),
                             ("pv", 1, 0), ("rden", 1, 0), ("bc_psum", 1, 0), ("bc", 1, 0), ("on", 1, 0)])
        ff_flags(3)
        stage_flags(4, LN + [("ctx_loaded0", 16, 0), ("ctx_loaded1", 16, 0), ("msk_loaded0", 32, 0), ("msk_loaded1", 32, 0), ("msk", 2, 0), ("quant", 6, 0), ("xT_psum", 1, 0), ("xT", 1, 0), ("q_psum", 1, 0), ("k_psum", 1, 0),
                             ("qdve", 3, 0), ("k", 4, 0), ("qT_psum", 1, 0), ("qT", 1, 0), ("sq", 2, 0), ("mx", 2, 0), ("mparts", 4, 0),
                             ("mxT_psum", 1, 0), ("mxT", 1, 0), ("st", 2, 0), ("p", 2, 2), ("pv", 1, 0), ("pvc", 1, 0), ("pvT", 1, 0), ("rden", 1, 0), ("on", 1, 0),
                             ("oquant", 6, 0), ("oT_psum", 1, 0), ("oT", 1, 0), ("y", 1, 0), ("fin", 2, 0)])
        ff_flags(5)
        stage_flags(6, LN + [("ctx_loaded0", 32, 0), ("ctx_loaded1", 32, 0), ("s_psum", 1, 0), ("s", 1, 0), ("y", 1, 0)])
        ff_flags(7)
        ends[0] = (x_done.sem, NB)
        for s in (1, 3, 5, 7):
            fl = f[s, "acc"]
            ends[s] = (fl.sem, fl.at(NB // 2, 0))
        for n, s in enumerate((2, 4, 6)):
            ends[s] = (x_done.sem, NB * (n + 2))

        block = ctx.enter_context(nc.Block())

        def items(eng, front, back, n=NB, unroll=2):
            front(0, 0, 0)
            with eng.Fori(0, n // unroll - 1) as i:
                for u in range(unroll):
                    back(i * unroll + u, u % 2, lambda v=u: front(i * unroll + (v + 1), (v + 1) % 2, i + (v + 1) // 2))
            for b in range(n - unroll, n):
                nxt = (lambda v=b: front(v + 1, (v + 1) % 2, (v + 1) // 2)) if b + 1 < n else (lambda: None)
                back(b, b % 2, nxt)

        def plain(eng):
            eng.sem_inc(waited, 1)

        def s0_sp(sp):
            F = lambda n: f[0, n]
            def load(b, s):
                sp.dma_start(ctxT[:, s], a["ctxT"][:, b]).then_inc(F(f"ctx_loaded{s}").sem, 16)
            load(0, 0)
            load(1, 1)
            with sp.Fori(0, NB // 2 - 1) as i:
                for u in range(2):
                    sp.wait_ge(F("qkv_psum").sem, F("qkv_psum").at(i * 2 + u, 1))
                    load(i * 2 + (u + 2), u)

        def ln_stats(s, dve, b, slot, i4):
            F = lambda n: f[s, n]
            nc.vector.bn_stats(stats[:, i4], x[:, b]).then_inc(F("stats").sem, 1)
            dve.wait_ge(F("stats").sem, F("stats").at(b, 1))
            plain(dve)
            nc.vector.bn_aggr(mv[:, i4], stats[:, i4]).then_inc(F("mv").sem, 1)

        def ln_apply(s, dve, b, i4, out_):
            F = lambda n: f[s, n]
            dve.wait_ge(F("rstd").sem, F("rstd").at(b, 1))
            nc.vector.tensor_scalar(out_, x[:, b], mv[:, i4, 0:1], rstd[:, i4], ALU.subtract, ALU.mult).then_inc(F("xn").sem, 1)

        def rstd_step(st, pool):
            F = lambda n: f[st, n]

            def rs(b, s):
                pool.wait_ge(F("mv").sem, F("mv").at(b, 1))
                plain(pool)
                nc.gpsimd.tensor_scalar(veps[:, s], mv[:, s, 1:2], EPS_LN, None, ALU.add).then_inc(F("veps").sem, 1)
                pool.wait_ge(F("veps").sem, F("veps").at(b, 1))
                nc.gpsimd.tensor_tensor(rstd[:, s], veps[:, s], minus_half[:], ALU.pow).then_inc(F("rstd").sem, 1)
            return rs

        def pool_stage(st, pool):
            rs = rstd_step(st, pool)
            step = 4 if st % 2 else 2
            with pool.Fori(0, NB // step) as i:
                for u in range(step):
                    rs(i * step + u, u)

        def split3(V, eng, src, dst, res, fl, item, k0=0):
            if V is nc.gpsimd:
                plain(eng)
            V.tensor_copy(dst(0), src).then_inc(fl.sem, 1)
            eng.wait_ge(fl.sem, fl.at(item, k0 + 1))
            V.tensor_tensor(res, src, dst(0), ALU.subtract).then_inc(fl.sem, 1)
            eng.wait_ge(fl.sem, fl.at(item, k0 + 2))
            if V is nc.gpsimd:
                plain(eng)
            V.tensor_copy(dst(1), res).then_inc(fl.sem, 1)
            eng.wait_ge(fl.sem, fl.at(item, k0 + 3))
            V.tensor_tensor(dst(2), res, dst(1), ALU.subtract).then_inc(fl.sem, 1)

        def pipeline(eng, first, body, last, ahead=1):
            first()
            body(None, 0, ahead, 0, ahead // 2, 0)
            loops = (NB - 1 - ahead) // 2
            with eng.Fori(0, loops) as i:
                for u in range(2):
                    body(i * 2 + u, i * 2 + (u + 1), i * 2 + (u + 1 + ahead), (u + 1) % 2, i + (1 + u + ahead) // 2, i + (1 + u) // 2)
            for b in range(2 * loops + 1, NB):
                n = b + ahead if b + ahead < NB else None
                body(b - 1, b, n, b % 2, n and n // 2, b // 2)
            last(NB - 1, (NB - 1) % 2)

        def s0_dve(dve):
            F = lambda n: f[0, n]
            V = nc.vector

            def wait(n, b, k):
                dve.wait_ge(F(n).sem, F(n).at(b, k))

            def split(b, s):
                P = F("parts")
                qv = q_f[:, s].rearrange("p (h d) -> p h d", d=D0)
                rv = q_r[:].rearrange("p (h d) -> p h d", d=D0)
                qp = lambda n, k, step=2: q_parts[:, s, :, 0:48].rearrange("p h (r d) -> p h r d", d=D0)[:, :, n:n + step * (k - 1) + 1:step]
                wait("qkv", b, 2)
                V.tensor_copy(qp(0, 3), qv.unsqueeze(2).to_broadcast([128, H0, 3, D0])).then_inc(P.sem, 1)
                kf = kv_f[:, s, :, 0:64].rearrange("p c (h d) -> p c h d", d=D0)
                kr = k_r[:].rearrange("p (c h d) -> p c h d", c=2, d=D0)
                kp = lambda n: k_parts[:, s, :, :, 8 * n:8 * n + 8]
                V.tensor_copy(kp(0), kf).then_inc(P.sem, 1)
                V.tensor_copy(kp(1), kf)
                V.tensor_copy(kp(5), kf)
                dve.wait_ge(P.sem, P.at(b, 1))
                V.tensor_tensor(rv, qv, qp(0, 1).rearrange("p h o d -> p h (o d)"), ALU.subtract).then_inc(P.sem, 1)
                dve.wait_ge(P.sem, P.at(b, 2))
                V.tensor_tensor(kr, kf, kp(0), ALU.subtract).then_inc(P.sem, 1)
                dve.wait_ge(P.sem, P.at(b, 3))
                V.tensor_copy(qp(1, 2), rv.unsqueeze(2).to_broadcast([128, H0, 2, D0])).then_inc(P.sem, 1)
                dve.wait_ge(P.sem, P.at(b, 4))
                V.tensor_copy(kp(2), kr)
                V.tensor_copy(kp(3), kr).then_inc(P.sem, 1)
                dve.wait_ge(P.sem, P.at(b, 5))
                V.tensor_tensor(qp(5, 1).rearrange("p h o d -> p h (o d)"), rv, qp(1, 1).rearrange("p h o d -> p h (o d)"), ALU.subtract)
                dve.wait_ge(P.sem, P.at(b, 6))
                V.tensor_tensor(kp(4), kr, kp(3), ALU.subtract).then_inc(P.sem, 1)
                vv = v0[:, s].rearrange("p c (h w) -> p c h w", h=HK0)[:, :, :, 0:D0]
                kvv = kv_f[:, s, :, 64:128].rearrange("p c (h d) -> p c h d", d=D0)
                V.tensor_copy(vv[0:64, 2], kvv[0:64, 0])
                V.tensor_copy(vv[64:128, 2], kvv[0:64, 1])
                V.tensor_copy(vv[:, 0:2], kvv).then_inc(P.sem, 1)

            def finish(p):
                wait("pv", p, 1)
                V.reciprocal(rden[64:72], bank(3)[64:72]).then_inc(F("rden").sem, 1)
                wait("bc_psum", p, 1)
                V.tensor_copy(bc_sb[0:64], bank(1)[0:64]).then_inc(F("bc").sem, 1)
                wait("bc", p, 1)
                V.tensor_tensor(oT0[:].rearrange("p g (b q) -> p b g q", b=NQB), bank(3)[0:64].rearrange("p (b g q) -> p b g q", b=NQB, g=G0),
                                bc_sb[0:64].rearrange("p (b g q) -> p b g q", b=NQB, g=G0), ALU.mult).then_inc(F("oT").sem, 1)

            def update(p):
                wait("y", p, 1)
                V.scalar_tensor_tensor(x[:, p], bank(2)[:, 0:C], gates[:, 0:1], x[:, p], ALU.mult, ALU.add).then_inc(x_done.sem, 1)

            def first():
                ln_stats(0, dve, 0, None, 0)
                ln_apply(0, dve, 0, 0, xn[:, 0, 0])
                split(0, 0)

            def body(p, b, n, s, turn, turn_b):
                if n is not None:
                    ln_stats(0, dve, n, None, 1 - s)
                for k, (qb, j, m) in enumerate(FILLS_Q):
                    w = 2 * KEYS_Q[qb][1]
                    wait("sq", b, k + 1)
                    src = bank(4 + 2 * (k % 2), 2).rearrange("p (e c) -> p e c", e=2)[:, :, 0:m * w].rearrange("p e (j w) -> p e j w", w=w)
                    V.tensor_reduce(mx0[:, qb, j:j + m].rearrange("p j e -> p e j"), src, axis=AX.X, op=ALU.max, negate=True).then_inc(F("mx").sem, 1)
                wait("mx", b, 6)
                split3(V, dve, mx0[:].rearrange("p q j e -> p (q j e)"), lambda r: mxp0[:, r], mxr0[:], F("mparts"), b)
                if n is not None:
                    ln_apply(0, dve, n, 1 - s, xn[:, 1 - s, 0])
                wait("mxT_psum", b, 1)
                V.tensor_copy(mxq0[0:96, :], bank(2).bitcast(BF16)[0:96, 0:128]).then_inc(F("mxT").sem, 1)
                if p is not None:
                    finish(p)
                    update(p)
                if n is not None:
                    split(n, 1 - s)

            def last(p, s):
                finish(p)
                update(p)

            pipeline(dve, first, body, last)

        def s0_act(act):
            F = lambda n: f[0, n]
            A = nc.scalar

            def wait(n, b, k):
                act.wait_ge(F(n).sem, F(n).at(b, k))

            def copy_xnT(b, s):
                wait("xnT_psum", b, 1)
                A.copy(xnT[:, s, :, 0:T], bank(0)[:, 0:C].rearrange("p (c t) -> p c t", c=NC)).then_inc(F("xnT").sem, 1)

            def copy_qkv(b, s):
                wait("qkv_psum", b, 1)
                A.activation(q_f[:, s], bank(0)[:, 128:384], ACT.Copy, scale=float(D0) ** -0.5).then_inc(F("qkv").sem, 1)
                A.copy(kv_f[:, s], bank(0).rearrange("p (c k) -> p c k", c=4)[:, 0:4:3, :]).then_inc(F("qkv").sem, 1)

            def first():
                copy_xnT(0, 0)
                copy_qkv(0, 0)

            def body(p, b, n, s, turn, turn_b):
                wait("kT_psum", b, 1)
                A.copy(kT0[:], bank(1).bitcast(BF16).rearrange("p (j c t) -> p j c t", j=4, c=2)).then_inc(F("qkT").sem, 1)
                for k in range(2):
                    wait("qT_psum", b, k + 1)
                    src = bank(1 + (k + 1) % 2).bitcast(BF16).rearrange("p (j g b q) -> p j b g q", j=2, g=G0, b=NQB)
                    A.copy(qT0[:, 2 * k], src[:, 0])
                    A.copy(qT0[:, 2 * k + 1], src[:, 1]).then_inc(F("qkT").sem, 1)
                for k in range(6):
                    wait("st", b, k + 1)
                    A.activation(PT[:, 1024 * k:1024 * (k + 1)], bank(4 + 2 * (k % 2), 2), ACT.Exp).then_inc(F("p").sem, 1)
                    if n is not None:
                        if k == 1:
                            copy_xnT(n, 1 - s)
                        if k == 3:
                            copy_qkv(n, 1 - s)

            pipeline(act, first, body, lambda p, s: None)

        def s0_pe(pe):
            F = lambda n: f[0, n]
            MM = nc.tensor.matmul

            def wait(n, b, k):
                pe.wait_ge(F(n).sem, F(n).at(b, k))

            def transpose_xn(b, s):
                wait("xn", b, 1)
                for c in range(NC):
                    t = nc.tensor.transpose(bank(0)[:, 128 * c:128 * (c + 1)], xn[:, s, 0, 128 * c:128 * (c + 1)], ident[:])
                t.then_inc(F("xnT_psum").sem, 1)

            def project(b, s, turn):
                wait(f"ctx_loaded{s}", turn, 16)
                wait("xnT", b, 1)
                for c in range(NC):
                    MM(bank(0)[:, 128:512], xnT[:, s, c, 0:T], w0x[:, c], start=(c == 0), stop=False, skip_group_check=True)
                for c in range(NC):
                    t = MM(bank(0)[:, 0:384], ctxT[:, s, c], w0c[:, c], start=False, stop=(c == NC - 1), skip_group_check=True)
                t.then_inc(F("qkv_psum").sem, 1)

            def values(b, s, blocks):
                for qb in blocks:
                    ks = [qb] if qb < 2 else [2 * qb - 2, 2 * qb - 1]
                    wait("p", b, ks[-1] + 1)
                    for hk in range(HK0):
                        for k in ks:
                            t = MM(bank(3)[0:72, 128 * qb:128 * (qb + 1)], v0[:, s, FILLS_T[k][1], 72 * hk:72 * (hk + 1)],
                                   PT[:].rearrange("p (k e j r) -> p k e j r", k=6, e=2, j=4)[:, k, hk % 2, hk // 2],
                                   start=(qb == 0 and hk == 0), stop=(hk == HK0 - 1 and k == ks[-1]), skip_group_check=True)
                if blocks[-1] == NQB - 1:
                    t.then_inc(F("pv").sem, 1)

            def spread(p):
                wait("rden", p, 1)
                MM(bank(1)[0:64], sel0[64:72], rden[64:72], start=True, stop=True).then_inc(F("bc_psum").sem, 1)

            def output(p):
                wait("oT", p, 1)
                for g in range(G0):
                    t = MM(bank(2)[:, 0:C], oT0[:, g], w0o[:, g], start=(g == 0), stop=(g == G0 - 1))
                t.then_inc(F("y").sem, 1)

            def q_op(hk, qb):
                r = 64 * (hk % 2)
                return qT0[r:r + 64, hk // 2, qb].rearrange("p g q -> p (g q)")

            def k_op(hk, c, k0, n):
                r = 64 * (hk % 2)
                return kT0[r:r + 64, hk // 2, c, k0:k0 + n]

            base = [0, 128, 256, 512]

            def ext(hk, qb, c, k0, n):
                o = 768 * hk + base[qb] + c * KEYS_T[qb] + k0
                return ext0[:, o:o + n]

            def body(p, b, n, s, turn, turn_b):
                if p is not None:
                    values(p, 1 - s, (0, 1))
                P = F("parts")
                kb, qa = bank(1).bitcast(BF16), bank(2).bitcast(BF16)
                pe.wait_ge(P.sem, P.at(b, 7))
                for j in range(4):
                    for c in range(2):
                        o = (j * 2 + c) * 128
                        t = nc.tensor.transpose(kb[:, o:o + 128], k_parts[:, s, c, 2 * j:2 * j + 2, :].rearrange("p h r -> p (h r)"), identb[:])
                t.then_inc(F("kT_psum").sem, 1)
                for k in range(2):
                    if k == 1:
                        if p is not None:
                            values(p, 1 - s, (2,))
                        wait("qkT", b, 1)
                    for j in range(2):
                        for g in range(G0):
                            o = (j * 4 + g) * 128
                            hk = 2 * (2 * k + j)
                            t = nc.tensor.transpose((qa if k == 0 else kb)[:, o:o + 128], q_parts[:, s, HK0 * g + hk:HK0 * g + hk + 2, :].rearrange("p h r -> p (h r)"), identb[:])
                    t.then_inc(F("qT_psum").sem, 1)
                wait("qkT", b, 3)
                for k, (qb, j0, m) in enumerate(FILLS_Q):
                    k0, w = KEYS_Q[qb]
                    if k < 2:
                        pe.wait_ge(F("p").sem, F("p").at(b, 0) - 1 + k)
                    else:
                        wait("mx", b, k - 1)
                    for e in range(2):
                        o = bank(4 + 2 * (k % 2) + e)
                        for j in range(m):
                            mk = ext0[:, base[qb]:base[qb] + 2 * KEYS_T[qb]].rearrange("p (c m) -> p c m", c=2)[:, :, k0:k0 + w]
                            MM(o[:, 2 * w * j:2 * w * (j + 1)], ohq0[:], mk, start=(j == 0), stop=False, skip_group_check=True)
                    for e in range(2):
                        o = bank(4 + 2 * (k % 2) + e)
                        for j in range(m):
                            hk = 2 * (j0 + j) + e
                            r = 64 * e
                            t = MM(o[:, 2 * w * j:2 * w * (j + 1)], q_op(hk, qb), kT0[r:r + 64, hk // 2, :, k0:k0 + w],
                                   start=False, stop=True, skip_group_check=True)
                    t.then_inc(F("sq").sem, 1)
                if p is not None:
                    values(p, 1 - s, (3,))
                M = F("mparts")
                pe.wait_ge(M.sem, M.at(b, 4))
                nc.tensor.transpose(bank(2).bitcast(BF16)[0:96, 0:128], mxp0[:].rearrange("p a r -> p (a r)"), identb[:]).then_inc(F("mxT_psum").sem, 1)
                wait("mxT", b, 1)
                for k, (qb, c) in enumerate(FILLS_T):
                    if k < 2:
                        wait("mx", b, 5 + k)
                    else:
                        pe.wait_ge(F("p").sem, F("p").at(b, k - 1))
                    parts = ((0, 0, 64), (1, 64, 64)) if c == 2 else ((c, 0, 128),)
                    for e in range(2):
                        o = bank(4 + 2 * (k % 2) + e)
                        for j in range(4):
                            for cc, r0, m in parts:
                                MM(o[r0:r0 + m, 128 * j:128 * (j + 1)], ext(2 * j + e, qb, cc, 0, m), mxq0[:],
                                   start=(j == 0), stop=False, skip_group_check=True)
                    for e in range(2):
                        o = bank(4 + 2 * (k % 2) + e)
                        for j in range(4):
                            for cc, r0, m in parts:
                                t = MM(o[r0:r0 + m, 128 * j:128 * (j + 1)], k_op(2 * j + e, cc, 0, m), q_op(2 * j + e, qb),
                                       start=False, stop=True, skip_group_check=True)
                    t.then_inc(F("st").sem, 1)
                    if k == 1 and n is not None:
                        transpose_xn(n, 1 - s)
                    if k == 2 and p is not None:
                        spread(p)
                    if k == 3 and n is not None:
                        project(n, 1 - s, turn)
                    if k == 4 and p is not None:
                        output(p)

            def first():
                transpose_xn(0, 0)
                project(0, 0, 0)

            def last(p, s):
                values(p, s, (0, 1, 2, 3))
                spread(p)
                output(p)

            pipeline(pe, first, body, last)

        def stage_over(eng, s):
            if s > 0:
                eng.wait_ge(*ends[s - 1])

        def ff_front_dve(st, dve, p, s):
            for u in range(2):
                ln_stats(st, dve, 2 * p + u, None, 2 * s + u)
            for u in range(2):
                ln_apply(st, dve, 2 * p + u, 2 * s + u, xn[:, s, u])

        def ff_front_pe(st, pe, p, s):
            F = lambda n: f[st, n]
            pe.wait_ge(F("xn").sem, F("xn").at(2 * p + 1, 1))
            for c in range(NC):
                for u in range(2):
                    t = nc.tensor.transpose(bank(0)[:, 256 * c + 128 * u:256 * c + 128 * (u + 1)], xn[:, s, u, 128 * c:128 * (c + 1)], ident[:])
            t.then_inc(F("xnT_psum").sem, 1)

        def ff_front_act(st, act, p, s):
            F = lambda n: f[st, n]
            act.wait_ge(F("xnT_psum").sem, F("xnT_psum").at(p, 1))
            nc.scalar.copy(xnT[:, s], bank(0).rearrange("p (c t) -> p c t", c=NC)).then_inc(F("xnT").sem, 1)

        def router_pe(st, pe, p, s):
            F = lambda n: f[st, n]
            pe.wait_ge(F("xnT").sem, F("xnT").at(p, 1))
            pe.wait_ge(F("lg").sem, F("lg").at(p, 0))
            for u in range(2):
                for c in range(NC):
                    t = nc.tensor.matmul(bank(1)[:, 8 * u:8 * u + 8], xnT[:, s, c, T * u:T * (u + 1)], wr[:, {1: 0, 3: 1, 7: 2}[st], c],
                                         start=(c == 0), stop=(c == NC - 1))
            t.then_inc(F("lg_psum").sem, 1)

        def bc(ap, shape):
            return ap.to_broadcast(shape)

        def router_dve(st, dve, p):
            F = lambda n: f[st, n]
            V = nc.vector
            R = F("route")
            gate = {1: 4, 3: 5, 7: 7}[st]
            k = [0]

            def step(ins):
                k[0] += 1
                ins.then_inc(R.sem, 1)

            def settle(back=0):
                dve.wait_ge(R.sem, R.at(p, k[0] - back))

            dve.wait_ge(F("lg_psum").sem, F("lg_psum").at(p, 1))
            V.tensor_copy(lg[:], bank(1)[:, 0:16].rearrange("p (u e) -> p u e", u=2)).then_inc(F("lg").sem, 1)
            src = lg
            dve.wait_ge(F("lg").sem, F("lg").at(p, 1))
            if st == 7:
                dve.wait_ge(F("tanh").sem, F("tanh").at(p, 1))
                step(V.tensor_scalar(sg8[:], th[:], 0.5, 0.5, ALU.mult, ALU.add))
                settle()
                step(V.tensor_tensor(sel8[:], sg8[:], bc(sbias[:].unsqueeze(1), [128, 2, TOP_E]), ALU.add))
                settle()
                src = sel8
            plain(dve)
            for u in range(2):
                step(V.max(v8[:, u], src[:, u]))
            settle()
            plain(dve)
            for u in range(2):
                step(V.max_index(i8[:, u], v8[:, u], src[:, u]))
            if st != 7:
                step(V.tensor_tensor(dl[:], v8[:, :, 1:2], v8[:, :, 0:1], ALU.subtract))
            settle()
            step(V.tensor_copy(idf[:], i8[:, :, 0:2]))
            settle()
            step(V.tensor_tensor(oh[:], bc(iota8[:].unsqueeze(1).unsqueeze(1), [128, 2, 2, TOP_E]), bc(idf[:].unsqueeze(3), [128, 2, 2, TOP_E]), ALU.is_equal))
            if st != 7:
                dve.wait_ge(F("tanh").sem, F("tanh").at(p, 1))
                V.tensor_scalar(wk[:, :, 0:1], th[:, :, 0:1], half[:, 1, gate:gate + 1], half[:, 0, gate:gate + 1], ALU.mult, ALU.add)
                step(V.tensor_scalar(wk[:, :, 1:2], th[:, :, 0:1], half[:, 0, gate:gate + 1], half[:, 0, gate:gate + 1], ALU.mult, ALU.add))
            else:
                settle()
                step(V.tensor_tensor(ohs[:], oh[:], bc(sg8[:].unsqueeze(2), [128, 2, 2, TOP_E]), ALU.mult))
                settle()
                step(V.tensor_reduce(wk[:], ohs[:], axis=AX.X, op=ALU.add))
                settle()
                step(V.tensor_tensor(den[:], wk[:, :, 0:1], wk[:, :, 1:2], ALU.add))
                settle()
                step(V.tensor_scalar(den[:], den[:], 1e-9, None, ALU.add))
                settle()
                step(V.reciprocal(den[:], den[:]))
                settle()
                step(V.scalar_tensor_tensor(wk[:], wk[:], gates[:, gate:gate + 1], bc(den[:], [128, 2, 2]), ALU.mult, ALU.mult))
            settle()
            step(V.tensor_tensor(ohs[:], oh[:], bc(wk[:].unsqueeze(3), [128, 2, 2, TOP_E]), ALU.mult))
            settle()
            step(V.tensor_tensor(cw[:], ohs[:, :, 0], ohs[:, :, 1], ALU.add))
            assert k[0] == R.per, k
            settle()

        def router_act(st, act, p):
            F = lambda n: f[st, n]
            if st == 7:
                act.wait_ge(F("lg").sem, F("lg").at(p, 1))
                nc.scalar.activation(th[:], lg[:], ACT.Tanh, scale=0.5).then_inc(F("tanh").sem, 1)
            else:
                act.wait_ge(F("route").sem, F("route").at(p, 5))
                nc.scalar.activation(th[:, :, 0:1], dl[:], ACT.Tanh, scale=0.5).then_inc(F("tanh").sem, 1)

        def glu_pe(st, pe):
            F = lambda n: f[st, n]
            MM = nc.tensor.matmul
            wa, wb, n = (w1a, w1b, 8) if st == 1 else (w7a, w7b, 16)

            def front(p, s, turn):
                ff_front_pe(st, pe, p, s)

            def back(p, s, nxt):
                router_pe(st, pe, p, s)
                for j in range(n + 1):
                    if j < n:
                        pe.wait_ge(F("h").sem, F("h").at(p, j - 1))
                        for v in range(2):
                            for c in range(NC):
                                t = MM(bank(2 + j % 2)[:, 256 * v:256 * (v + 1)], wa[:, j, c, v], xnT[:, s, c], start=(c == 0), stop=(c == NC - 1))
                        t.then_inc(F("up").sem, 1)
                    if j == n // 2:
                        nxt()
                    if j > 0:
                        i = j - 1
                        pe.wait_ge(F("h").sem, F("h").at(p, i + 1))
                        if i < 8:
                            pe.wait_ge(F("acc").sem, F("acc").at(p, i - 1 if (st == 1 or i >= 2) else -1))
                        elif i == 8:
                            pe.wait_ge(F("acc").sem, F("acc").at(p, 0))
                        for u in range(2):
                            o = bank(4 + i % 2 if i < 8 else 6)[:, C * u:C * (u + 1)]
                            if i < 8:
                                t = MM(o, hT[:, i % 2, T * u:T * (u + 1)], wb[:, i], start=True, stop=True)
                            else:
                                t = MM(o, hT[:, i % 2, T * u:T * (u + 1)], wb[:, i], start=(i == 8 and u == 0), stop=(i == n - 1), skip_group_check=True)
                        t.then_inc(F("y").sem, 1)

            items(pe, front, back, n=NB // 2)

        def glu_act(st, act):
            F = lambda n: f[st, n]
            n = 8 if st == 1 else 16

            def front(p, s, turn):
                ff_front_act(st, act, p, s)

            def back(p, s, nxt):
                for j in range(n):
                    if j == 1:
                        router_act(st, act, p)
                    act.wait_ge(F("up").sem, F("up").at(p, j + 1))
                    act.wait_ge(F("h").sem, F("h").at(p, j - 1))
                    nc.scalar.activation(sil[:, j % 2], bank(2 + j % 2)[:, 0:256], ACT.Silu).then_inc(F("silu").sem, 1)
                    if j == n // 2:
                        nxt()

            items(act, front, back, n=NB // 2)

        def glu_dve(st, dve):
            F = lambda n: f[st, n]
            V = nc.vector
            n = 8 if st == 1 else 16

            def front(p, s, turn):
                ff_front_dve(st, dve, p, s)

            def back(p, s, nxt):
                acc = F("acc")
                if st == 1:
                    nxt()
                router_dve(st, dve, p)
                if st == 7:
                    nxt()
                for j in range(n + 1):
                    if j < n:
                        dve.wait_ge(F("silu").sem, F("silu").at(p, j + 1))
                        dve.wait_ge(F("y").sem, F("y").at(p, j - 1))
                        V.tensor_tensor(hT[:, j % 2], sil[:, j % 2], bank(2 + j % 2)[:, 256:512], ALU.mult).then_inc(F("h").sem, 1)
                    if 0 < j <= 8:
                        i = j - 1
                        dve.wait_ge(F("y").sem, F("y").at(p, i + 1))
                        if i > 0:
                            dve.wait_ge(acc.sem, acc.at(p, i))
                        for u in range(2):
                            t = V.scalar_tensor_tensor(x[:, 2 * p + u], bank(4 + i % 2)[:, C * u:C * (u + 1)], cw[:, u, i:i + 1], x[:, 2 * p + u], ALU.mult, ALU.add)
                        t.then_inc(acc.sem, 1)
                if st == 7:
                    dve.wait_ge(F("y").sem, F("y").at(p, 16))
                    dve.wait_ge(acc.sem, acc.at(p, 8))
                    V.scalar_tensor_tensor(x[:, bass.ds(2 * p, 2)], bank(6).rearrange("p (u c) -> p u c", u=2), gates[:, 7:8], x[:, bass.ds(2 * p, 2)],
                                           ALU.mult, ALU.add).then_inc(acc.sem, 1)

            items(dve, front, back, n=NB // 2)

        def s3_pe(pe):
            F = lambda n: f[3, n]
            MM = nc.tensor.matmul

            def front(p, s, turn):
                ff_front_pe(3, pe, p, s)

            def back(p, s, nxt):
                router_pe(3, pe, p, s)
                for j in range(4):
                    if j == 2:
                        nxt()
                    pe.wait_ge(F("acc").sem, F("acc").at(p, 4 * j - 4))
                    for u in range(2):
                        o = bank(2 + 2 * (j % 2) + u)
                        for c in range(NC):
                            MM(o, xnT[:, s, c, T * u:T * (u + 1)], w3e[:, c, 512 * j:512 * (j + 1)], start=(c == 0), stop=False)
                        t = MM(o, ones96[:], ebias[:, 512 * j:512 * (j + 1)], start=False, stop=True)
                    t.then_inc(F("y").sem, 1)

            items(pe, front, back, n=NB // 2)

        def s3_act(act):
            def front(p, s, turn):
                ff_front_act(3, act, p, s)

            def back(p, s, nxt):
                router_act(3, act, p)
                nxt()

            items(act, front, back, n=NB // 2)

        def s3_dve(dve):
            F = lambda n: f[3, n]

            def front(p, s, turn):
                ff_front_dve(3, dve, p, s)

            def back(p, s, nxt):
                acc = F("acc")
                nxt()
                router_dve(3, dve, p)
                for j in range(4):
                    dve.wait_ge(F("y").sem, F("y").at(p, j + 1))
                    for e in range(2):
                        for u in range(2):
                            k = 4 * j + 2 * e + u
                            if k >= 2:
                                dve.wait_ge(acc.sem, acc.at(p, k - 1))
                            nc.vector.scalar_tensor_tensor(x[:, 2 * p + u], bank(2 + 2 * (j % 2) + u)[:, C * e:C * (e + 1)], cw[:, u, 2 * j + e:2 * j + e + 1],
                                                           x[:, 2 * p + u], ALU.mult, ALU.add).then_inc(acc.sem, 1)

            items(dve, front, back, n=NB // 2)

        def s5_pe(pe):
            F = lambda n: f[5, n]

            def front(p, s, turn):
                ff_front_pe(5, pe, p, s)

            def back(p, s, nxt):
                pe.wait_ge(F("xnT").sem, F("xnT").at(p, 1))
                nxt()
                pe.wait_ge(F("acc").sem, F("acc").at(p, -1))
                for u in range(2):
                    for c in range(NC):
                        t = nc.tensor.matmul(bank(2 + s)[:, C * u:C * (u + 1)], xnT[:, s, c, T * u:T * (u + 1)], fsum[:, c], start=(c == 0), stop=(c == NC - 1))
                t.then_inc(F("y").sem, 1)

            items(pe, front, back, n=NB // 2)

        def s5_act(act):
            def front(p, s, turn):
                ff_front_act(5, act, p, s)

            def back(p, s, nxt):
                nxt()

            items(act, front, back, n=NB // 2)

        def s5_dve(dve):
            F = lambda n: f[5, n]
            V = nc.vector

            def front(p, s, turn):
                ff_front_dve(5, dve, p, s)

            def back(p, s, nxt):
                nxt()
                xs = x[:, bass.ds(2 * p, 2)]
                V.tensor_tensor(xs, xs, fb[:].unsqueeze(1).to_broadcast([128, 2, C]), ALU.add).then_inc(F("bias").sem, 1)
                dve.wait_ge(F("bias").sem, F("bias").at(p, 1))
                dve.wait_ge(F("y").sem, F("y").at(p, 1))
                V.scalar_tensor_tensor(xs, bank(2 + s).rearrange("p (u c) -> p u c", u=2), gs5[:], xs, ALU.mult, ALU.add).then_inc(F("acc").sem, 1)

            items(dve, front, back, n=NB // 2)

        POS_Q, POS_K = (0, 1, 0, 1, 0, 2), (0, 0, 1, 1, 2, 0)

        def s2_sp(sp):
            F = lambda n: f[2, n]

            def load_k(b, s):
                for r in range(6):
                    sp.dma_start(kop[16 * r:16 * (r + 1), s], kscr[b, POS_K[r]].rearrange("(h d) n -> d h n", d=16)).then_inc(F(f"k_loaded{s}").sem, 16)

            def load_v(b, s):
                sp.dma_start(v_raw[:, s], a["ctxT16"][:, b]).then_inc(F(f"v_loaded{s}").sem, 16)

            def store_q(b, s, turn):
                sp.wait_ge(F("parts").sem, F("parts").at(b, 5))
                sp.dma_start(qscr[s].rearrange("r p n -> p r n"), xparts[:, s]).then_inc(F(f"q_stored{s}").sem, 16)

            def load_q(b, s, turn):
                sp.wait_ge(F(f"q_stored{s}").sem, F(f"q_stored{s}").at(turn, 16))
                for r in range(6):
                    sp.dma_start(qop[16 * r:16 * (r + 1), s], qscr[s, POS_Q[r]].rearrange("(h d) n -> d h n", d=16)).then_inc(F(f"q_loaded{s}").sem, 16)

            for u in range(2):
                sp.wait_ge(c_out[u], 16 * (NB // 2))
            for b in range(2):
                load_k(b, b)
                load_v(b, b)
            for b in range(2):
                store_q(b, b, 0)
                load_q(b, b, 0)
            with sp.Fori(0, NB // 2 - 1) as i:
                for u in range(2):
                    b, n = i * 2 + u, i * 2 + (u + 2)
                    store_q(n, u, i + 1)
                    sp.wait_ge(F("st").sem, F("st").at(b, 4))
                    load_k(n, u)
                    load_q(n, u, i + 1)
                    sp.wait_ge(F("v").sem, F("v").at(b, 1))
                    load_v(n, u)

        def s2_pool(pool):
            F = lambda n: f[2, n]
            P = nc.gpsimd
            rs = rstd_step(2, pool)

            def lay(b, s, turn, wait=True):
                pool.wait_ge(F(f"v_loaded{s}").sem, F(f"v_loaded{s}").at(turn, 16))
                plain(pool)
                if wait:
                    pool.wait_ge(F("pv").sem, F("pv").at(b, -1))
                    plain(pool)
                raw = v_raw[:, s].rearrange("p (l h d) -> p l h d", l=2, d=16)
                P.tensor_copy(v2a[:, s].rearrange("p l (h w) -> p l h w", h=4)[:, :, :, 0:16], raw[:, :, 0:4])
                P.tensor_copy(v2b[:, s, :, 64:640].rearrange("p l (h w) -> p l h w", h=4)[:, :, :, 0:16], raw[:, :, 4:8]).then_inc(F("v").sem, 1)

            P.memset(tail, 0.0).then_inc(v2_ready, 1)
            P.memset(rd2[:], 0.0).then_inc(v2_ready, 1)
            pool.wait_ge(v2_ready, 1)
            for h in range(4):
                P.memset(v2a[:, :, :, 64 + 69 * h:65 + 69 * h], 1.0)
                P.memset(v2b[:, :, :, 129 * h:129 * h + 1], 1.0)
            rs(0, 0)
            rs(1, 1)
            lay(0, 0, 0, False)
            rs(2, 0)
            lay(1, 1, 0, False)
            loops = (NB - 4) // 2
            with pool.Fori(0, loops) as i:
                for u in range(2):
                    rs(i * 2 + (u + 3), (u + 1) % 2)
                    lay(i * 2 + (u + 2), u, i + 1)
            b = NB - 3
            rs(b + 2, (b + 2) % 2)
            lay(b + 1, (b + 1) % 2, (b + 1) // 2)
            lay(b + 2, (b + 2) % 2, (b + 2) // 2)

        def s2_dve(dve):
            F = lambda n: f[2, n]
            V = nc.vector

            def wait(n, b, k):
                dve.wait_ge(F(n).sem, F(n).at(b, k))

            def operands(b, s):
                ln_apply(2, dve, b, s, xn[:, s, 0])
                P = F("parts")
                wait("xn", b, 1)
                split3(V, dve, xn[:, s, 0], lambda n: xparts[:, s, n], xres[:], P, b)
                V.tensor_copy(dl[:, 0, 0:1], dl[:, 0, 0:1]).then_inc(P.sem, 1)

            def finish(p):
                wait("bc_psum", p, 1)
                V.reciprocal(bc_sb[:, 0:C], bank(2)[:, 0:C]).then_inc(F("bc").sem, 1)
                wait("bc", p, 1)
                V.scalar_tensor_tensor(q_tmp[0:64], bank(3)[0:64, 0:C], gg[0:64], bc_sb[0:64, 0:C], ALU.mult, ALU.mult)
                V.scalar_tensor_tensor(q_tmp[64:128], bank(3)[64:128, C:2 * C], gg[64:128], bc_sb[64:128, 0:C], ALU.mult, ALU.mult).then_inc(F("on").sem, 1)
                wait("on", p, 1)
                V.tensor_tensor(x[:, p], x[:, p], q_tmp[:], ALU.add).then_inc(x_done.sem, 1)

            def first():
                for b in range(2):
                    ln_stats(2, dve, b, None, b)
                    operands(b, b)

            def body(p, b, n, s, turn, turn_b):
                if n is not None:
                    ln_stats(2, dve, n, None, s)
                for k in range(4):
                    wait("sq", b, k + 1)
                    V.tensor_reduce(mx2[:, k // 2, 4 * (k % 2):4 * (k % 2) + 4], bank(4 + 2 * (k % 2), 2).rearrange("p (h l) -> p h l", h=4),
                                    axis=AX.X, op=ALU.max, negate=True).then_inc(F("mx").sem, 1)
                wait("mx", b, 4)
                split3(V, dve, mx2[:], lambda n: mxp2[:, :, n], mxr2[:], F("mparts"), b)
                wait("mxT_psum", b, 1)
                V.tensor_copy(mxq2[0:24, :], bank(1).bitcast(BF16)[0:24, 0:256]).then_inc(F("mxT").sem, 1)
                if p is not None:
                    finish(p)
                if n is not None:
                    operands(n, s)

            pipeline(dve, first, body, lambda p, s: finish(p), ahead=2)

        def s2_act(act):
            F = lambda n: f[2, n]

            def sums(p):
                act.wait_ge(F("pv").sem, F("pv").at(p, 1))
                nc.scalar.copy(rd2[64:68], bank(3)[64:68, 0:C])
                nc.scalar.copy(rd2[0:4], bank(3)[0:4, C:2 * C]).then_inc(F("rden").sem, 1)

            def body(p, b, n, s, turn, turn_b):
                if p is not None:
                    sums(p)
                for k in range(4):
                    act.wait_ge(F("st").sem, F("st").at(b, k + 1))
                    nc.scalar.activation(PT[:, 1024 * k:1024 * (k + 1)], bank(4 + 2 * (k % 2), 2), ACT.Exp, scale=0.25).then_inc(F("p").sem, 1)

            pipeline(act, lambda: act.wait_ge(v2_ready, 2), body, lambda p, s: sums(p), ahead=2)

        def s2_pe(pe):
            F = lambda n: f[2, n]
            MM = nc.tensor.matmul

            def wait(n, b, k):
                pe.wait_ge(F(n).sem, F(n).at(b, k))

            def values(b, s, heads):
                ptv = PT[:, 0:4096].rearrange("p (h l q) -> p h l q", h=8, l=2)
                wait("v", b, 1)
                if heads[0] == 0:
                    pe.wait_ge(x_done.sem, b + NB)
                    plain(pe)
                for h in heads:
                    wait("p", b, h // 2 + 1)
                    for lt in range(2):
                        g, o = (v2a[:, s, lt, 68 * h:68 * (h + 1)], bank(3)[0:68, 0:C]) if h < 4 else (v2b[:, s, lt, 128 * (h - 4):128 * (h - 3)], bank(3)[:, C:2 * C])
                        t = MM(o, g, ptv[:, h, lt], start=(h % 4 == 0 and lt == 0), stop=(h % 4 == 3 and lt == 1), skip_group_check=True)
                if heads[-1] == 7:
                    t.then_inc(F("pv").sem, 1)

            def spread(p):
                wait("rden", p, 1)
                MM(bank(2)[:, 0:C], sel2s[0:68], rd2[:], start=True, stop=True).then_inc(F("bc_psum").sem, 1)

            def body(p, b, n, s, turn, turn_b):
                wait(f"q_loaded{s}", turn_b, 96)
                wait(f"k_loaded{s}", turn_b, 96)
                for k in range(4):
                    if k < 2:
                        wait("p", b, k - 1)
                    else:
                        wait("mx", b, k - 1)
                    qt, h0 = k // 2, 4 * (k % 2)
                    for h in range(4):
                        t = MM(bank(4 + 2 * (k % 2), 2)[:, 256 * h:256 * (h + 1)], qop[:, s, h0 + h, 128 * qt:128 * (qt + 1)], kop[:, s, h0 + h], start=True, stop=True)
                    t.then_inc(F("sq").sem, 1)
                    if p is not None and k == 1:
                        values(p, 1 - s, range(0, 4))
                if p is not None:
                    values(p, 1 - s, range(4, 8))
                wait("mparts", b, 4)
                plain(pe)
                for qt in range(2):
                    t = nc.tensor.transpose(bank(1).bitcast(BF16)[0:24, 128 * qt:128 * (qt + 1)], mxp2[:, qt].rearrange("p r h -> p (r h)"), identb[:])
                t.then_inc(F("mxT_psum").sem, 1)
                if p is not None:
                    spread(p)
                wait("mxT", b, 1)
                for k in range(4):
                    if k < 2:
                        wait("mx", b, 3 + k)
                    else:
                        wait("p", b, k - 1)
                    for j in range(2):
                        h = 2 * k + j
                        for lt in range(2):
                            o = bank(4 + 2 * (k % 2) + j)[:, 256 * lt:256 * (lt + 1)]
                            MM(o, sel2[:, h], mxq2[:], start=True, stop=False)
                            t = MM(o, kop[:, s, h, 128 * lt:128 * (lt + 1)], qop[:, s, h], start=False, stop=True)
                    t.then_inc(F("st").sem, 1)

            def last(p, s):
                values(p, s, range(8))
                spread(p)

            pipeline(pe, lambda: None, body, last, ahead=2)

        MAGIC = 1.5 * 2 ** 23

        def quant(dve, src, dst, sc, tmp, fl, item, k0, amax_done=False):
            V = nc.vector

            def settle(k):
                dve.wait_ge(fl.sem, fl.at(item, k0 + k))
            V.tensor_reduce(sc[:, 0:1], src, axis=AX.X, op=ALU.max, apply_absolute_value=True).then_inc(fl.sem, 1)
            settle(1)
            V.tensor_scalar(sc[:, 1:2], sc[:, 0:1], 1.0 / 127.0, 1e-8, ALU.mult, ALU.max).then_inc(fl.sem, 1)
            settle(2)
            V.reciprocal(sc[:, 2:3], sc[:, 1:2]).then_inc(fl.sem, 1)
            settle(3)
            V.tensor_scalar(tmp, src, sc[:, 2:3], 127.0, ALU.mult, ALU.min).then_inc(fl.sem, 1)
            settle(4)
            V.tensor_scalar(tmp, tmp, -127.0, MAGIC, ALU.max, ALU.add).then_inc(fl.sem, 1)
            settle(5)
            V.tensor_scalar(dst, tmp, MAGIC, None, ALU.subtract).then_inc(fl.sem, 1)

        wq_n = staging[:, 0:1024].rearrange("p (w o c) -> p w o c", w=2, o=2)
        wprep = Flag(sem("wprep"), 0)
        wprep_pe = sem("wprep_pe")

        def s4_weights_dve(dve):
            dve.wait_ge(v4_ready, 2)
            k = 0
            for w in range(2):
                for o in range(2):
                    n = 2 * w + o
                    if k:
                        dve.wait_ge(wprep.sem, k)
                    quant(dve, wq_n[:, w, o], qw[:, w, o], wsc[:, n].rearrange("p a b -> p (a b)"), qt_f[:], wprep, 0, k)
                    k += 6
                    V = nc.vector
                    V.tensor_scalar(diag[:, n], ident[:], wsc[:, n].rearrange("p a b -> p (a b)")[:, 1:2], None, ALU.mult).then_inc(wprep.sem, 1)
                    k += 1
            dve.wait_ge(wprep_pe, 1)
            V.tensor_copy(ident_r[:], ident[:])
            V.tensor_scalar(rows4[:, 3], bank(1)[:, 0:256], 0.25, None, ALU.mult)
            V.tensor_scalar(rows4[:, 4], bank(1)[:, 256:512], gates[:, 2:3], None, ALU.mult)
            V.tensor_scalar(rows4[:, 0], rows4[:, 0], 0.25, None, ALU.mult)
            V.tensor_scalar(rows4[:, 2], rows4[:, 2], gates[:, 2:3], None, ALU.mult)
            for w in range(2):
                t = V.tensor_copy(qwT[:, w], bank(2 + w).bitcast(BF16)[:, 0:512].rearrange("p (c o) -> p c o", c=2))
            t.then_inc(wprep.sem, 1)
            k += 1
            dve.wait_ge(wprep.sem, k)
            return k

        def s4_weights_pe(pe):
            pe.wait_ge(wprep.sem, 28)
            for w in range(2):
                for o in range(2):
                    nc.tensor.matmul(bank(1)[:, 256 * w + 128 * o:256 * w + 128 * (o + 1)], onesf[:], diag[:, 2 * w + o], start=True, stop=True)
                    for c in range(2):
                        t = nc.tensor.transpose(bank(2 + w).bitcast(BF16)[:, 256 * c + 128 * o:256 * c + 128 * (o + 1)], qw[:, w, o, 128 * c:128 * (c + 1)], identb[:])
            t.then_inc(wprep_pe, 1)
            pe.wait_ge(wprep.sem, 29)

        def s4_sp(sp):
            F = lambda n: f[4, n]

            def load(b, s):
                sp.dma_start(ctxT[:, s], a["ctxT"][:, b]).then_inc(F(f"ctx_loaded{s}").sem, 16)
                sp.dma_start(msk[:, s, 0], a["mask"][:, b]).then_inc(F(f"msk_loaded{s}").sem, 16)
                sp.dma_start(msk[:, s, 1], a["maskT"][:, b]).then_inc(F(f"msk_loaded{s}").sem, 16)
            load(0, 0)
            load(1, 1)
            with sp.Fori(0, NB // 2 - 1) as i:
                for u in range(2):
                    b = i * 2 + u
                    sp.wait_ge(F("q_psum").sem, F("q_psum").at(b, 1))
                    sp.wait_ge(F("msk").sem, F("msk").at(b, 2))
                    load(i * 2 + (u + 2), u)

        def s4_pool(pool):
            F = lambda n: f[4, n]
            P = nc.gpsimd
            rs = rstd_step(4, pool)

            def split(b, s, turn, wait=True):
                pool.wait_ge(F(f"msk_loaded{s}").sem, F(f"msk_loaded{s}").at(turn, 32))
                plain(pool)
                if wait:
                    pool.wait_ge(F("st").sem, F("st").at(b, -2))
                    plain(pool)
                P.tensor_copy(mskp[:, s, :, 0], msk[:, s]).then_inc(F("msk").sem, 1)
                pool.wait_ge(F("msk").sem, F("msk").at(b, 1))
                P.tensor_tensor(mskp[:, s, :, 1], msk[:, s], mskp[:, s, :, 0].bitcast(F32), ALU.subtract).then_inc(F("msk").sem, 1)

            rs(0, 0)
            split(0, 0, 0, False)
            rs(1, 1)
            split(1, 1, 0, False)
            with pool.Fori(0, NB // 2 - 1) as i:
                for u in range(2):
                    rs(i * 2 + (u + 2), u)
                    split(i * 2 + (u + 2), u, i + 1)

        def s4_dve(dve):
            F = lambda n: f[4, n]
            V = nc.vector

            def wait(n, b, k):
                dve.wait_ge(F(n).sem, F(n).at(b, k))

            def quantise(b, s):
                ln_apply(4, dve, b, s, xn[:, s, 0])
                wait("xn", b, 1)
                quant(dve, xn[:, s, 0], qx[:], qsc[:, s], qt_f[:], F("quant"), b, 0)

            def scale(b, s):
                wait("q_psum", b, 1)
                D = F("qdve")
                V.scalar_tensor_tensor(q_tmp[:], bank(1)[:, 0:C], qsc[:, s, 1:2], rows4[:, 3], ALU.mult, ALU.mult).then_inc(D.sem, 1)
                for r in range(4):
                    t = V.tensor_tensor(v4[:, s, r].rearrange("p (g w) -> p g w", w=84)[:, :, 0:16], bank(1)[:, C:2 * C].rearrange("p (g r d) -> p r g d", r=4, d=16)[:, r],
                                        rows4[:, 1].rearrange("p (g r d) -> p r g d", r=4, d=16)[:, r], ALU.add)
                t.then_inc(D.sem, 1)
                dve.wait_ge(D.sem, D.at(b, 1))
                V.tensor_tensor(qpad[:, :, 0:16], q_tmp[:].rearrange("p (h d) -> p h d", d=16), rows4[:, 0].rearrange("p (h d) -> p h d", d=16), ALU.add).then_inc(D.sem, 1)

            def finish(p):
                wait("pvT", p, 1)
                pv = bank(3)[:, 0:272].rearrange("p (r m) -> p r m", m=68)
                V.reciprocal(rden[:, 0:16].rearrange("p (r g) -> p r g", g=4), pv[:, :, 64:68]).then_inc(F("rden").sem, 1)
                wait("rden", p, 1)
                ov = o_n[:].rearrange("p q h -> p (q h)")
                for r in range(4):
                    t = V.tensor_tensor(ov.rearrange("p (g r d) -> p r g d", r=4, d=16)[:, r], pv[:, r, 0:64].rearrange("p (g d) -> p g d", d=16),
                                        rden[:, 4 * r:4 * r + 4].unsqueeze(2).to_broadcast([128, 4, 16]), ALU.mult)
                t.then_inc(F("on").sem, 1)
                wait("on", p, 1)
                quant(dve, ov, qo[:], osc[:], qt_f[:], F("oquant"), p, 0)

            def update(p, n):
                if n is not None:
                    wait("qdve", n, 3)
                wait("y", p, 1)
                fin = F("fin")
                V.scalar_tensor_tensor(q_tmp[:], bank(3)[:, 0:C], osc[:, 1:2], rows4[:, 4], ALU.mult, ALU.mult).then_inc(fin.sem, 1)
                wait("fin", p, 1)
                V.tensor_tensor(q_tmp[:], q_tmp[:], rows4[:, 2], ALU.add).then_inc(fin.sem, 1)
                wait("fin", p, 2)
                V.tensor_tensor(x[:, p], x[:, p], q_tmp[:], ALU.add).then_inc(x_done.sem, 1)

            def first():
                ln_stats(4, dve, 0, None, 0)
                quantise(0, 0)
                scale(0, 0)

            def body(p, b, n, s, turn, turn_b):
                if n is not None:
                    ln_stats(4, dve, n, None, 1 - s)
                for k in range(2):
                    wait("sq", b, k + 1)
                    V.tensor_reduce(mx4[:, 8 * k:8 * k + 8], bank(4 + 2 * k, 2).rearrange("p (h l) -> p h l", h=8), axis=AX.X, op=ALU.max, negate=True).then_inc(F("mx").sem, 1)
                wait("mx", b, 2)
                split3(V, dve, mx4[:], lambda r: mxp4[:, r], mxr4[:], F("mparts"), b)
                if n is not None:
                    quantise(n, 1 - s)
                wait("mxT_psum", b, 1)
                V.tensor_copy(mxq4[0:48, :], bank(2).bitcast(BF16)[0:48, 0:128]).then_inc(F("mxT").sem, 1)
                if p is not None:
                    finish(p)
                if n is not None:
                    scale(n, 1 - s)
                if p is not None:
                    update(p, n)

            def last(p, s):
                finish(p)
                update(p, None)

            pipeline(dve, first, body, last)

        def s4_act(act):
            F = lambda n: f[4, n]
            A = nc.scalar

            def wait(n, b, k):
                act.wait_ge(F(n).sem, F(n).at(b, k))

            def copy_x(b):
                wait("xT_psum", b, 1)
                A.copy(qxT[:], bank(0).bitcast(BF16)[:, 0:256].rearrange("p (c t) -> p c t", c=2)).then_inc(F("xT").sem, 1)

            def copy_k(b, s):
                wait("k_psum", b, 1)
                for g in range(4):
                    A.activation(kT4[:, s, g], bank(2)[:, 128 * g:128 * (g + 1)], ACT.Identity, bias=bkc[:, g:g + 1]).then_inc(F("k").sem, 1)

            def copy_q(b, s):
                wait("qT_psum", b, 1)
                A.copy(qT4[:, s], bank(0).rearrange("p (g t) -> p g t", g=4)).then_inc(F("qT").sem, 1)

            def copy_o(p):
                wait("oT_psum", p, 1)
                A.copy(qoT[:], bank(3).bitcast(BF16)[:, 512:768].rearrange("p (c t) -> p c t", c=2)).then_inc(F("oT").sem, 1)

            def first():
                copy_x(0)
                copy_k(0, 0)
                copy_q(0, 0)

            def copy_values(p):
                wait("pv", p, 1)
                A.copy(bc_sb[0:68], bank(3)[0:68]).then_inc(F("pvc").sem, 1)

            def body(p, b, n, s, turn, turn_b):
                if p is not None:
                    copy_values(p)
                for k in range(2):
                    wait("st", b, k + 1)
                    A.activation(PT[:, 1024 * k:1024 * (k + 1)], bank(4 + 2 * k, 2), ACT.Exp).then_inc(F("p").sem, 1)
                    if k == 0 and n is not None:
                        copy_x(n)
                if n is not None:
                    copy_k(n, 1 - s)
                if p is not None:
                    copy_o(p)
                if n is not None:
                    copy_q(n, 1 - s)

            pipeline(act, first, body, lambda p, s: (copy_values(p), copy_o(p)))

        def s4_pe(pe):
            F = lambda n: f[4, n]
            MM = nc.tensor.matmul

            def wait(n, b, k):
                pe.wait_ge(F(n).sem, F(n).at(b, k))

            def transpose_x(b):
                wait("quant", b, 6)
                for c in range(2):
                    t = nc.tensor.transpose(bank(0).bitcast(BF16)[:, 128 * c:128 * (c + 1)], qx[:, 128 * c:128 * (c + 1)], identb[:])
                t.then_inc(F("xT_psum").sem, 1)

            def project(b, s, turn):
                wait(f"ctx_loaded{s}", turn, 16)
                for g in range(4):
                    for c in range(2):
                        t = MM(bank(2)[:, 128 * g:128 * (g + 1)], wkT[:, c, g], ctxT[:, s, c], start=(c == 0), stop=(c == 1))
                t.then_inc(F("k_psum").sem, 1)
                for c in range(2):
                    MM(bank(1)[:, C:2 * C], ctxT[:, s, c], wvT[:, c], start=(c == 0), stop=(c == 1))
                wait("xT", b, 1)
                for c in range(2):
                    t = MM(bank(1)[:, 0:C], qxT[:, c], qwT[:, 0, c], start=(c == 0), stop=(c == 1))
                t.then_inc(F("q_psum").sem, 1)

            def transpose_q(b):
                wait("qdve", b, 3)
                qv = qpad[:].rearrange("p h d -> p (h d)")
                for g in range(4):
                    t = nc.tensor.transpose(bank(0)[:, 128 * g:128 * (g + 1)], qv[:, 128 * g:128 * (g + 1)], ident[:])
                t.then_inc(F("qT_psum").sem, 1)

            def add_mask(s, which, r):
                for part in range(2):
                    MM(bank(4 + r), ident_r[:], mskp[:, s, which, part].unsqueeze(1).to_broadcast([128, 4, T]), start=(part == 0), stop=False, skip_group_check=True)

            def values(p, s):
                ptv = PT[:, 0:2048].rearrange("p (r g q) -> p r g q", r=4, g=4)
                pe.wait_ge(x_done.sem, p + 2 * NB)
                plain(pe)
                for r in range(4):
                    wait("p", p, r // 2 + 1)
                    for g in range(4):
                        t = MM(bank(3)[0:68, 128 * r:128 * (r + 1)], v4[:, s, r, 68 * g:68 * (g + 1)], ptv[:, r, g], start=(r == 0 and g == 0), stop=(g == 3), skip_group_check=True)
                t.then_inc(F("pv").sem, 1)

            def transpose_values(p):
                wait("pvc", p, 1)
                plain(pe)
                for r in range(4):
                    t = nc.tensor.transpose(bank(3)[:, 68 * r:68 * (r + 1)], bc_sb[0:68, 128 * r:128 * (r + 1)], ident[0:68, 0:68])
                t.then_inc(F("pvT").sem, 1)

            def transpose_o(p):
                wait("oquant", p, 6)
                for c in range(2):
                    t = nc.tensor.transpose(bank(3).bitcast(BF16)[:, 512 + 128 * c:512 + 128 * (c + 1)], qo[:, 128 * c:128 * (c + 1)], identb[:])
                t.then_inc(F("oT_psum").sem, 1)

            def output(p):
                wait("oT", p, 1)
                for c in range(2):
                    t = MM(bank(3)[:, 0:C], qoT[:, c], qwT[:, 1, c], start=(c == 0), stop=(c == 1))
                t.then_inc(F("y").sem, 1)

            def first():
                transpose_x(0)
                project(0, 0, 0)
                transpose_q(0)

            def body(p, b, n, s, turn, turn_b):
                wait("msk", b, 2)
                for k in range(2):
                    wait("p", b, k - 1)
                    for r in (2 * k, 2 * k + 1):
                        add_mask(s, 0, r)
                    if k == 0:
                        wait("k", b, 4)
                        wait("qT", b, 1)
                    for g in range(4):
                        for r in (2 * k, 2 * k + 1):
                            t = MM(bank(4 + r)[:, 128 * g:128 * (g + 1)], qT4[32 * r:32 * r + 16, s, g], kT4[32 * r:32 * r + 16, s, g], start=False, stop=True, skip_group_check=True)
                    t.then_inc(F("sq").sem, 1)
                if p is not None:
                    values(p, 1 - s)
                wait("mparts", b, 4)
                plain(pe)
                nc.tensor.transpose(bank(2).bitcast(BF16)[0:48, 0:128], mxp4[:].rearrange("p r h -> p (r h)"), identb[:]).then_inc(F("mxT_psum").sem, 1)
                for k in range(2):
                    wait("mx", b, k + 1)
                    for r in (2 * k, 2 * k + 1):
                        add_mask(s, 1, r)
                        if r == 0:
                            wait("mxT", b, 1)
                        for g in range(4):
                            MM(bank(4 + r)[:, 128 * g:128 * (g + 1)], sel4[:, 4 * r + g], mxq4[:], start=False, stop=False, skip_group_check=True)
                    for g in range(4):
                        for r in (2 * k, 2 * k + 1):
                            t = MM(bank(4 + r)[:, 128 * g:128 * (g + 1)], kT4[32 * r:32 * r + 16, s, g], qT4[32 * r:32 * r + 16, s, g], start=False, stop=True, skip_group_check=True)
                    t.then_inc(F("st").sem, 1)
                    if k == 0 and n is not None:
                        transpose_x(n)
                    if k == 0 and p is not None:
                        transpose_values(p)
                if n is not None:
                    project(n, 1 - s, turn)
                if p is not None:
                    transpose_o(p)
                if n is not None:
                    transpose_q(n)
                if p is not None:
                    output(p)

            def last(p, s):
                values(p, s)
                transpose_values(p)
                transpose_o(p)
                output(p)

            pipeline(pe, first, body, last)

        def s6_sp(sp):
            F = lambda n: f[6, n]

            def load(b, s):
                sp.dma_start(ctxT[:, s], a["ctxT"][:, b]).then_inc(F(f"ctx_loaded{s}").sem, 16)
                sp.dma_start(cnat[:, s], a["ctx"][:, b]).then_inc(F(f"ctx_loaded{s}").sem, 16)
            load(0, 0)
            load(1, 1)
            with sp.Fori(0, NB // 2 - 1) as i:
                for u in range(2):
                    sp.wait_ge(F("y").sem, F("y").at(i * 2 + u, 1))
                    load(i * 2 + (u + 2), u)

        sgm = PT[:, 0:1024].rearrange("p (s n m) -> p s n m", s=2, n=2)

        def s6_dve(dve):
            F = lambda n: f[6, n]

            def front(b, s, turn):
                ln_stats(6, dve, b, None, s)
                ln_apply(6, dve, b, s, xn[:, s, 0])

            def back(b, s, nxt):
                nxt()
                dve.wait_ge(F("y").sem, F("y").at(b, 1))
                nc.vector.scalar_tensor_tensor(x[:, b], bank(4 + s)[:, 0:C], gates[:, 3:4], x[:, b], ALU.mult, ALU.add).then_inc(x_done.sem, 1)

            items(dve, front, back)

        def s6_act(act):
            F = lambda n: f[6, n]

            def front(b, s, turn):
                act.wait_ge(F("s_psum").sem, F("s_psum").at(b, 1))
                nc.scalar.activation(sgm[:, s], bank(2 + s).rearrange("p (n m) -> p n m", n=2), ACT.Sigmoid, scale=float(T) ** -0.5).then_inc(F("s").sem, 1)

            def back(b, s, nxt):
                nxt()

            items(act, front, back)

        def s6_pe(pe):
            F = lambda n: f[6, n]
            MM = nc.tensor.matmul

            def front(b, s, turn):
                pe.wait_ge(F("xn").sem, F("xn").at(b, 1))
                pe.wait_ge(F(f"ctx_loaded{s}").sem, F(f"ctx_loaded{s}").at(turn, 32))
                for n in range(2):
                    t = MM(bank(2 + s)[:, C * n:C * (n + 1)], xn[:, s, 0, 128 * n:128 * (n + 1)], cnat[:, s], start=True, stop=True)
                t.then_inc(F("s_psum").sem, 1)

            def back(b, s, nxt):
                nxt()
                pe.wait_ge(F("s").sem, F("s").at(b, 1))
                pe.wait_ge(x_done.sem, b + (3 * NB - 1))
                for n in range(2):
                    t = MM(bank(4 + s)[:, 0:C], ctxT[:, s, n], sgm[:, s, n], start=(n == 0), stop=(n == 1))
                t.then_inc(F("y").sem, 1)

            items(pe, front, back)

        c_in = [sem("c_in0"), sem("c_in1")]
        c_parts = Flag(sem("c_parts"), 4)
        c_out = [sem("c_out0"), sem("c_out1")]

        def ctx_pipeline(pool, fetch):
            rs = rstd_step(0, pool)

            def one(b, u, turn, first, last):
                rs(b, u)
                pool.wait_ge(c_in[u], turn * 16 + 16)
                plain(pool)
                if not first:
                    pool.wait_ge(c_out[u], turn * 16)
                split3(nc.gpsimd, pool, cnat[:, u], lambda n: cparts[:, u, n], cres[:], c_parts, b)
                pool.wait_ge(c_parts.sem, c_parts.at(b, 4))
                pool.dma_start(kscr[b].rearrange("r p n -> p r n"), cparts[:, u]).then_inc(c_out[u], 16)
                if not last:
                    fetch(b + 2, u)
            for u in range(2):
                one(u, u, 0, True, False)
            with pool.Fori(1, NB // 2 - 1) as i:
                for u in range(2):
                    one(i * 2 + u, u, i, False, False)
            for u in range(2):
                one(NB - 2 + u, u, NB // 2 - 1, False, True)


        @block.sync
        def _(sp):
            for q in range(4):
                sp.dma_start(x[:, 4 * q:4 * q + 4], a["x"][:, 4 * q:4 * q + 4]).then_inc(loaded_x, 16)
            sp.dma_start(arena[:, 0:10240], a["w13"]).then_inc(w_loaded[1], 16)
            s0_sp(sp)
            if n_stages > 2:
                stage_over(sp, 2)
                s2_sp(sp)
                sp.dma_start(wkT, a["wkT"]).then_inc(w_loaded[3], 16)
                sp.dma_start(wvT, a["wvT"]).then_inc(w_loaded[3], 16)
                sp.dma_start(sel4, a["sel4"].bitcast(BF16)).then_inc(w_loaded[3], 16)
            if n_stages > 3:
                stage_over(sp, 3)
                sp.dma_start(staging[:, 0:1024], a["w4n"]).then_inc(w_loaded[4], 16)
            if n_stages > 4:
                stage_over(sp, 4)
                s4_sp(sp)
                stage_over(sp, 5)
                sp.dma_start(arena[:, 0:12288], a["w7"]).then_inc(w_loaded[7], 16)
                sp.dma_start(staging, a["w5"]).then_inc(w_loaded[5], 16)
            if n_stages > 6:
                stage_over(sp, 6)
                s6_sp(sp)
            sp.wait_ge(*ends[n_stages - 1])
            done = sem("stored")
            sp.dma_start(out, x[:]).then_inc(done, 16)
            sp.wait_ge(done, 16)

        @block.scalar
        def _(act):
            n = 0
            for t, name in ((ident, "ident"), (gates, "gates"), (w0x, "w0x"), (w0c, "w0c"), (w0o, "w0o"), (wr, "wr"), (iota8, "iota8"), (sel0, "sel0"), (sel2s, "sel2s"),
                            (sbias, "sbias"), (bkc, "bkc"), (fb, "fb")):
                act.dma_start(t[:], a[name]).then_inc(loaded_c, 16)
            act.dma_start(rows4[:, 0:3], a["rows4"]).then_inc(loaded_c, 16)
            for t, name in ((ext0, "ext0"), (mxq0, "mxq0"), (ohq0, "ohq0"), (sel2, "sel2")):
                act.dma_start(t[:], a[name].bitcast(BF16)).then_inc(loaded_c, 16)
            for s in range(2):
                act.dma_start(q_parts[:, s], a["q_const"].bitcast(BF16)).then_inc(loaded_c, 16)
                act.dma_start(k_parts[:, s], a["k_const"].bitcast(BF16)).then_inc(loaded_c, 16)
            act.dma_start(eb_f, a["eb"]).then_inc(loaded_c, 16)
            act.wait_ge(loaded_c, LOADS_0)
            A = nc.scalar
            A.activation(gates[:, 0:8], gates[:, 0:8], ACT.Tanh).then_inc(gates_ready, 1)
            give(act, [(0, "p")])
            s0_act(act)
            for s, prog in enumerate((None, lambda: glu_act(1, act), lambda: s2_act(act), lambda: s3_act(act), lambda: s4_act(act),
                                      lambda: s5_act(act), lambda: s6_act(act), lambda: glu_act(7, act))):
                if 0 < s < n_stages:
                    stage_over(act, s)
                    prog()

        @block.vector
        def _(dve):
            V = nc.vector
            dve.wait_ge(loaded_c, LOADS_0)
            dve.wait_ge(loaded_x, 64)
            V.memset(minus_half[:], -0.5)
            V.memset(v0, 0.0)
            V.memset(qpad[:], 0.0)
            V.memset(onesf[:], 1.0)
            V.memset(ones96[:], 1.0)
            V.memset(mxq2[:], 0.0)
            V.memset(mxq4[:], 0.0)
            V.memset(dl[:], 0.0)
            V.memset(th[:], 0.0)
            V.tensor_copy(identb[:], ident[:]).then_inc(zero_ready, 1)
            dve.wait_ge(zero_ready, 1)
            for h in range(HK0):
                V.memset(v0[:, :, :, 73 * h + 64:73 * h + 65], 1.0)
            give(dve, [(s, n) for s in (1, 3, 5, 7) for n in ("h", "acc", "lg")])
            G = prep_w
            V.tensor_copy(eb_b, eb_f).then_inc(G.sem, 1)
            dve.wait_ge(G.sem, 1)
            V.tensor_copy(ebias[0:32], eb_b[0:32])
            V.tensor_tensor(eb_r, eb_f, eb_b, ALU.subtract).then_inc(G.sem, 1)
            dve.wait_ge(G.sem, 2)
            V.tensor_copy(eb_b, eb_r).then_inc(G.sem, 1)
            dve.wait_ge(G.sem, 3)
            V.tensor_copy(ebias[32:64], eb_b[32:64])
            V.tensor_tensor(ebias[64:96], eb_r[64:96], eb_b[64:96], ALU.subtract).then_inc(G.sem, 1)
            dve.wait_ge(G.sem, 4)
            dve.wait_ge(gates_ready, 1)
            V.tensor_scalar(half[:, 0], gates[:], 0.5, None, ALU.mult)
            V.tensor_scalar(half[:, 1], gates[:], -0.5, None, ALU.mult)
            V.tensor_scalar(gs5[:], gates[:, 6:7], float(8.0 ** -0.5), None, ALU.mult)
            V.tensor_scalar(fb[:], fb[:], gates[:, 6:7], None, ALU.mult)
            V.tensor_tensor(gg[:], gates[:, 1:2], gates[:, 8:9], ALU.mult).then_inc(G.sem, 1)
            dve.wait_ge(G.sem, 5)
            s0_dve(dve)
            if n_stages > 1:
                stage_over(dve, 1)
                glu_dve(1, dve)
            if n_stages > 2:
                stage_over(dve, 2)
                s2_dve(dve)
            if n_stages > 3:
                stage_over(dve, 3)
                s3_dve(dve)
            if n_stages > 4:
                stage_over(dve, 4)
                dve.wait_ge(w_loaded[4], 16)
                s4_weights_dve(dve)
                s4_dve(dve)
            if n_stages > 5:
                stage_over(dve, 5)
                dve.wait_ge(w_loaded[5], 16)
                V.tensor_reduce(fsum.rearrange("p c n -> p (c n)"), staging.rearrange("p (r m) -> p m r", r=8), axis=AX.X, op=ALU.add).then_inc(G.sem, 1)
                s5_dve(dve)
            if n_stages > 6:
                stage_over(dve, 6)
                s6_dve(dve)
            if n_stages > 7:
                stage_over(dve, 7)
                glu_dve(7, dve)

        @block.gpsimd
        def _(pool):
            pool.wait_ge(zero_ready, 1)
            if n_stages > 2:
                def fetch(b, u):
                    pool.dma_start(cnat[:, u], a["ctx"][:, b]).then_inc(c_in[u], 16)
                fetch(0, 0)
                fetch(1, 1)
                ctx_pipeline(pool, fetch)
            for s in range(1 if n_stages > 2 else 0, n_stages):
                stage_over(pool, s)
                if s == 2:
                    s2_pool(pool)
                elif s == 4:
                    s4_pool(pool)
                else:
                    pool_stage(s, pool)
                if s == 3:
                    nc.gpsimd.memset(v4, 0.0).then_inc(v4_ready, 1)
                    pool.wait_ge(v4_ready, 1)
                    for g in range(4):
                        t = nc.gpsimd.memset(v4[:, :, :, 69 * g + 64:69 * g + 65], 1.0)
                    t.then_inc(v4_ready, 1)

        @block.tensor
        def _(pe):
            pe.wait_ge(loaded_c, LOADS_0)
            pe.wait_ge(prep_w.sem, 5)
            give(pe, [(1, "y")])
            s0_pe(pe)
            for s, prog in enumerate((None, lambda: glu_pe(1, pe), lambda: s2_pe(pe), lambda: s3_pe(pe), lambda: (s4_weights_pe(pe), s4_pe(pe)),
                                      lambda: s5_pe(pe), lambda: s6_pe(pe), lambda: glu_pe(7, pe))):
                if 0 < s < n_stages:
                    stage_over(pe, s)
                    if s in (1, 3):
                        pe.wait_ge(w_loaded[1], 16)
                    if s == 4:
                        pe.wait_ge(w_loaded[3], 48)
                    if s == 5:
                        pe.wait_ge(prep_w.sem, 6)
                    if s == 7:
                        pe.wait_ge(w_loaded[7], 16)
                    prog()


LOADS_0 = 16 * (12 + 1 + 4 + 4 + 1)


def layouts(inp):
    def bf16(v):
        u = np.ascontiguousarray(v, np.float32).view(np.uint32).astype(np.uint64)
        return ((u + 0x7FFF + ((u >> 16) & 1)) >> 16).astype(np.uint16)

    def back(bits):
        return (bits.astype(np.uint32) << 16).view(np.float32)

    def chunks(w):
        return np.ascontiguousarray(w.reshape(NC, 128, -1).transpose(1, 0, 2))

    d = {}
    d["x"] = np.ascontiguousarray(inp["x"].transpose(1, 0, 2))
    d["ctxT"] = np.ascontiguousarray(inp["ctx_2048"].reshape(NB, T, NC, 128).transpose(3, 0, 2, 1))
    d["ident"] = np.eye(128, dtype=np.float32)
    g = np.concatenate([inp["g_xattn"], inp["g_ffn"], inp["L1_xattn_gamma"].reshape(1)])
    d["gates"] = np.ascontiguousarray(np.broadcast_to(g, (128, 9)))
    wq = inp["L0_xattn_Wq"].reshape(2 * C, HK0, G0, D0).transpose(0, 2, 1, 3).reshape(2 * C, C)
    d["w0x"] = chunks(np.concatenate([wq[C:], inp["L0_xattn_Wk"], inp["L0_xattn_Wv"]], 1))
    d["w0c"] = chunks(np.concatenate([inp["L0_xattn_Wsk"], inp["L0_xattn_Wsv"], wq[:C]], 1))
    d["w0o"] = np.ascontiguousarray(inp["L0_xattn_Wo"].reshape(HK0, G0, D0, C).transpose(0, 2, 1, 3).reshape(64, G0, C))
    sel = np.zeros((128, 64), np.float32)
    sel[64:72] = np.repeat(np.eye(HK0), D0, 1)
    d["sel0"] = sel
    ext = np.zeros((128, HK0, sum(2 * k for k in KEYS_T)), np.float32)
    o = 0
    for qb in range(NQB):
        for c, win in ((0, W_SSM), (1, W_ATT)):
            m = KEYS_T[qb]
            for hk in range(HK0):
                for part in range(3):
                    ext[32 * part + 8 * qb + hk, hk, o:o + m] = 1.0
            delta = (QB * qb + np.arange(QB))[:, None] - np.arange(m)[None, :]
            ext[96:128, :, o:o + m] = np.where((delta >= 0) & (delta < win), 0.0, MASKED)[:, None, :]
            o += m
    d["ext0"] = bf16(ext.reshape(128, -1))
    oh = np.zeros((128, 128), np.float32)
    oh[96:128] = np.tile(np.eye(QB), (1, G0))
    d["mxq0"] = bf16(oh)
    d["ohq0"] = bf16(oh)
    slopes = np.power(np.float32(2.0), -8.0 * np.arange(H0, dtype=np.float32) / H0).astype(np.float32)
    qc = np.zeros((128, H0, R0), np.float32)
    rest = slopes.copy()
    for part in range(3):
        p = back(bf16(rest))
        qc[:, :, 48 + part] = p.reshape(HK0, G0).T.reshape(-1)
        rest = rest - p
    kc = np.zeros((128, 2, HK0, R0), np.float32)
    kc[:, :, :, 48:51] = (np.arange(T) - 64)[:, None, None, None]
    d["q_const"], d["k_const"] = bf16(qc), bf16(kc)
    def units(gate, value, down):
        up = np.stack([gate, value], 2).reshape(-1, NC, 128, 2, 128).transpose(2, 0, 1, 3, 4)
        return up.reshape(128, -1), down.transpose(1, 0, 2).reshape(128, -1)

    up, down = units(inp["L0_ffn_w1"], inp["L0_ffn_w2"], inp["L0_ffn_w3"])
    d["w13"] = np.ascontiguousarray(np.concatenate([up, down, chunks(inp["L1_ffn_expert_w"].transpose(2, 0, 1).reshape(C, -1)).reshape(128, -1)], 1))
    w12 = inp["L3_ffn_w12"].transpose(0, 2, 1)
    s1, s2 = (inp[n].reshape(8, 128, C).transpose(0, 2, 1) for n in ("L3_ffn_sw1", "L3_ffn_sw2"))
    down = np.concatenate([inp["L3_ffn_w3"].transpose(0, 2, 1), inp["L3_ffn_sw3"].T.reshape(8, 128, C)])
    d["w7"] = np.ascontiguousarray(np.concatenate(units(np.concatenate([w12[:, :, :128], s1]), np.concatenate([w12[:, :, 128:], s2]), down), 1))
    d["wr"] = np.ascontiguousarray(np.stack([chunks(inp[n].T) for n in ("L0_ffn_router_w", "L1_ffn_gate_w", "L3_ffn_router_w")], 1))
    d["iota8"] = np.ascontiguousarray(np.broadcast_to(np.arange(8, dtype=np.float32), (128, 8)))
    d["sbias"] = np.ascontiguousarray(np.broadcast_to(inp["L3_ffn_expert_bias"], (128, 8)))
    eb = np.zeros((96, TOP_E * C), np.float32)
    eb[0:96:32] = inp["L1_ffn_expert_b"].reshape(-1)
    d["eb"] = eb
    d["ctx"] = np.ascontiguousarray(inp["ctx_2048"].transpose(1, 0, 2))
    d["ctxT16"] = np.ascontiguousarray(inp["ctx_2048"].reshape(NB, 8, 16, 2, 128).transpose(4, 0, 3, 1, 2).reshape(128, NB, 256))
    sel = np.zeros((68, 128), np.float32)
    sel[0:4, 64:] = np.repeat(np.eye(4), 16, 1)
    sel[64:, 0:64] = np.repeat(np.eye(4), 16, 1)
    d["sel2s"] = sel
    sel = np.zeros((96, 8, 128), np.float32)
    for h in range(8):
        sel[h:24:8, h] = 1.0
    d["sel2"] = bf16(sel)
    wk = np.zeros((C, 4, 4, 32), np.float32)
    wk[..., :16] = inp["L2_xattn_wk"].T.reshape(C, 4, 4, 16)
    d["wkT"] = np.ascontiguousarray(chunks(wk.reshape(C, -1)).reshape(128, NC, 4, 128))
    bk = np.zeros((4, 4, 32), np.float32)
    bk[..., :16] = inp["L2_xattn_bk"].reshape(4, 4, 16)
    d["bkc"] = np.ascontiguousarray(bk.reshape(4, 128).T)
    d["wvT"] = chunks(inp["L2_xattn_wv"].T)
    d["rows4"] = np.ascontiguousarray(np.broadcast_to(np.stack([inp["L2_xattn_bq"], inp["L2_xattn_bv"], inp["L2_xattn_bo"]]), (128, 3, C)))
    d["w4n"] = np.ascontiguousarray(np.stack([inp[n].reshape(2, 128, C).transpose(1, 0, 2) for n in ("L2_xattn_wq", "L2_xattn_wo")], 1).reshape(128, -1))
    d["mask"] = np.ascontiguousarray(inp["mask_BxSxS2_ff0"].transpose(1, 0, 2))
    d["maskT"] = np.ascontiguousarray(inp["mask_BxSxS2_ff0"].transpose(2, 0, 1))
    sel = np.zeros((96, 16, 128), np.float32)
    for h in range(16):
        sel[h:48:16, h] = 1.0
    d["sel4"] = bf16(sel)
    d["w5"] = np.ascontiguousarray(inp["L2_ffn_factors"].reshape(8, NC, 128, C).transpose(2, 0, 1, 3).reshape(128, -1))
    d["fb"] = np.ascontiguousarray(np.broadcast_to(inp["L2_ffn_bias"], (128, C)))
    return d


def kernel(**inputs):
    import numpy as _np
    import concourse.bacc as _bacc
    from concourse import mybir as _mybir
    from concourse.bass_utils import run_bass_kernel_spmd as _run

    nc = _bacc.Bacc("TRN2", target_bir_lowering=False, num_devices=1)
    arrays, a = {}, {}
    for name, v in layouts(inputs).items():
        arrays["in_" + name] = v
        a[name] = nc.dram_tensor("in_" + name, v.shape, _mybir.dt.from_np(v.dtype), kind="ExternalInput").ap()
    out = nc.dram_tensor("out", (T, NB, C), F32, kind="ExternalOutput").ap()
    bass_program(nc, a, out)
    r = _run(nc, [arrays], core_ids=[0])
    return _np.ascontiguousarray(r.results[0]["out"].transpose(1, 0, 2))
```

```python
import numpy as np
from contextlib import ExitStack

import concourse.bass as bass
from concourse import mybir

F32 = mybir.dt.float32
BF16 = mybir.dt.bfloat16
F32R = mybir.dt.float32r
U32 = mybir.dt.uint32
ALU = mybir.AluOpType
ACT = mybir.ActivationFunctionType
AX = mybir.AxisListType

NB = 16
T = 128
C = 256
NC = C // 128
EPS_LN = 1e-5

H0, HK0, D0 = 32, 8, 8
G0 = H0 // HK0
QB = 32
NQB = T // QB
W_SSM, W_ATT = 64, 32
R0 = 64
MASKED = -1e30
KEYS_T = [64, 64, 128, 128]
KEYS_Q = [(0, 32), (0, 64), (0, 96), (32, 96)]
FILLS_Q = [(0, 0, 4), (1, 0, 4), (2, 0, 2), (2, 2, 2), (3, 0, 2), (3, 2, 2)]
FILLS_T = [(0, 2), (1, 2), (2, 0), (2, 1), (3, 0), (3, 1)]

TOP_E = 8


class Flag:

    def __init__(self, sem, per, credit=0, base=0):
        self.sem, self.per, self.credit = sem, per, base + credit
        self.given = credit

    def at(self, item, k):
        return item * self.per + (k + self.credit)


def bass_program(nc, a, out, n_stages=8):
    ctx = ExitStack()
    with ctx:
        def sb(name, shape, dt=F32):
            return ctx.enter_context(nc.sbuf_tensor(name, shape, dt))

        def sem(name):
            return ctx.enter_context(nc.semaphore(name))

        def here():
            return (nc.sbuf_base + 31) // 32 * 32

        psum = ctx.enter_context(nc.psum_tensor("psum", [128, 8 * 512], F32))

        def bank(n, k=1):
            return psum[:, 512 * n:512 * (n + k)]

        x = sb("x", [128, NB, C])
        ident = sb("ident", [128, 128])
        identb = sb("identb", [128, 128], BF16)
        gates = sb("gates", [128, 9])
        loaded_x = [sem("loaded_x0"), sem("loaded_x1")]
        loaded_later = sem("loaded_later")
        loaded_c = sem("loaded_c")
        gates_ready = sem("gates_ready")
        x_done = Flag(sem("x_done"), 1)
        stats = sb("stats", [128, 4, 6])
        mv = sb("mv", [128, 4, 2])
        veps = sb("veps", [128, 4, 1])
        rstd = sb("rstd", [128, 4, 1])
        minus_half = sb("minus_half", [128, 1])
        xn = sb("xn", [128, 2, 2, C])
        xnT = sb("xnT", [128, 2, NC, 2 * T])
        zero_ready = sem("zero_ready")
        waited = sem("waited")

        early = here()
        w_attn = sb("w_attn", [128, 2560])
        w0x = w_attn[:, 0:768].rearrange("p (c n) -> p c n", c=NC)
        w0c = w_attn[:, 768:1536].rearrange("p (c n) -> p c n", c=NC)
        w0o = w_attn[0:64, 1536:2560].rearrange("p (g n) -> p g n", g=G0)
        ext0_at = here()
        ext0 = sb("ext0", [128, HK0 * sum(2 * k for k in KEYS_T)], BF16)
        k_parts = sb("k_parts", [128, 2, 2, HK0, R0], BF16)
        qT0 = sb("qT0", [128, HK0 // 2, NQB, G0, QB], BF16)
        kT0 = sb("kT0", [128, HK0 // 2, 2, T], BF16)
        PT = sb("PT", [128, 12 * 512])
        mxq0 = sb("mxq0", [128, 128], BF16)
        ohq0 = sb("ohq0", [128, 128], BF16)
        ctxT = sb("ctxT", [128, 2, NC, T])
        q_f_at = here()
        q_f = sb("q_f", [128, 2, C])
        kv_f = sb("kv_f", [128, 2, 2, 128])
        q_r = sb("q_r", [128, C])
        k_r = sb("k_r", [128, 128])
        mx0 = sb("mx0", [128, NQB, HK0 // 2, 2])
        mxr0 = sb("mxr0", [128, 32])
        mxp0 = sb("mxp0", [128, 3, 32], BF16)
        rden_at = here()
        rden = sb("rden", [128, 512])
        bc_sb = sb("bc_sb", [128, 512])
        sel0 = sb("sel0", [128, 64])
        o_n = sb("o_n", [128, NQB, 64])
        oT0 = sb("oT0", [64, G0, T])

        arena_at = here()
        arena = sb("arena", [128, 10240 + 3904])
        tail = arena[:, 10240:]
        v0 = arena[:, 10240:14080].rearrange("p (s c w) -> p s c w", s=2, c=3)
        w3e = arena[:, 6144:10240].rearrange("p (c n) -> p c n", c=NC)
        wr = sb("wr", [128, 3, NC, TOP_E])
        iota8 = sb("iota8", [128, TOP_E])
        eb_n = sb("eb_n", [128, 16])
        eb_r = sb("eb_r", [128, 16])
        eb_p = sb("eb_p", [128, 3, 16], BF16)
        ebias = sb("ebias", [96, TOP_E * C], BF16)
        ones96 = sb("ones96", [96, 128], BF16)
        sbias = sb("sbias", [128, TOP_E])
        staging = PT[:, 0:4096]
        q_const = sb("q_const", [128, H0 * 16], BF16)
        k_const = sb("k_const", [128, 2 * HK0 * 16], BF16)
        loaded_s0 = sem("loaded_s0")
        half = sb("half", [128, 2, 9])
        lg = sb("lg", [128, 2, TOP_E])
        sg8 = sb("sg8", [128, 2, TOP_E])
        sel8 = sb("sel8", [128, 2, TOP_E])
        v8 = sb("v8", [128, 2, 8])
        i8 = sb("i8", [128, 2, 8], U32)
        idf = sb("idf", [128, 2, 2])
        dl = sb("dl", [128, 2, 1])
        th = sb("th", [128, 2, 8])
        wk = sb("wk", [128, 2, 2])
        den = sb("den", [128, 2, 1])
        oh = sb("oh", [128, 2, 2, TOP_E])
        ohs = sb("ohs", [128, 2, 2, TOP_E])
        cw = sb("cw", [128, 2, 2, TOP_E])
        sil = sb("sil", [128, 2, 2 * T])
        qop = ext0[0:96, 0:4096].rearrange("p (s h n) -> p s h n", s=2, h=8)
        xparts_at = here()
        xparts = sb("xparts", [128, 2, 3, C], BF16)
        xres = sb("xres", [128, C])
        v_raw = sb("v_raw", [128, 2, 2 * 128])
        v2a = tail[:, 0:1344].rearrange("p (s l w) -> p s l w", s=2, l=2)
        v2b = tail[:, 1344:3904].rearrange("p (s l w) -> p s l w", s=2, l=2)
        rd2 = sb("rd2", [68, C])
        sel2s = sb("sel2s", [68, 128])
        v2_ready = sem("v2_ready")
        sel2 = sb("sel2", [96, 8, 128], BF16)
        mxq2 = sb("mxq2", [96, C], BF16)
        mx2 = sb("mx2", [128, 2, 8])
        mxr2 = sb("mxr2", [128, 2, 8])
        mxp2 = sb("mxp2", [128, 2, 3, 8], BF16)
        gg = sb("gg", [128, 1])
        cnat = sb("cnat", [128, 2, C])
        cparts_at = here()
        cparts = sb("cparts", [128, 2, 3, C], BF16)
        cres = sb("cres", [128, C])
        wkT = w_attn[:, 0:1024].rearrange("p (c g m) -> p c g m", c=NC, g=4)
        wvT = w_attn[:, 1024:1536].rearrange("p (c n) -> p c n", c=NC)
        sel4 = w_attn[0:96, 1536:2560].bitcast(BF16).rearrange("p (h m) -> p h m", h=16)
        bkc = sb("bkc", [128, 4])
        rows4 = sb("rows4", [128, 5, C])
        qwT = sb("qwT", [128, 2, NC, C], BF16)
        qw = sb("qw", [128, 2, 2, C], BF16)
        wsc = sb("wsc", [128, 4, 2, 2])
        diag = staging[:, 1024:1536].rearrange("p (n m) -> p n m", n=4)
        onesf = sb("onesf", [128, 128])
        qsc = sb("qsc", [128, 2, 4])
        qt_f = sb("qt_f", [128, C])
        qx = sb("qx", [128, C], BF16)
        qxT = sb("qxT", [128, NC, T], BF16)
        q_tmp = sb("q_tmp", [128, C])
        qpad = sb("qpad", [128, 16, 32])
        qT4 = qT0[:].rearrange("p j b g q -> p (j b g q)").bitcast(F32).rearrange("p (s g t) -> p s g t", s=2, g=4)
        kT4 = k_parts[:].rearrange("p s c h r -> p (s c h r)").bitcast(F32).rearrange("p (s g t) -> p s g t", s=2, g=4)
        v4 = tail[:, 0:2688].rearrange("p (s r w) -> p s r w", s=2, r=4)
        v4_ready = sem("v4_ready")
        msk = q_f[:].rearrange("p s (w t) -> p s w t", w=2)
        mxq4 = sb("mxq4", [96, 128], BF16)
        mx4 = sb("mx4", [128, 16])
        mxr4 = sb("mxr4", [128, 16])
        mxp4 = sb("mxp4", [128, 3, 16], BF16)
        osc = sb("osc", [128, 4])
        fsum = kv_f[:].rearrange("p s c k -> p (s c k)").rearrange("p (c n) -> p c n", c=NC)
        fb = sb("fb", [128, C])
        gs5 = sb("gs5", [128, 1])

        qo = sb("qo", [128, C], BF16)
        qoT = sb("qoT", [128, NC, T], BF16)
        def over(at, name, shape, dt=F32):
            return nc.alloc_sbuf_tensor_at(name, shape, dt, offset=at)

        W7 = 12288
        w7h = over(arena_at, "w7h", [128, W7], F32R)
        w7l = over(early, "w7l", [128, W7], F32R)
        xnTh = over(q_f_at, "xnTh", [128, 2, NC, 2 * T], F32R)
        xnTl = over(arena_at + 4 * (10240 + 2880), "xnTl", [128, 2, NC, 2 * T], F32R)
        w1h = over(early, "w1h", [128, 6144], F32R)
        w1l = over(arena_at, "w1l", [128, 6144], F32R)
        w3h = over(ext0_at, "w3h", [128, NC, 2048], F32R)
        w3l = over(arena_at + 4 * 6144, "w3l", [128, NC, 2048], F32R)
        hTh = over(xparts_at, "hTh", [128, 4, 2 * T], F32R)
        hTl = over(cparts_at, "hTl", [128, 4, 2 * T], F32R)
        hTf = over(rden_at, "hTf", [128, 4, 2 * T])
        parts_at = here()
        W7C = W7 // NB
        w7_raw = over(parts_at, "w7_raw", [128, 2, W7C])
        with nc.sbuf_tensor("q_parts", [128, 2, H0, R0], BF16) as q_parts:
            kop = q_parts[:].rearrange("p s h r -> p (s h r)")[0:96].rearrange("p (s h n) -> p s h n", s=2, h=8)
        mskp = sb("mskp", [128, 2, 2, 2, T], F32R)
        ident_r = sb("ident_r", [128, 128], F32R)
        eb_in, eb_out, eb_loaded = sem("eb_in"), sem("eb_out"), sem("eb_loaded")
        eb_split = Flag(sem("eb_split"), 5, 1)
        factors = PT[:, 2048:6144]
        fsum_ready = sem("fsum_ready")
        escr = nc.dram_tensor("escr", (3, TOP_E * C), BF16, kind="Internal").ap()
        kscr = nc.dram_tensor("kscr", (NB, 3, 128, C), BF16, kind="Internal").ap()
        qscr = nc.dram_tensor("qscr", (2, 3, 128, C), BF16, kind="Internal").ap()
        ends = {}
        w1_high, w1_low, w3_high, w3_low = sem("w1_high"), sem("w1_low"), sem("w3_high"), sem("w3_low")
        w_loaded = [sem(f"w_loaded{k}") for k in range(8)]
        prep_w = Flag(sem("prep_w"), 0)

        f = {}
        shared = {}

        def stage_flags(s, names, n_items=NB):
            for n, per, credit in names:
                count = NB // 2 if n[-1] in "01" else NB if (n, per, credit) in LN else n_items
                if (n, credit) not in shared:
                    shared[n, credit] = [sem(n + (f"_{credit}" if credit else "")), 0]
                entry = shared[n, credit]
                f[s, n] = Flag(entry[0], per, credit, entry[1])
                entry[1] += per * count

        given = set()

        def give(eng, keys):
            for key in keys:
                fl = f.get(key)
                if fl and fl.given and (key[1], fl.given) not in given:
                    given.add((key[1], fl.given))
                    eng.sem_inc(fl.sem, fl.given)

        LN = [("stats", 1, 0), ("mv", 1, 0), ("veps", 1, 0), ("rstd", 1, 0), ("xn", 1, 0)]

        stage_flags(0, [
            ("ctx_loaded0", 16, 0), ("ctx_loaded1", 16, 0),
            ("stats", 1, 0), ("mv", 1, 0), ("veps", 1, 0), ("rstd", 1, 0), ("xn", 1, 0), ("xnT_psum", 1, 0), ("xnT", 1, 0),
            ("qkv_psum", 1, 0), ("qkv", 2, 0), ("parts", 8, 0), ("kT_psum", 1, 0), ("qT_psum", 2, 0), ("qkT", 3, 0),
            ("sq", 6, 0), ("mx", 6, 0), ("mparts", 4, 0), ("mxT_psum", 1, 0), ("mxT", 1, 0),
            ("st", 6, 0), ("p", 6, 2), ("pv", 1, 0), ("rden", 1, 0), ("bc_psum", 1, 0), ("bc", 1, 0), ("oT", 1, 0), ("y", 1, 0)])


        def ff_flags(s):
            n = {1: 8, 3: 4, 5: 1, 7: 16}[s]
            names = LN + [("xnT_psum", 1, 0), ("xnT", 1, 0), ("y", n, 4 if s in (1, 7) else 0),
                          ("acc", {1: 8, 3: 16, 5: 1, 7: 9}[s], {1: 2, 3: 8, 5: 2, 7: 2}[s])]
            if s == 5:
                names += [("bias", 1, 0)]
            else:
                names += [("lg_psum", 1, 0), ("lg", 1, 1), ("route", {1: 7, 3: 7, 7: 14}[s], 0), ("tanh", 1, 0)]
            if s != 5:
                names += [("xnTh", 1, 0), ("xnTl", 1, 0)]
            if s in (1, 7):
                names += [("hh", n, 0), ("hl", n, 0)]
            if s in (1, 7):
                names += [("up", n, 0), ("silu", n, 0), ("h", n, 2)]
            stage_flags(s, names, NB // 2)

        ff_flags(1)
        stage_flags(2, LN + [("parts", 5, 0), ("q_stored0", 16, 0), ("q_stored1", 16, 0), ("q_loaded0", 96, 0), ("q_loaded1", 96, 0),
                             ("k_loaded0", 96, 0), ("k_loaded1", 96, 0), ("v_loaded0", 16, 0), ("v_loaded1", 16, 0), ("v", 1, 0),
                             ("sq", 4, 0), ("mx", 4, 0), ("mparts", 4, 0), ("mxT_psum", 1, 0), ("mxT", 1, 0), ("st", 4, 0), ("p", 4, 2),
                             ("pv", 1, 0), ("rden", 1, 0), ("bc_psum", 1, 0), ("bc", 1, 0), ("on", 1, 0)])
        ff_flags(3)
        stage_flags(4, LN + [("ctx_loaded0", 16, 0), ("ctx_loaded1", 16, 0), ("msk_loaded0", 32, 0), ("msk_loaded1", 32, 0), ("msk", 2, 0), ("quant", 6, 0), ("xT_psum", 1, 0), ("xT", 1, 0), ("q_psum", 1, 0), ("k_psum", 1, 0),
                             ("qdve", 3, 0), ("k", 4, 0), ("qT_psum", 1, 0), ("qT", 1, 0), ("sq", 2, 0), ("mx", 2, 0), ("mparts", 4, 0),
                             ("mxT_psum", 1, 0), ("mxT", 1, 0), ("st", 2, 0), ("p", 2, 2), ("pv", 1, 0), ("pvc", 1, 0), ("pvT", 1, 0), ("rden", 1, 0), ("on", 1, 0),
                             ("oquant", 6, 0), ("oT_psum", 1, 0), ("oT", 1, 0), ("y", 1, 0), ("fin", 2, 0)])
        ff_flags(5)
        stage_flags(6, LN + [("w7_raw0", 16, 0), ("w7_raw1", 16, 0), ("w7_high", 1, 0), ("w7_low", 1, 0), ("ctx_loaded0", 16, 0), ("ctx_loaded1", 16, 0), ("rows_loaded0", 16, 0), ("rows_loaded1", 16, 0), ("s_psum", 1, 0), ("s", 1, 0), ("y", 1, 0)])
        ff_flags(7)
        ends[0] = (x_done.sem, NB)
        for s in (1, 3, 5, 7):
            fl = f[s, "acc"]
            ends[s] = (fl.sem, fl.at(NB // 2, 0))
        for n, s in enumerate((2, 4, 6)):
            ends[s] = (x_done.sem, NB * (n + 2))

        block = ctx.enter_context(nc.Block())

        def plain(eng):
            eng.sem_inc(waited, 1)

        def s0_sp_first(sp):
            for b in range(2):
                sp.dma_start(ctxT[:, b], a["ctxT"][:, b]).then_inc(f[0, f"ctx_loaded{b}"].sem, 16)

        def s0_sp(sp):
            F = lambda n: f[0, n]
            def load(b, s):
                sp.dma_start(ctxT[:, s], a["ctxT"][:, b]).then_inc(F(f"ctx_loaded{s}").sem, 16)
            with sp.Fori(0, NB // 2 - 1) as i:
                for u in range(2):
                    sp.wait_ge(F("qkv_psum").sem, F("qkv_psum").at(i * 2 + u, 1))
                    load(i * 2 + (u + 2), u)

        def ln_stats(s, dve, b, slot, i4):
            F = lambda n: f[s, n]
            nc.vector.bn_stats(stats[:, i4], x[:, b]).then_inc(F("stats").sem, 1)
            dve.wait_ge(F("stats").sem, F("stats").at(b, 1))
            plain(dve)
            nc.vector.bn_aggr(mv[:, i4], stats[:, i4]).then_inc(F("mv").sem, 1)

        def ln_apply(s, dve, b, i4, out_):
            F = lambda n: f[s, n]
            dve.wait_ge(F("rstd").sem, F("rstd").at(b, 1))
            nc.vector.tensor_scalar(out_, x[:, b], mv[:, i4, 0:1], rstd[:, i4], ALU.subtract, ALU.mult).then_inc(F("xn").sem, 1)

        def rstd_step(st, pool):
            F = lambda n: f[st, n]

            def rs(b, s):
                pool.wait_ge(F("mv").sem, F("mv").at(b, 1))
                plain(pool)
                nc.gpsimd.tensor_scalar(veps[:, s], mv[:, s, 1:2], EPS_LN, None, ALU.add).then_inc(F("veps").sem, 1)
                pool.wait_ge(F("veps").sem, F("veps").at(b, 1))
                nc.gpsimd.tensor_tensor(rstd[:, s], veps[:, s], minus_half[:], ALU.pow).then_inc(F("rstd").sem, 1)
            return rs

        def pool_stage(st, pool):
            rs = rstd_step(st, pool)
            step = 4 if st % 2 else 2
            with pool.Fori(0, NB // step) as i:
                for u in range(step):
                    rs(i * step + u, u)

        def split3(V, eng, src, dst, res, fl, item, k0=0):
            if V is nc.gpsimd:
                plain(eng)
            V.tensor_copy(dst(0), src).then_inc(fl.sem, 1)
            eng.wait_ge(fl.sem, fl.at(item, k0 + 1))
            V.tensor_tensor(res, src, dst(0), ALU.subtract).then_inc(fl.sem, 1)
            eng.wait_ge(fl.sem, fl.at(item, k0 + 2))
            if V is nc.gpsimd:
                plain(eng)
            V.tensor_copy(dst(1), res).then_inc(fl.sem, 1)
            eng.wait_ge(fl.sem, fl.at(item, k0 + 3))
            V.tensor_tensor(dst(2), res, dst(1), ALU.subtract).then_inc(fl.sem, 1)

        def pipeline(eng, first, body, last, ahead=1, n_items=NB):
            first()
            body(None, 0, ahead, 0, ahead // 2, 0)
            loops = (n_items - 1 - ahead) // 2
            with eng.Fori(0, loops) as i:
                for u in range(2):
                    body(i * 2 + u, i * 2 + (u + 1), i * 2 + (u + 1 + ahead), (u + 1) % 2, i + (1 + u + ahead) // 2, i + (1 + u) // 2)
            for b in range(2 * loops + 1, n_items):
                n = b + ahead if b + ahead < n_items else None
                body(b - 1, b, n, b % 2, n and n // 2, b // 2)
            last(n_items - 1, (n_items - 1) % 2)

        def s0_dve(dve):
            F = lambda n: f[0, n]
            V = nc.vector

            def wait(n, b, k):
                dve.wait_ge(F(n).sem, F(n).at(b, k))

            def split(b, s):
                P = F("parts")
                qv = q_f[:, s].rearrange("p (h d) -> p h d", d=D0)
                rv = q_r[:].rearrange("p (h d) -> p h d", d=D0)
                qp = lambda n, k, step=2: q_parts[:, s, :, 0:48].rearrange("p h (r d) -> p h r d", d=D0)[:, :, n:n + step * (k - 1) + 1:step]
                wait("qkv", b, 2)
                V.tensor_copy(qp(0, 3), qv.unsqueeze(2).to_broadcast([128, H0, 3, D0])).then_inc(P.sem, 1)
                kf = kv_f[:, s, :, 0:64].rearrange("p c (h d) -> p c h d", d=D0)
                kr = k_r[:].rearrange("p (c h d) -> p c h d", c=2, d=D0)
                kp = lambda n: k_parts[:, s, :, :, 8 * n:8 * n + 8]
                V.tensor_copy(kp(0), kf).then_inc(P.sem, 1)
                V.tensor_copy(kp(1), kf)
                V.tensor_copy(kp(5), kf)
                dve.wait_ge(P.sem, P.at(b, 1))
                V.tensor_tensor(rv, qv, qp(0, 1).rearrange("p h o d -> p h (o d)"), ALU.subtract).then_inc(P.sem, 1)
                dve.wait_ge(P.sem, P.at(b, 2))
                V.tensor_tensor(kr, kf, kp(0), ALU.subtract).then_inc(P.sem, 1)
                dve.wait_ge(P.sem, P.at(b, 3))
                V.tensor_copy(qp(1, 2), rv.unsqueeze(2).to_broadcast([128, H0, 2, D0])).then_inc(P.sem, 1)
                dve.wait_ge(P.sem, P.at(b, 4))
                V.tensor_copy(kp(2), kr)
                V.tensor_copy(kp(3), kr).then_inc(P.sem, 1)
                dve.wait_ge(P.sem, P.at(b, 5))
                V.tensor_tensor(qp(5, 1).rearrange("p h o d -> p h (o d)"), rv, qp(1, 1).rearrange("p h o d -> p h (o d)"), ALU.subtract)
                dve.wait_ge(P.sem, P.at(b, 6))
                V.tensor_tensor(kp(4), kr, kp(3), ALU.subtract).then_inc(P.sem, 1)
                vv = v0[:, s].rearrange("p c (h w) -> p c h w", h=HK0)[:, :, :, 0:D0]
                kvv = kv_f[:, s, :, 64:128].rearrange("p c (h d) -> p c h d", d=D0)
                V.tensor_copy(vv[0:64, 2], kvv[0:64, 0])
                V.tensor_copy(vv[64:128, 2], kvv[0:64, 1])
                V.tensor_copy(vv[:, 0:2], kvv).then_inc(P.sem, 1)

            def finish(p):
                wait("pv", p, 1)
                V.reciprocal(rden[64:72], bank(3)[64:72]).then_inc(F("rden").sem, 1)
                wait("bc_psum", p, 1)
                V.tensor_copy(bc_sb[0:64], bank(1)[0:64]).then_inc(F("bc").sem, 1)
                wait("bc", p, 1)
                V.tensor_tensor(oT0[:].rearrange("p g (b q) -> p b g q", b=NQB), bank(3)[0:64].rearrange("p (b g q) -> p b g q", b=NQB, g=G0),
                                bc_sb[0:64].rearrange("p (b g q) -> p b g q", b=NQB, g=G0), ALU.mult).then_inc(F("oT").sem, 1)

            def update(p):
                wait("y", p, 1)
                V.scalar_tensor_tensor(x[:, p], bank(2)[:, 0:C], gates[:, 0:1], x[:, p], ALU.mult, ALU.add).then_inc(x_done.sem, 1)

            def first():
                ln_stats(0, dve, 0, None, 0)
                ln_apply(0, dve, 0, 0, xn[:, 0, 0])
                split(0, 0)
                dve.wait_ge(loaded_x[1], 16)

            def body(p, b, n, s, turn, turn_b):
                if n is not None:
                    ln_stats(0, dve, n, None, 1 - s)
                for k, (qb, j, m) in enumerate(FILLS_Q):
                    w = 2 * KEYS_Q[qb][1]
                    wait("sq", b, k + 1)
                    src = bank(4 + 2 * (k % 2), 2).rearrange("p (e c) -> p e c", e=2)[:, :, 0:m * w].rearrange("p e (j w) -> p e j w", w=w)
                    V.tensor_reduce(mx0[:, qb, j:j + m].rearrange("p j e -> p e j"), src, axis=AX.X, op=ALU.max, negate=True).then_inc(F("mx").sem, 1)
                wait("mx", b, 6)
                split3(V, dve, mx0[:].rearrange("p q j e -> p (q j e)"), lambda r: mxp0[:, r], mxr0[:], F("mparts"), b)
                if n is not None:
                    ln_apply(0, dve, n, 1 - s, xn[:, 1 - s, 0])
                wait("mxT_psum", b, 1)
                V.tensor_copy(mxq0[0:96, :], bank(2).bitcast(BF16)[0:96, 0:128]).then_inc(F("mxT").sem, 1)
                if p is not None:
                    finish(p)
                    update(p)
                if n is not None:
                    split(n, 1 - s)

            def last(p, s):
                finish(p)
                update(p)

            pipeline(dve, first, body, last)

        def s0_act(act):
            F = lambda n: f[0, n]
            A = nc.scalar

            def wait(n, b, k):
                act.wait_ge(F(n).sem, F(n).at(b, k))

            def copy_xnT(b, s):
                wait("xnT_psum", b, 1)
                A.copy(xnT[:, s, :, 0:T], bank(0)[:, 0:C].rearrange("p (c t) -> p c t", c=NC)).then_inc(F("xnT").sem, 1)

            def copy_qkv(b, s):
                wait("qkv_psum", b, 1)
                A.activation(q_f[:, s], bank(0)[:, 128:384], ACT.Copy, scale=float(D0) ** -0.5).then_inc(F("qkv").sem, 1)
                A.copy(kv_f[:, s], bank(0).rearrange("p (c k) -> p c k", c=4)[:, 0:4:3, :]).then_inc(F("qkv").sem, 1)

            def first():
                copy_xnT(0, 0)
                copy_qkv(0, 0)

            def body(p, b, n, s, turn, turn_b):
                wait("kT_psum", b, 1)
                A.copy(kT0[:], bank(1).bitcast(BF16).rearrange("p (j c t) -> p j c t", j=4, c=2)).then_inc(F("qkT").sem, 1)
                for k in range(2):
                    wait("qT_psum", b, k + 1)
                    src = bank(1 + (k + 1) % 2).bitcast(BF16).rearrange("p (j g b q) -> p j b g q", j=2, g=G0, b=NQB)
                    A.copy(qT0[:, 2 * k], src[:, 0])
                    A.copy(qT0[:, 2 * k + 1], src[:, 1]).then_inc(F("qkT").sem, 1)
                if n is not None:
                    copy_xnT(n, 1 - s)
                for k in range(6):
                    wait("st", b, k + 1)
                    A.activation(PT[:, 1024 * k:1024 * (k + 1)], bank(4 + 2 * (k % 2), 2), ACT.Exp).then_inc(F("p").sem, 1)
                    if n is not None and k == 3:
                        copy_qkv(n, 1 - s)

            pipeline(act, first, body, lambda p, s: None)

        def s0_pe(pe):
            F = lambda n: f[0, n]
            MM = nc.tensor.matmul

            def wait(n, b, k):
                pe.wait_ge(F(n).sem, F(n).at(b, k))

            def transpose_xn(b, s):
                wait("xn", b, 1)
                for c in range(NC):
                    t = nc.tensor.transpose(bank(0)[:, 128 * c:128 * (c + 1)], xn[:, s, 0, 128 * c:128 * (c + 1)], ident[:])
                t.then_inc(F("xnT_psum").sem, 1)

            def project(b, s, turn):
                wait(f"ctx_loaded{s}", turn, 16)
                wait("xnT", b, 1)
                for c in range(NC):
                    MM(bank(0)[:, 128:512], xnT[:, s, c, 0:T], w0x[:, c], start=(c == 0), stop=False, skip_group_check=True)
                for c in range(NC):
                    t = MM(bank(0)[:, 0:384], ctxT[:, s, c], w0c[:, c], start=False, stop=(c == NC - 1), skip_group_check=True)
                t.then_inc(F("qkv_psum").sem, 1)

            def values(b, s, blocks, heads=range(HK0)):
                for qb in blocks:
                    ks = [qb] if qb < 2 else [2 * qb - 2, 2 * qb - 1]
                    wait("p", b, ks[-1] + 1)
                    for hk in heads:
                        for k in ks:
                            t = MM(bank(3)[0:72, 128 * qb:128 * (qb + 1)], v0[:, s, FILLS_T[k][1], 72 * hk:72 * (hk + 1)],
                                   PT[:].rearrange("p (k e j r) -> p k e j r", k=6, e=2, j=4)[:, k, hk % 2, hk // 2],
                                   start=(qb == 0 and hk == 0), stop=(hk == HK0 - 1 and k == ks[-1]), skip_group_check=True)
                if blocks[-1] == NQB - 1 and heads[-1] == HK0 - 1:
                    t.then_inc(F("pv").sem, 1)

            def spread(p):
                wait("rden", p, 1)
                MM(bank(1)[0:64], sel0[64:72], rden[64:72], start=True, stop=True).then_inc(F("bc_psum").sem, 1)

            def output(p):
                wait("oT", p, 1)
                for g in range(G0):
                    t = MM(bank(2)[:, 0:C], oT0[:, g], w0o[:, g], start=(g == 0), stop=(g == G0 - 1))
                t.then_inc(F("y").sem, 1)

            def q_op(hk, qb):
                r = 64 * (hk % 2)
                return qT0[r:r + 64, hk // 2, qb].rearrange("p g q -> p (g q)")

            def k_op(hk, c, k0, n):
                r = 64 * (hk % 2)
                return kT0[r:r + 64, hk // 2, c, k0:k0 + n]

            base = [0, 128, 256, 512]

            def ext(hk, qb, c, k0, n):
                o = 768 * hk + base[qb] + c * KEYS_T[qb] + k0
                return ext0[:, o:o + n]

            def body(p, b, n, s, turn, turn_b):
                if p is not None:
                    values(p, 1 - s, (0, 1))
                P = F("parts")
                kb, qa = bank(1).bitcast(BF16), bank(2).bitcast(BF16)
                pe.wait_ge(P.sem, P.at(b, 7))
                for j in range(4):
                    for c in range(2):
                        o = (j * 2 + c) * 128
                        t = nc.tensor.transpose(kb[:, o:o + 128], k_parts[:, s, c, 2 * j:2 * j + 2, :].rearrange("p h r -> p (h r)"), identb[:])
                t.then_inc(F("kT_psum").sem, 1)
                for k in range(2):
                    if k == 1:
                        if p is not None:
                            values(p, 1 - s, (2,), range(0, 4))
                        wait("qkT", b, 1)
                    for j in range(2):
                        for g in range(G0):
                            o = (j * 4 + g) * 128
                            hk = 2 * (2 * k + j)
                            t = nc.tensor.transpose((qa if k == 0 else kb)[:, o:o + 128], q_parts[:, s, HK0 * g + hk:HK0 * g + hk + 2, :].rearrange("p h r -> p (h r)"), identb[:])
                    t.then_inc(F("qT_psum").sem, 1)
                if p is not None:
                    values(p, 1 - s, (2,), range(4, 8))
                wait("qkT", b, 3)
                for k, (qb, j0, m) in enumerate(FILLS_Q):
                    k0, w = KEYS_Q[qb]
                    if k < 2:
                        pe.wait_ge(F("p").sem, F("p").at(b, 0) - 1 + k)
                    else:
                        wait("mx", b, k - 1)
                    for e in range(2):
                        o = bank(4 + 2 * (k % 2) + e)
                        for j in range(m):
                            mk = ext0[:, base[qb]:base[qb] + 2 * KEYS_T[qb]].rearrange("p (c m) -> p c m", c=2)[:, :, k0:k0 + w]
                            MM(o[:, 2 * w * j:2 * w * (j + 1)], ohq0[:], mk, start=(j == 0), stop=False, skip_group_check=True)
                    for e in range(2):
                        o = bank(4 + 2 * (k % 2) + e)
                        for j in range(m):
                            hk = 2 * (j0 + j) + e
                            r = 64 * e
                            t = MM(o[:, 2 * w * j:2 * w * (j + 1)], q_op(hk, qb), kT0[r:r + 64, hk // 2, :, k0:k0 + w],
                                   start=False, stop=True, skip_group_check=True)
                    t.then_inc(F("sq").sem, 1)
                    if p is not None and k in (1, 2, 3):
                        values(p, 1 - s, (3,), {1: range(0, 2), 2: range(2, 3), 3: range(3, 4)}[k])
                if p is not None:
                    values(p, 1 - s, (3,), range(4, 8))
                M = F("mparts")
                pe.wait_ge(M.sem, M.at(b, 4))
                nc.tensor.transpose(bank(2).bitcast(BF16)[0:96, 0:128], mxp0[:].rearrange("p a r -> p (a r)"), identb[:]).then_inc(F("mxT_psum").sem, 1)
                if n is not None:
                    transpose_xn(n, 1 - s)
                wait("mxT", b, 1)
                for k, (qb, c) in enumerate(FILLS_T):
                    if k < 2:
                        wait("mx", b, 5 + k)
                    else:
                        pe.wait_ge(F("p").sem, F("p").at(b, k - 1))
                    parts = ((0, 0, 64), (1, 64, 64)) if c == 2 else ((c, 0, 128),)
                    for e in range(2):
                        o = bank(4 + 2 * (k % 2) + e)
                        for j in range(4):
                            for cc, r0, m in parts:
                                MM(o[r0:r0 + m, 128 * j:128 * (j + 1)], ext(2 * j + e, qb, cc, 0, m), mxq0[:],
                                   start=(j == 0), stop=False, skip_group_check=True)
                    for e in range(2):
                        o = bank(4 + 2 * (k % 2) + e)
                        for j in range(4):
                            for cc, r0, m in parts:
                                t = MM(o[r0:r0 + m, 128 * j:128 * (j + 1)], k_op(2 * j + e, cc, 0, m), q_op(2 * j + e, qb),
                                       start=False, stop=True, skip_group_check=True)
                    t.then_inc(F("st").sem, 1)
                    if k == 2 and p is not None:
                        spread(p)
                    if k == 3 and n is not None:
                        project(n, 1 - s, turn)
                    if k == 4 and p is not None:
                        output(p)

            def first():
                transpose_xn(0, 0)
                project(0, 0, 0)
                pe.wait_ge(gates_ready, 3)
                pe.wait_ge(loaded_s0, 32)

            def last(p, s):
                values(p, s, (0, 1, 2, 3))
                spread(p)
                output(p)

            pipeline(pe, first, body, last)

        def stage_over(eng, s):
            if s > 0:
                eng.wait_ge(*ends[s - 1])

        MAGIC = 1.5 * 2 ** 23

        def quant(dve, src, dst, sc, tmp, fl, item, k0, amax_done=False):
            V = nc.vector

            def settle(k):
                dve.wait_ge(fl.sem, fl.at(item, k0 + k))
            V.tensor_reduce(sc[:, 0:1], src, axis=AX.X, op=ALU.max, apply_absolute_value=True).then_inc(fl.sem, 1)
            settle(1)
            V.tensor_scalar(sc[:, 1:2], sc[:, 0:1], 1.0 / 127.0, 1e-8, ALU.mult, ALU.max).then_inc(fl.sem, 1)
            settle(2)
            V.reciprocal(sc[:, 2:3], sc[:, 1:2]).then_inc(fl.sem, 1)
            settle(3)
            V.tensor_scalar(tmp, src, sc[:, 2:3], 127.0, ALU.mult, ALU.min).then_inc(fl.sem, 1)
            settle(4)
            V.tensor_scalar(tmp, tmp, -127.0, MAGIC, ALU.max, ALU.add).then_inc(fl.sem, 1)
            settle(5)
            V.tensor_scalar(dst, tmp, MAGIC, None, ALU.subtract).then_inc(fl.sem, 1)

        wq_n = staging[:, 0:1024].rearrange("p (w o c) -> p w o c", w=2, o=2)
        wprep = Flag(sem("wprep"), 0)
        wprep_pe = sem("wprep_pe")

        def s4_weight_quant(dve, n):
            w, o = n // 2, n % 2
            k = 7 * n
            if n == 0:
                dve.wait_ge(w_loaded[4], 16)
            else:
                dve.wait_ge(wprep.sem, k)
            quant(dve, wq_n[:, w, o], qw[:, w, o], wsc[:, n].rearrange("p a b -> p (a b)"), qt_f[:], wprep, 0, k)
            nc.vector.tensor_scalar(diag[:, n], ident[:], wsc[:, n].rearrange("p a b -> p (a b)")[:, 1:2], None, ALU.mult).then_inc(wprep.sem, 1)

        def s4_weights_dve(dve):
            V = nc.vector
            k = 28
            dve.wait_ge(wprep_pe, 1)
            V.tensor_scalar(rows4[:, 3], bank(1)[:, 0:256], 0.25, None, ALU.mult)
            V.tensor_scalar(rows4[:, 4], bank(1)[:, 256:512], gates[:, 2:3], None, ALU.mult)
            V.tensor_scalar(rows4[:, 0], rows4[:, 0], 0.25, None, ALU.mult)
            V.tensor_scalar(rows4[:, 2], rows4[:, 2], gates[:, 2:3], None, ALU.mult)
            for w in range(2):
                t = V.tensor_copy(qwT[:, w], bank(2 + w).bitcast(BF16)[:, 0:512].rearrange("p (c o) -> p c o", c=2))
            t.then_inc(wprep.sem, 1)
            k += 1
            dve.wait_ge(wprep.sem, k)
            return k

        def s4_weights_pe(pe):
            pe.wait_ge(wprep.sem, 28)
            for w in range(2):
                for o in range(2):
                    nc.tensor.matmul(bank(1)[:, 256 * w + 128 * o:256 * w + 128 * (o + 1)], onesf[:], diag[:, 2 * w + o], start=True, stop=True)
                    for c in range(2):
                        t = nc.tensor.transpose(bank(2 + w).bitcast(BF16)[:, 256 * c + 128 * o:256 * c + 128 * (o + 1)], qw[:, w, o, 128 * c:128 * (c + 1)], identb[:])
            t.then_inc(wprep_pe, 1)
            pe.wait_ge(wprep.sem, 29)

        def ff_front_dve(st, dve, p, s):
            ff_stats(st, dve, p, s)
            ff_apply(st, dve, p, s)

        def ff_stats(st, dve, p, s):
            F = lambda n: f[st, n]
            for u in range(2):
                nc.vector.bn_stats(stats[:, 2 * s + u], x[:, 2 * p + u]).then_inc(F("stats").sem, 1)
            for u in range(2):
                dve.wait_ge(F("stats").sem, F("stats").at(2 * p + u, 1))
                plain(dve)
                nc.vector.bn_aggr(mv[:, 2 * s + u], stats[:, 2 * s + u]).then_inc(F("mv").sem, 1)

        def ff_apply(st, dve, p, s):
            for u in range(2):
                ln_apply(st, dve, 2 * p + u, 2 * s + u, xn[:, s, u])

        def ff_front_pe(st, pe, p, s):
            F = lambda n: f[st, n]
            pe.wait_ge(F("xn").sem, F("xn").at(2 * p + 1, 1))
            for c in range(NC):
                for u in range(2):
                    t = nc.tensor.transpose(bank(0)[:, 256 * c + 128 * u:256 * c + 128 * (u + 1)], xn[:, s, u, 128 * c:128 * (c + 1)], ident[:])
            t.then_inc(F("xnT_psum").sem, 1)

        def ff_front_act(st, act, p, s):
            F = lambda n: f[st, n]
            act.wait_ge(F("xnT_psum").sem, F("xnT_psum").at(p, 1))
            nc.scalar.copy(xnT[:, s], bank(0).rearrange("p (c t) -> p c t", c=NC)).then_inc(F("xnT").sem, 1)
            if st != 5:
                nc.scalar.copy(xnTh[:, s], bank(0).rearrange("p (c t) -> p c t", c=NC)).then_inc(F("xnTh").sem, 1)

        def router_pe(st, pe, p, s):
            F = lambda n: f[st, n]
            pe.wait_ge(F("xnT").sem, F("xnT").at(p, 1))
            pe.wait_ge(F("lg").sem, F("lg").at(p, 0))
            for u in range(2):
                for c in range(NC):
                    t = nc.tensor.matmul(bank(1)[:, 8 * u:8 * u + 8], xnT[:, s, c, T * u:T * (u + 1)], wr[:, {1: 0, 3: 1, 7: 2}[st], c],
                                         start=(c == 0), stop=(c == NC - 1))
            t.then_inc(F("lg_psum").sem, 1)

        def bc(ap, shape):
            return ap.to_broadcast(shape)

        ROUTE_STEPS = {1: 8, 3: 8, 7: 15}

        def router_step(st, dve, p, s, k):
            F = lambda n: f[st, n]
            V = nc.vector
            R = F("route")
            gate = {1: 4, 3: 5, 7: 7}[st]
            src = sel8 if st == 7 else lg
            if k == 0:
                dve.wait_ge(F("lg_psum").sem, F("lg_psum").at(p, 1))
                V.tensor_copy(lg[:], bank(1)[:, 0:16].rearrange("p (u e) -> p u e", u=2)).then_inc(F("lg").sem, 1)
                return
            if k == 1:
                dve.wait_ge(F("lg").sem, F("lg").at(p, 1))
            else:
                dve.wait_ge(R.sem, R.at(p, k - 1))
            name = {7: (None, "sg", "sel", "max", "index", "float", "hot", "pick", "weights", "sum", "eps", "recip", "norm", "spread", "row")}.get(
                st, (None, "max", "index", "float", "hot", "weights", "spread", "row"))[k]
            if name == "sg":
                dve.wait_ge(F("tanh").sem, F("tanh").at(p, 1))
                t = V.tensor_scalar(sg8[:], th[:], 0.5, 0.5, ALU.mult, ALU.add)
            elif name == "sel":
                t = V.tensor_tensor(sel8[:], sg8[:], bc(sbias[:].unsqueeze(1), [128, 2, TOP_E]), ALU.add)
            elif name == "max":
                plain(dve)
                for u in range(2):
                    t = V.max(v8[:, u], src[:, u])
            elif name == "index":
                plain(dve)
                for u in range(2):
                    t = V.max_index(i8[:, u], v8[:, u], src[:, u])
                if st != 7:
                    t = V.tensor_tensor(dl[:], v8[:, :, 1:2], v8[:, :, 0:1], ALU.subtract)
            elif name == "float":
                t = V.tensor_copy(idf[:], i8[:, :, 0:2])
            elif name == "hot":
                t = V.tensor_tensor(oh[:], bc(iota8[:].unsqueeze(1).unsqueeze(1), [128, 2, 2, TOP_E]), bc(idf[:].unsqueeze(3), [128, 2, 2, TOP_E]), ALU.is_equal)
            elif name == "weights" and st != 7:
                dve.wait_ge(F("tanh").sem, F("tanh").at(p, 1))
                V.tensor_scalar(wk[:, :, 0:1], th[:, :, 0:1], half[:, 1, gate:gate + 1], half[:, 0, gate:gate + 1], ALU.mult, ALU.add)
                t = V.tensor_scalar(wk[:, :, 1:2], th[:, :, 0:1], half[:, 0, gate:gate + 1], half[:, 0, gate:gate + 1], ALU.mult, ALU.add)
            elif name == "pick":
                t = V.tensor_tensor(ohs[:], oh[:], bc(sg8[:].unsqueeze(2), [128, 2, 2, TOP_E]), ALU.mult)
            elif name == "weights":
                t = V.tensor_reduce(wk[:], ohs[:], axis=AX.X, op=ALU.add)
            elif name == "sum":
                t = V.tensor_tensor(den[:], wk[:, :, 0:1], wk[:, :, 1:2], ALU.add)
            elif name == "eps":
                t = V.tensor_scalar(den[:], den[:], 1e-9, None, ALU.add)
            elif name == "recip":
                t = V.reciprocal(den[:], den[:])
            elif name == "norm":
                t = V.scalar_tensor_tensor(wk[:], wk[:], gates[:, gate:gate + 1], bc(den[:], [128, 2, 2]), ALU.mult, ALU.mult)
            elif name == "spread":
                t = V.tensor_tensor(ohs[:], oh[:], bc(wk[:].unsqueeze(3), [128, 2, 2, TOP_E]), ALU.mult)
            elif name == "row":
                t = V.tensor_tensor(cw[:, s], ohs[:, :, 0], ohs[:, :, 1], ALU.add)
            t.then_inc(R.sem, 1)

        def low_x(st, dve, b, s):
            F = lambda n: f[st, n]
            dve.wait_ge(F("xnTh").sem, F("xnTh").at(b, 1))
            nc.vector.tensor_tensor(xnTl[:, s], xnT[:, s], xnTh[:, s].bitcast(F32), ALU.subtract).then_inc(F("xnTl").sem, 1)

        def router_done(st, dve, p):
            dve.wait_ge(f[st, "route"].sem, f[st, "route"].at(p, ROUTE_STEPS[st] - 1))

        def router_act(st, act, p):
            F = lambda n: f[st, n]
            if st == 7:
                act.wait_ge(F("lg").sem, F("lg").at(p, 1))
                nc.scalar.activation(th[:], lg[:], ACT.Tanh, scale=0.5).then_inc(F("tanh").sem, 1)
            else:
                act.wait_ge(F("route").sem, F("route").at(p, 2))
                nc.scalar.activation(th[:, :, 0:1], dl[:], ACT.Tanh, scale=0.5).then_inc(F("tanh").sem, 1)

        WHEN = {1: dict(norm=0, transpose=2, copy=2, router=3, low=3, tanh=5), 7: dict(norm=1, transpose=3, copy=4, router=5, low=5, tanh=7)}
        STEPS = {1: {4: range(0, 3), 5: range(3, 5), 6: range(5, 7), 7: range(7, 8)},
                 7: {6: range(0, 1), 7: range(1, 3), 8: range(3, 5), 9: range(5, 7), 10: range(7, 9), 11: range(9, 11), 12: range(11, 13), 13: range(13, 15)}}

        def glu_pe(st, pe):
            F = lambda n: f[st, n]
            MM = nc.tensor.matmul
            units, lag, when = {1: 8, 7: 16}[st], 2, WHEN[st]

            weights = {1: (w1h, w1l), 7: (w7h, w7l)}[st]

            def up(b, s, j):
                pe.wait_ge(F("h").sem, F("h").at(b, j - 1))
                for v in range(2):
                    o = bank(2 + j % 2)[:, 256 * v:256 * (v + 1)]
                    for c in range(NC):
                        wh, wl = (w[:, 512 * j + 256 * c + 128 * v:512 * j + 256 * c + 128 * (v + 1)] for w in weights)
                        MM(o, wh, xnTh[:, s, c], start=(c == 0), stop=False)
                        MM(o, wh, xnTl[:, s, c], start=False, stop=False)
                        t = MM(o, wl, xnTh[:, s, c], start=False, stop=(c == NC - 1))
                t.then_inc(F("up").sem, 1)

            def down(b, i):
                pe.wait_ge(F("hl").sem, F("hl").at(b, i + 1))
                if i < 8:
                    pe.wait_ge(F("acc").sem, F("acc").at(b, i - 1 if (st == 1 or i >= 2) else -1))
                elif i == 8:
                    pe.wait_ge(F("acc").sem, F("acc").at(b, 0))
                for u in range(2):
                    o = bank(4 + i % 2 if i < 8 else 6)[:, C * u:C * (u + 1)]
                    first, last = (True, True) if i < 8 else (i == 8 and u == 0, i == units - 1)
                    k = 512 * units + C * i
                    wh, wl = (w[:, k:k + C] for w in weights)
                    hh, hl = (h[:, i % 4, T * u:T * (u + 1)] for h in (hTh, hTl))
                    MM(o, hh, wh, start=first, stop=False, skip_group_check=True)
                    MM(o, hh, wl, start=False, stop=False, skip_group_check=True)
                    t = MM(o, hl, wh, start=False, stop=last, skip_group_check=True)
                t.then_inc(F("y").sem, 1)

            def first():
                ff_front_pe(st, pe, 0, 0)
                router_pe(st, pe, 0, 0)

            def body(p, b, n, s, turn, turn_b):
                pe.wait_ge(F("xnT").sem, F("xnT").at(b, 1))
                pe.wait_ge(F("xnTl").sem, F("xnTl").at(b, 1))
                for j in range(units):
                    if st == 1 and p is None:
                        pe.wait_ge(w1_low, j + 1)
                    up(b, s, j)
                    if j >= 2:
                        down(b, j - 2)
                    elif p is not None:
                        down(p, units - 2 + j)
                    if n is not None:
                        if j == when["transpose"]:
                            ff_front_pe(st, pe, n, 1 - s)
                        if j == when["router"]:
                            router_pe(st, pe, n, 1 - s)

            def last(p, s):
                down(p, units - 2)
                down(p, units - 1)

            pipeline(pe, first, body, last, n_items=NB // 2)

        def glu_act(st, act):
            F = lambda n: f[st, n]
            units, when = {1: 8, 7: 16}[st], WHEN[st]

            def high(b, i):
                act.wait_ge(F("h").sem, F("h").at(b, i + 1))
                nc.scalar.copy(hTh[:, i % 4], hTf[:, i % 4]).then_inc(F("hh").sem, 1)

            def split_weights(j):
                for k, m in ((512 * j, 512), (4096 + C * j, C)):
                    t = nc.scalar.copy(w1h[:, k:k + m], arena[:, k:k + m])
                t.then_inc(w1_high, 1)

            def first():
                if st == 1:
                    act.wait_ge(w_loaded[1], 16)
                    split_weights(0)
                    split_weights(1)
                ff_front_act(st, act, 0, 0)
                router_act(st, act, 0)

            def body(p, b, n, s, turn, turn_b):
                for j in range(units):
                    act.wait_ge(F("up").sem, F("up").at(b, j + 1))
                    act.wait_ge(F("h").sem, F("h").at(b, j - 1))
                    nc.scalar.activation(sil[:, j % 2], bank(2 + j % 2)[:, 0:256], ACT.Silu).then_inc(F("silu").sem, 1)
                    if j > 0:
                        high(b, j - 1)
                    elif p is not None:
                        high(p, units - 1)
                    if st == 1 and p is None and j + 2 < units:
                        split_weights(j + 2)
                    if n is not None:
                        if j == when["copy"]:
                            ff_front_act(st, act, n, 1 - s)
                        if j == when["tanh"]:
                            router_act(st, act, n)

            pipeline(act, first, body, lambda p, s: high(p, units - 1), n_items=NB // 2)

        def glu_dve(st, dve):
            F = lambda n: f[st, n]
            V = nc.vector
            units, lag, when = {1: 8, 7: 16}[st], 2, WHEN[st]

            def multiply(b, j):
                dve.wait_ge(F("silu").sem, F("silu").at(b, j + 1))
                dve.wait_ge(F("y").sem, F("y").at(b, j - 3))
                V.tensor_tensor(hTf[:, j % 4], sil[:, j % 2], bank(2 + j % 2)[:, 256:512], ALU.mult).then_inc(F("h").sem, 1)

            def low(b, i):
                dve.wait_ge(F("hh").sem, F("hh").at(b, i + 1))
                V.tensor_tensor(hTl[:, i % 4], hTf[:, i % 4], hTh[:, i % 4].bitcast(F32), ALU.subtract).then_inc(F("hl").sem, 1)

            def split_weights(j):
                dve.wait_ge(w1_high, j + 1)
                for k, m in ((512 * j, 512), (4096 + C * j, C)):
                    t = V.tensor_tensor(w1l[:, k:k + m], arena[:, k:k + m], w1h[:, k:k + m].bitcast(F32), ALU.subtract)
                t.then_inc(w1_low, 1)

            def add(b, s, i):
                acc = F("acc")
                dve.wait_ge(F("y").sem, F("y").at(b, i + 1))
                if i > 0:
                    dve.wait_ge(acc.sem, acc.at(b, i))
                for u in range(2):
                    t = V.scalar_tensor_tensor(x[:, 2 * b + u], bank(4 + i % 2)[:, C * u:C * (u + 1)], cw[:, s, u, i:i + 1], x[:, 2 * b + u], ALU.mult, ALU.add)
                t.then_inc(acc.sem, 1)

            def first():
                ff_front_dve(st, dve, 0, 0)
                if st == 1:
                    split_weights(0)
                low_x(st, dve, 0, 0)
                if st == 1:
                    split_weights(1)
                for k in range(ROUTE_STEPS[st]):
                    router_step(st, dve, 0, 0, k)

            def body(p, b, n, s, turn, turn_b):
                for j in range(units):
                    multiply(b, j)
                    if j > 0:
                        low(b, j - 1)
                    elif p is not None:
                        low(p, units - 1)
                    if st == 1 and p is None and j + 2 < units:
                        split_weights(j + 2)
                    if j >= 2 and j - 2 < 8:
                        if j == 2:
                            router_done(st, dve, b)
                        add(b, s, j - 2)
                    elif p is not None and st == 1:
                        add(p, 1 - s, units - 2 + j)
                    elif p is not None and j == 1:
                        add_shared(p)
                    if n is not None:
                        if j == when["norm"]:
                            ff_stats(st, dve, n, 1 - s)
                        if j == when["norm"] + 1:
                            ff_apply(st, dve, n, 1 - s)
                        if j == when["low"]:
                            low_x(st, dve, n, 1 - s)
                        for k in STEPS[st].get(j, ()):
                            router_step(st, dve, n, 1 - s, k)

            def add_shared(p):
                dve.wait_ge(F("y").sem, F("y").at(p, units))
                dve.wait_ge(F("acc").sem, F("acc").at(p, 8))
                V.scalar_tensor_tensor(x[:, bass.ds(2 * p, 2)], bank(6).rearrange("p (u c) -> p u c", u=2), gates[:, 7:8], x[:, bass.ds(2 * p, 2)],
                                       ALU.mult, ALU.add).then_inc(F("acc").sem, 1)

            def last(p, s):
                low(p, units - 1)
                if st == 7:
                    add_shared(p)
                else:
                    add(p, s, units - 2)
                    add(p, s, units - 1)
                    if n_stages > 4:
                        for q in range(4):
                            s4_weight_quant(dve, q)

            pipeline(dve, first, body, last, n_items=NB // 2)

        def s3_pe(pe):
            F = lambda n: f[3, n]
            MM = nc.tensor.matmul

            def first():
                ff_front_pe(3, pe, 0, 0)
                router_pe(3, pe, 0, 0)

            def body(p, b, n, s, turn, turn_b):
                pe.wait_ge(F("xnTl").sem, F("xnTl").at(b, 1))
                for j in range(4):
                    if p is None:
                        pe.wait_ge(w3_low, j + 1)
                    pe.wait_ge(F("acc").sem, F("acc").at(b, 4 * j - 4))
                    for u in range(2):
                        o = bank(2 + 2 * (j % 2) + u)
                        for c in range(NC):
                            xh, xl = (v[:, s, c, T * u:T * (u + 1)] for v in (xnTh, xnTl))
                            wh, wl = (w[:, c, 512 * j:512 * (j + 1)] for w in (w3h, w3l))
                            MM(o, xh, wh, start=(c == 0), stop=False)
                            MM(o, xh, wl, start=False, stop=False)
                            MM(o, xl, wh, start=False, stop=False)
                        t = MM(o, ones96[:], ebias[:, 512 * j:512 * (j + 1)], start=False, stop=True)
                    t.then_inc(F("y").sem, 1)
                    if n is not None:
                        if j == 1:
                            ff_front_pe(3, pe, n, 1 - s)
                        if j == 2:
                            router_pe(3, pe, n, 1 - s)

            pipeline(pe, first, body, lambda p, s: None, n_items=NB // 2)

        def s3_act(act):
            def front(b, s):
                ff_front_act(3, act, b, s)
                router_act(3, act, b)

            def first():
                for j in range(4):
                    if j == 1:
                        front(0, 0)
                    nc.scalar.copy(w3h[:, :, 512 * j:512 * (j + 1)], w3e[:, :, 512 * j:512 * (j + 1)]).then_inc(w3_high, 1)

            pipeline(act, first, lambda p, b, n, s, turn, turn_b: front(n, 1 - s) if n is not None else None, lambda p, s: None, n_items=NB // 2)

        def s3_dve(dve):
            F = lambda n: f[3, n]

            def split_weights(j):
                dve.wait_ge(w3_high, j + 1)
                cols = slice(512 * j, 512 * (j + 1))
                nc.vector.tensor_tensor(w3l[:, :, cols], w3e[:, :, cols], w3h[:, :, cols].bitcast(F32), ALU.subtract).then_inc(w3_low, 1)

            def first():
                ff_front_dve(3, dve, 0, 0)
                split_weights(0)
                low_x(3, dve, 0, 0)
                for k in range(ROUTE_STEPS[3]):
                    router_step(3, dve, 0, 0, k)
                for j in range(1, 4):
                    split_weights(j)

            def body(p, b, n, s, turn, turn_b):
                acc = F("acc")
                router_done(3, dve, b)
                if n is not None:
                    ff_stats(3, dve, n, 1 - s)
                for j in range(4):
                    dve.wait_ge(F("y").sem, F("y").at(b, j + 1))
                    for e in range(2):
                        for u in range(2):
                            k = 4 * j + 2 * e + u
                            if k >= 2:
                                dve.wait_ge(acc.sem, acc.at(b, k - 1))
                            nc.vector.scalar_tensor_tensor(x[:, 2 * b + u], bank(2 + 2 * (j % 2) + u)[:, C * e:C * (e + 1)], cw[:, s, u, 2 * j + e:2 * j + e + 1],
                                                           x[:, 2 * b + u], ALU.mult, ALU.add).then_inc(acc.sem, 1)
                    if n is not None:
                        if j == 0:
                            ff_apply(3, dve, n, 1 - s)
                        if j == 2:
                            low_x(3, dve, n, 1 - s)
                        if j == 3:
                            for k in range(ROUTE_STEPS[3]):
                                router_step(3, dve, n, 1 - s, k)

            pipeline(dve, first, body, lambda p, s: None, n_items=NB // 2)

        def s5_pe(pe):
            F = lambda n: f[5, n]

            def body(p, b, n, s, turn, turn_b):
                pe.wait_ge(F("xnT").sem, F("xnT").at(b, 1))
                if n is not None:
                    ff_front_pe(5, pe, n, 1 - s)
                pe.wait_ge(F("acc").sem, F("acc").at(b, -1))
                for u in range(2):
                    for c in range(NC):
                        t = nc.tensor.matmul(bank(2 + s)[:, C * u:C * (u + 1)], xnT[:, s, c, T * u:T * (u + 1)], fsum[:, c], start=(c == 0), stop=(c == NC - 1))
                t.then_inc(F("y").sem, 1)

            pipeline(pe, lambda: ff_front_pe(5, pe, 0, 0), body, lambda p, s: None, n_items=NB // 2)

        def s5_act(act):
            with act.Fori(0, NB // 4) as i:
                for u in range(2):
                    ff_front_act(5, act, i * 2 + u, u)

        def s5_dve(dve):
            F = lambda n: f[5, n]
            V = nc.vector

            def first():
                ff_front_dve(5, dve, 0, 0)
                ff_front_dve(5, dve, 1, 1)

            def body(p, b, n, s, turn, turn_b):
                xs = x[:, bass.ds(2 * b, 2)]
                V.tensor_tensor(xs, xs, fb[:].unsqueeze(1).to_broadcast([128, 2, C]), ALU.add).then_inc(F("bias").sem, 1)
                if n is not None:
                    dve.wait_ge(F("xnT_psum").sem, F("xnT_psum").at(b, 1))
                    ff_front_dve(5, dve, n, s)
                dve.wait_ge(F("bias").sem, F("bias").at(b, 1))
                dve.wait_ge(F("y").sem, F("y").at(b, 1))
                V.scalar_tensor_tensor(xs, bank(2 + s).rearrange("p (u c) -> p u c", u=2), gs5[:], xs, ALU.mult, ALU.add).then_inc(F("acc").sem, 1)

            pipeline(dve, first, body, lambda p, s: None, ahead=2, n_items=NB // 2)

        POS_Q, POS_K = (0, 1, 0, 1, 0, 2), (0, 0, 1, 1, 2, 0)

        def s2_sp(sp):
            F = lambda n: f[2, n]

            def load_k(b, s):
                for r in range(6):
                    sp.dma_start(kop[16 * r:16 * (r + 1), s], kscr[b, POS_K[r]].rearrange("(h d) n -> d h n", d=16)).then_inc(F(f"k_loaded{s}").sem, 16)

            def load_v(b, s):
                sp.dma_start(v_raw[:, s], a["ctxT16"][:, b]).then_inc(F(f"v_loaded{s}").sem, 16)

            def store_q(b, s, turn):
                sp.wait_ge(F("parts").sem, F("parts").at(b, 5))
                sp.dma_start(qscr[s].rearrange("r p n -> p r n"), xparts[:, s]).then_inc(F(f"q_stored{s}").sem, 16)

            def load_q(b, s, turn):
                sp.wait_ge(F(f"q_stored{s}").sem, F(f"q_stored{s}").at(turn, 16))
                for r in range(6):
                    sp.dma_start(qop[16 * r:16 * (r + 1), s], qscr[s, POS_Q[r]].rearrange("(h d) n -> d h n", d=16)).then_inc(F(f"q_loaded{s}").sem, 16)

            for u in range(2):
                sp.wait_ge(c_out[u], 16 * (NB // 2))
            for b in range(2):
                load_k(b, b)
                load_v(b, b)
            stage_over(sp, 2)
            for b in range(2):
                store_q(b, b, 0)
                load_q(b, b, 0)
            with sp.Fori(0, NB // 2 - 1) as i:
                for u in range(2):
                    b, n = i * 2 + u, i * 2 + (u + 2)
                    store_q(n, u, i + 1)
                    sp.wait_ge(F("st").sem, F("st").at(b, 4))
                    load_k(n, u)
                    load_q(n, u, i + 1)
                    sp.wait_ge(F("v").sem, F("v").at(b, 1))
                    load_v(n, u)

        def s2_pool(pool):
            F = lambda n: f[2, n]
            P = nc.gpsimd
            rs = rstd_step(2, pool)

            def lay(b, s, turn, wait=True):
                pool.wait_ge(F(f"v_loaded{s}").sem, F(f"v_loaded{s}").at(turn, 16))
                plain(pool)
                if wait:
                    pool.wait_ge(F("pv").sem, F("pv").at(b, -1))
                    plain(pool)
                raw = v_raw[:, s].rearrange("p (l h d) -> p l h d", l=2, d=16)
                P.tensor_copy(v2a[:, s].rearrange("p l (h w) -> p l h w", h=4)[:, :, :, 0:16], raw[:, :, 0:4])
                P.tensor_copy(v2b[:, s, :, 64:640].rearrange("p l (h w) -> p l h w", h=4)[:, :, :, 0:16], raw[:, :, 4:8]).then_inc(F("v").sem, 1)

            P.memset(tail, 0.0).then_inc(v2_ready, 1)
            P.memset(rd2[:], 0.0).then_inc(v2_ready, 1)
            pool.wait_ge(v2_ready, 1)
            for h in range(4):
                P.memset(v2a[:, :, :, 64 + 69 * h:65 + 69 * h], 1.0)
                P.memset(v2b[:, :, :, 129 * h:129 * h + 1], 1.0)
            rs(0, 0)
            rs(1, 1)
            lay(0, 0, 0, False)
            rs(2, 0)
            lay(1, 1, 0, False)
            loops = (NB - 4) // 2
            with pool.Fori(0, loops) as i:
                for u in range(2):
                    rs(i * 2 + (u + 3), (u + 1) % 2)
                    lay(i * 2 + (u + 2), u, i + 1)
            b = NB - 3
            rs(b + 2, (b + 2) % 2)
            lay(b + 1, (b + 1) % 2, (b + 1) // 2)
            lay(b + 2, (b + 2) % 2, (b + 2) // 2)

        def s2_dve(dve):
            F = lambda n: f[2, n]
            V = nc.vector

            def wait(n, b, k):
                dve.wait_ge(F(n).sem, F(n).at(b, k))

            def operands(b, s):
                ln_apply(2, dve, b, s, xn[:, s, 0])
                P = F("parts")
                wait("xn", b, 1)
                split3(V, dve, xn[:, s, 0], lambda n: xparts[:, s, n], xres[:], P, b)
                V.tensor_copy(dl[:, 0, 0:1], dl[:, 0, 0:1]).then_inc(P.sem, 1)

            def finish(p):
                wait("bc_psum", p, 1)
                V.reciprocal(bc_sb[:, 0:C], bank(2)[:, 0:C]).then_inc(F("bc").sem, 1)
                wait("bc", p, 1)
                V.scalar_tensor_tensor(q_tmp[0:64], bank(3)[0:64, 0:C], gg[0:64], bc_sb[0:64, 0:C], ALU.mult, ALU.mult)
                V.scalar_tensor_tensor(q_tmp[64:128], bank(3)[64:128, C:2 * C], gg[64:128], bc_sb[64:128, 0:C], ALU.mult, ALU.mult).then_inc(F("on").sem, 1)
                wait("on", p, 1)
                V.tensor_tensor(x[:, p], x[:, p], q_tmp[:], ALU.add).then_inc(x_done.sem, 1)

            def first():
                for b in range(2):
                    ln_stats(2, dve, b, None, b)
                for b in range(2):
                    operands(b, b)
                if n_stages > 4:
                    s4_weights_dve(dve)

            def body(p, b, n, s, turn, turn_b):
                if n is not None:
                    ln_stats(2, dve, n, None, s)
                for k in range(4):
                    wait("sq", b, k + 1)
                    V.tensor_reduce(mx2[:, k // 2, 4 * (k % 2):4 * (k % 2) + 4], bank(4 + 2 * (k % 2), 2).rearrange("p (h l) -> p h l", h=4),
                                    axis=AX.X, op=ALU.max, negate=True).then_inc(F("mx").sem, 1)
                wait("mx", b, 4)
                split3(V, dve, mx2[:], lambda n: mxp2[:, :, n], mxr2[:], F("mparts"), b)
                wait("mxT_psum", b, 1)
                V.tensor_copy(mxq2[0:24, :], bank(1).bitcast(BF16)[0:24, 0:256]).then_inc(F("mxT").sem, 1)
                if p is not None:
                    finish(p)
                if n is not None:
                    operands(n, s)

            pipeline(dve, first, body, lambda p, s: finish(p), ahead=2)

        def s2_act(act):
            F = lambda n: f[2, n]

            def sums(p):
                act.wait_ge(F("pv").sem, F("pv").at(p, 1))
                nc.scalar.copy(rd2[64:68], bank(3)[64:68, 0:C])
                nc.scalar.copy(rd2[0:4], bank(3)[0:4, C:2 * C]).then_inc(F("rden").sem, 1)

            def body(p, b, n, s, turn, turn_b):
                if p is not None:
                    sums(p)
                for k in range(4):
                    act.wait_ge(F("st").sem, F("st").at(b, k + 1))
                    nc.scalar.activation(PT[:, 1024 * k:1024 * (k + 1)], bank(4 + 2 * (k % 2), 2), ACT.Exp, scale=0.25).then_inc(F("p").sem, 1)

            pipeline(act, lambda: act.wait_ge(v2_ready, 2), body, lambda p, s: sums(p), ahead=2)

        def s2_pe(pe):
            F = lambda n: f[2, n]
            MM = nc.tensor.matmul

            def wait(n, b, k):
                pe.wait_ge(F(n).sem, F(n).at(b, k))

            def values(b, s, heads):
                ptv = PT[:, 0:4096].rearrange("p (h l q) -> p h l q", h=8, l=2)
                wait("v", b, 1)
                if heads[0] == 0:
                    pe.wait_ge(x_done.sem, b + NB)
                    plain(pe)
                for h in heads:
                    wait("p", b, h // 2 + 1)
                    for lt in range(2):
                        g, o = (v2a[:, s, lt, 68 * h:68 * (h + 1)], bank(3)[0:68, 0:C]) if h < 4 else (v2b[:, s, lt, 128 * (h - 4):128 * (h - 3)], bank(3)[:, C:2 * C])
                        t = MM(o, g, ptv[:, h, lt], start=(h % 4 == 0 and lt == 0), stop=(h % 4 == 3 and lt == 1), skip_group_check=True)
                if heads[-1] == 7:
                    t.then_inc(F("pv").sem, 1)

            def spread(p):
                wait("rden", p, 1)
                MM(bank(2)[:, 0:C], sel2s[0:68], rd2[:], start=True, stop=True).then_inc(F("bc_psum").sem, 1)

            def body(p, b, n, s, turn, turn_b):
                if p is not None:
                    values(p, 1 - s, range(0, 2))
                wait(f"q_loaded{s}", turn_b, 96)
                wait(f"k_loaded{s}", turn_b, 96)
                for k in range(4):
                    if k < 2:
                        wait("p", b, k - 1)
                    else:
                        wait("mx", b, k - 1)
                    qt, h0 = k // 2, 4 * (k % 2)
                    for h in range(4):
                        t = MM(bank(4 + 2 * (k % 2), 2)[:, 256 * h:256 * (h + 1)], qop[:, s, h0 + h, 128 * qt:128 * (qt + 1)], kop[:, s, h0 + h], start=True, stop=True)
                    t.then_inc(F("sq").sem, 1)
                    if p is not None and k == 1:
                        values(p, 1 - s, range(2, 4))
                if p is not None:
                    values(p, 1 - s, range(4, 7))
                wait("mparts", b, 4)
                plain(pe)
                for qt in range(2):
                    t = nc.tensor.transpose(bank(1).bitcast(BF16)[0:24, 128 * qt:128 * (qt + 1)], mxp2[:, qt].rearrange("p r h -> p (r h)"), identb[:])
                t.then_inc(F("mxT_psum").sem, 1)
                if p is not None:
                    values(p, 1 - s, range(7, 8))
                wait("mxT", b, 1)
                for k in range(4):
                    if k < 2:
                        wait("mx", b, 3 + k)
                    else:
                        wait("p", b, k - 1)
                    for j in range(2):
                        h = 2 * k + j
                        for lt in range(2):
                            o = bank(4 + 2 * (k % 2) + j)[:, 256 * lt:256 * (lt + 1)]
                            MM(o, sel2[:, h], mxq2[:], start=True, stop=False)
                            t = MM(o, kop[:, s, h, 128 * lt:128 * (lt + 1)], qop[:, s, h], start=False, stop=True)
                    t.then_inc(F("st").sem, 1)
                    if p is not None and k == 0:
                        spread(p)

            def last(p, s):
                values(p, s, range(8))
                spread(p)

            pipeline(pe, lambda: None, body, last, ahead=2)

        def s4_sp(sp):
            F = lambda n: f[4, n]

            def load(b, s):
                sp.dma_start(ctxT[:, s], a["ctxT"][:, b]).then_inc(F(f"ctx_loaded{s}").sem, 16)
                sp.dma_start(msk[:, s, 0], a["mask"][:, b]).then_inc(F(f"msk_loaded{s}").sem, 16)
                sp.dma_start(msk[:, s, 1], a["maskT"][:, b]).then_inc(F(f"msk_loaded{s}").sem, 16)
            load(0, 0)
            load(1, 1)
            with sp.Fori(0, NB // 2 - 1) as i:
                for u in range(2):
                    b = i * 2 + u
                    sp.wait_ge(F("k_psum").sem, F("k_psum").at(b, 1))
                    sp.wait_ge(F("msk").sem, F("msk").at(b, 2))
                    load(i * 2 + (u + 2), u)

        def s4_pool(pool):
            F = lambda n: f[4, n]
            P = nc.gpsimd
            rs = rstd_step(4, pool)

            def split(b, s, turn, wait=True):
                pool.wait_ge(F(f"msk_loaded{s}").sem, F(f"msk_loaded{s}").at(turn, 32))
                plain(pool)
                if wait:
                    pool.wait_ge(F("st").sem, F("st").at(b, -2))
                    plain(pool)
                P.tensor_copy(mskp[:, s, :, 0], msk[:, s]).then_inc(F("msk").sem, 1)
                pool.wait_ge(F("msk").sem, F("msk").at(b, 1))
                P.tensor_tensor(mskp[:, s, :, 1], msk[:, s], mskp[:, s, :, 0].bitcast(F32), ALU.subtract).then_inc(F("msk").sem, 1)

            rs(0, 0)
            split(0, 0, 0, False)
            rs(1, 1)
            split(1, 1, 0, False)
            with pool.Fori(0, NB // 2 - 1) as i:
                for u in range(2):
                    rs(i * 2 + (u + 2), u)
                    split(i * 2 + (u + 2), u, i + 1)

        def s4_dve(dve):
            F = lambda n: f[4, n]
            V = nc.vector

            def wait(n, b, k):
                dve.wait_ge(F(n).sem, F(n).at(b, k))

            def quantise(b, s):
                ln_apply(4, dve, b, s, xn[:, s, 0])
                wait("xn", b, 1)
                quant(dve, xn[:, s, 0], qx[:], qsc[:, s], qt_f[:], F("quant"), b, 0)

            def scale(b, s):
                wait("q_psum", b, 1)
                D = F("qdve")
                V.scalar_tensor_tensor(q_tmp[:], bank(1)[:, 0:C], qsc[:, s, 1:2], rows4[:, 3], ALU.mult, ALU.mult).then_inc(D.sem, 1)
                for r in range(4):
                    t = V.tensor_tensor(v4[:, s, r].rearrange("p (g w) -> p g w", w=84)[:, :, 0:16], bank(1)[:, C:2 * C].rearrange("p (g r d) -> p r g d", r=4, d=16)[:, r],
                                        rows4[:, 1].rearrange("p (g r d) -> p r g d", r=4, d=16)[:, r], ALU.add)
                t.then_inc(D.sem, 1)
                dve.wait_ge(D.sem, D.at(b, 1))
                V.tensor_tensor(qpad[:, :, 0:16], q_tmp[:].rearrange("p (h d) -> p h d", d=16), rows4[:, 0].rearrange("p (h d) -> p h d", d=16), ALU.add).then_inc(D.sem, 1)

            def finish(p):
                wait("pvT", p, 1)
                pv = bank(3)[:, 0:272].rearrange("p (r m) -> p r m", m=68)
                V.reciprocal(rden[:, 0:16].rearrange("p (r g) -> p r g", g=4), pv[:, :, 64:68]).then_inc(F("rden").sem, 1)
                wait("rden", p, 1)
                ov = o_n[:].rearrange("p q h -> p (q h)")
                for r in range(4):
                    t = V.tensor_tensor(ov.rearrange("p (g r d) -> p r g d", r=4, d=16)[:, r], pv[:, r, 0:64].rearrange("p (g d) -> p g d", d=16),
                                        rden[:, 4 * r:4 * r + 4].unsqueeze(2).to_broadcast([128, 4, 16]), ALU.mult)
                t.then_inc(F("on").sem, 1)
                wait("on", p, 1)
                quant(dve, ov, qo[:], osc[:], qt_f[:], F("oquant"), p, 0)

            def update(p, n):
                if n is not None:
                    wait("qdve", n, 3)
                wait("y", p, 1)
                fin = F("fin")
                V.scalar_tensor_tensor(q_tmp[:], bank(3)[:, 0:C], osc[:, 1:2], rows4[:, 4], ALU.mult, ALU.mult).then_inc(fin.sem, 1)
                wait("fin", p, 1)
                V.tensor_tensor(q_tmp[:], q_tmp[:], rows4[:, 2], ALU.add).then_inc(fin.sem, 1)
                wait("fin", p, 2)
                V.tensor_tensor(x[:, p], x[:, p], q_tmp[:], ALU.add).then_inc(x_done.sem, 1)

            def first():
                ln_stats(4, dve, 0, None, 0)
                quantise(0, 0)
                scale(0, 0)

            def body(p, b, n, s, turn, turn_b):
                if n is not None:
                    ln_stats(4, dve, n, None, 1 - s)
                for k in range(2):
                    wait("sq", b, k + 1)
                    V.tensor_reduce(mx4[:, 8 * k:8 * k + 8], bank(4 + 2 * k, 2).rearrange("p (h l) -> p h l", h=8), axis=AX.X, op=ALU.max, negate=True).then_inc(F("mx").sem, 1)
                wait("mx", b, 2)
                split3(V, dve, mx4[:], lambda r: mxp4[:, r], mxr4[:], F("mparts"), b)
                if n is not None:
                    quantise(n, 1 - s)
                wait("mxT_psum", b, 1)
                V.tensor_copy(mxq4[0:48, :], bank(2).bitcast(BF16)[0:48, 0:128]).then_inc(F("mxT").sem, 1)
                if p is not None:
                    finish(p)
                if n is not None:
                    scale(n, 1 - s)
                if p is not None:
                    update(p, n)

            def last(p, s):
                finish(p)
                update(p, None)

            pipeline(dve, first, body, last)

        def s4_act(act):
            F = lambda n: f[4, n]
            A = nc.scalar

            def wait(n, b, k):
                act.wait_ge(F(n).sem, F(n).at(b, k))

            def copy_x(b):
                wait("xT_psum", b, 1)
                A.copy(qxT[:], bank(0).bitcast(BF16)[:, 0:256].rearrange("p (c t) -> p c t", c=2)).then_inc(F("xT").sem, 1)

            def copy_k(b, s):
                wait("k_psum", b, 1)
                for g in range(4):
                    A.activation(kT4[:, s, g], bank(2)[:, 128 * g:128 * (g + 1)], ACT.Identity, bias=bkc[:, g:g + 1]).then_inc(F("k").sem, 1)

            def copy_q(b, s):
                wait("qT_psum", b, 1)
                A.copy(qT4[:, s], bank(0).rearrange("p (g t) -> p g t", g=4)).then_inc(F("qT").sem, 1)

            def copy_o(p):
                wait("oT_psum", p, 1)
                A.copy(qoT[:], bank(3).bitcast(BF16)[:, 512:768].rearrange("p (c t) -> p c t", c=2)).then_inc(F("oT").sem, 1)

            def first():
                copy_x(0)
                copy_k(0, 0)
                copy_q(0, 0)

            def copy_values(p):
                wait("pv", p, 1)
                A.copy(bc_sb[0:68], bank(3)[0:68]).then_inc(F("pvc").sem, 1)

            def body(p, b, n, s, turn, turn_b):
                if p is not None:
                    copy_values(p)
                for k in range(2):
                    wait("st", b, k + 1)
                    A.activation(PT[:, 1024 * k:1024 * (k + 1)], bank(4 + 2 * k, 2), ACT.Exp).then_inc(F("p").sem, 1)
                    if k == 0 and n is not None:
                        copy_x(n)
                if n is not None:
                    copy_k(n, 1 - s)
                if p is not None:
                    copy_o(p)
                if n is not None:
                    copy_q(n, 1 - s)

            pipeline(act, first, body, lambda p, s: (copy_values(p), copy_o(p)))

        def s4_pe(pe):
            F = lambda n: f[4, n]
            MM = nc.tensor.matmul

            def wait(n, b, k):
                pe.wait_ge(F(n).sem, F(n).at(b, k))

            def transpose_x(b):
                wait("quant", b, 6)
                for c in range(2):
                    t = nc.tensor.transpose(bank(0).bitcast(BF16)[:, 128 * c:128 * (c + 1)], qx[:, 128 * c:128 * (c + 1)], identb[:])
                t.then_inc(F("xT_psum").sem, 1)

            def project(b, s, turn):
                wait(f"ctx_loaded{s}", turn, 16)
                for c in range(2):
                    MM(bank(1)[:, C:2 * C], ctxT[:, s, c], wvT[:, c], start=(c == 0), stop=(c == 1))
                wait("xT", b, 1)
                for c in range(2):
                    t = MM(bank(1)[:, 0:C], qxT[:, c], qwT[:, 0, c], start=(c == 0), stop=(c == 1))
                t.then_inc(F("q_psum").sem, 1)
                for g in range(4):
                    for c in range(2):
                        t = MM(bank(2)[:, 128 * g:128 * (g + 1)], wkT[:, c, g], ctxT[:, s, c], start=(c == 0), stop=(c == 1))
                t.then_inc(F("k_psum").sem, 1)

            def transpose_q(b):
                wait("qdve", b, 3)
                qv = qpad[:].rearrange("p h d -> p (h d)")
                for g in range(4):
                    t = nc.tensor.transpose(bank(0)[:, 128 * g:128 * (g + 1)], qv[:, 128 * g:128 * (g + 1)], ident[:])
                t.then_inc(F("qT_psum").sem, 1)

            def add_mask(s, which, r):
                for part in range(2):
                    MM(bank(4 + r), ident_r[:], mskp[:, s, which, part].unsqueeze(1).to_broadcast([128, 4, T]), start=(part == 0), stop=False, skip_group_check=True)

            def values(p, s):
                ptv = PT[:, 0:2048].rearrange("p (r g q) -> p r g q", r=4, g=4)
                pe.wait_ge(x_done.sem, p + 2 * NB)
                plain(pe)
                for r in range(4):
                    wait("p", p, r // 2 + 1)
                    for g in range(4):
                        t = MM(bank(3)[0:68, 128 * r:128 * (r + 1)], v4[:, s, r, 68 * g:68 * (g + 1)], ptv[:, r, g], start=(r == 0 and g == 0), stop=(g == 3), skip_group_check=True)
                t.then_inc(F("pv").sem, 1)

            def transpose_values(p):
                wait("pvc", p, 1)
                plain(pe)
                for r in range(4):
                    t = nc.tensor.transpose(bank(3)[:, 68 * r:68 * (r + 1)], bc_sb[0:68, 128 * r:128 * (r + 1)], ident[0:68, 0:68])
                t.then_inc(F("pvT").sem, 1)

            def transpose_o(p):
                wait("oquant", p, 6)
                for c in range(2):
                    t = nc.tensor.transpose(bank(3).bitcast(BF16)[:, 512 + 128 * c:512 + 128 * (c + 1)], qo[:, 128 * c:128 * (c + 1)], identb[:])
                t.then_inc(F("oT_psum").sem, 1)

            def output(p):
                wait("oT", p, 1)
                for c in range(2):
                    t = MM(bank(3)[:, 0:C], qoT[:, c], qwT[:, 1, c], start=(c == 0), stop=(c == 1))
                t.then_inc(F("y").sem, 1)

            def first():
                transpose_x(0)
                project(0, 0, 0)
                transpose_q(0)

            def body(p, b, n, s, turn, turn_b):
                wait("msk", b, 2)
                for k in range(2):
                    wait("p", b, k - 1)
                    for r in (2 * k, 2 * k + 1):
                        add_mask(s, 0, r)
                    if k == 0:
                        wait("k", b, 4)
                        wait("qT", b, 1)
                    for g in range(4):
                        for r in (2 * k, 2 * k + 1):
                            t = MM(bank(4 + r)[:, 128 * g:128 * (g + 1)], qT4[32 * r:32 * r + 16, s, g], kT4[32 * r:32 * r + 16, s, g], start=False, stop=True, skip_group_check=True)
                    t.then_inc(F("sq").sem, 1)
                if p is not None:
                    values(p, 1 - s)
                wait("mparts", b, 4)
                plain(pe)
                nc.tensor.transpose(bank(2).bitcast(BF16)[0:48, 0:128], mxp4[:].rearrange("p r h -> p (r h)"), identb[:]).then_inc(F("mxT_psum").sem, 1)
                for k in range(2):
                    wait("mx", b, k + 1)
                    for r in (2 * k, 2 * k + 1):
                        add_mask(s, 1, r)
                    for r in (2 * k, 2 * k + 1):
                        if r == 0:
                            wait("mxT", b, 1)
                        for g in range(4):
                            MM(bank(4 + r)[:, 128 * g:128 * (g + 1)], sel4[:, 4 * r + g], mxq4[:], start=False, stop=False, skip_group_check=True)
                    for g in range(4):
                        for r in (2 * k, 2 * k + 1):
                            t = MM(bank(4 + r)[:, 128 * g:128 * (g + 1)], kT4[32 * r:32 * r + 16, s, g], qT4[32 * r:32 * r + 16, s, g], start=False, stop=True, skip_group_check=True)
                    t.then_inc(F("st").sem, 1)
                    if k == 0 and n is not None:
                        transpose_x(n)
                    if k == 0 and p is not None:
                        transpose_values(p)
                if n is not None:
                    project(n, 1 - s, turn)
                if p is not None:
                    transpose_o(p)
                if n is not None:
                    transpose_q(n)
                if p is not None:
                    output(p)

            def last(p, s):
                values(p, s)
                transpose_values(p)
                transpose_o(p)
                output(p)

            pipeline(pe, first, body, last)

        def s6_sp(sp):
            F = lambda n: f[6, n]

            def load(b, s):
                sp.dma_start(ctxT[:, s], a["ctxT"][:, b]).then_inc(F(f"ctx_loaded{s}").sem, 16)

            def load_rows(b, s):
                sp.dma_start(cnat[:, s], a["ctx"][:, b]).then_inc(F(f"rows_loaded{s}").sem, 16)

            def load_w(b, s):
                sp.dma_start(w7_raw[:, s], a["w7"][:, bass.ds(b * W7C, W7C)]).then_inc(F(f"w7_raw{s}").sem, 16)
            for b in range(2):
                load(b, b)
                load_rows(b, b)
                load_w(b, b)
            stage_over(sp, 6)
            with sp.Fori(0, NB // 2 - 1) as i:
                for u in range(2):
                    sp.wait_ge(F("s_psum").sem, F("s_psum").at(i * 2 + u, 1))
                    load_rows(i * 2 + (u + 2), u)
                    sp.wait_ge(F("w7_low").sem, F("w7_low").at(i * 2 + u, 1))
                    load_w(i * 2 + (u + 2), u)
                    sp.wait_ge(F("y").sem, F("y").at(i * 2 + u, 1))
                    load(i * 2 + (u + 2), u)

        sgm = PT[:, 5120:6144].rearrange("p (s n m) -> p s n m", s=2, n=2)

        def s6_dve(dve):
            F = lambda n: f[6, n]

            def norm(b, s):
                ln_stats(6, dve, b, None, s)
                ln_apply(6, dve, b, s, xn[:, s, 0])

            def first():
                norm(0, 0)
                norm(1, 1)

            def body(p, b, n, s, turn, turn_b):
                if n is not None:
                    dve.wait_ge(F("s_psum").sem, F("s_psum").at(b, 1))
                    norm(n, s)
                dve.wait_ge(F("w7_high").sem, F("w7_high").at(b, 1))
                nc.vector.tensor_tensor(w7l[:, bass.ds(b * W7C, W7C)], w7_raw[:, s], w7h[:, bass.ds(b * W7C, W7C)].bitcast(F32), ALU.subtract).then_inc(F("w7_low").sem, 1)
                dve.wait_ge(F("y").sem, F("y").at(b, 1))
                nc.vector.scalar_tensor_tensor(x[:, b], bank(4 + s)[:, 0:C], gates[:, 3:4], x[:, b], ALU.mult, ALU.add).then_inc(x_done.sem, 1)

            pipeline(dve, first, body, lambda p, s: None, ahead=2)

        def s6_act(act):
            F = lambda n: f[6, n]
            with act.Fori(0, NB // 2) as i:
                for s in range(2):
                    b = i * 2 + s
                    act.wait_ge(F("s_psum").sem, F("s_psum").at(b, 1))
                    nc.scalar.activation(sgm[:, s], bank(2 + s).rearrange("p (n m) -> p n m", n=2), ACT.Sigmoid, scale=float(T) ** -0.5).then_inc(F("s").sem, 1)
                    act.wait_ge(F(f"w7_raw{s}").sem, F(f"w7_raw{s}").at(i, 16))
                    nc.scalar.copy(w7h[:, bass.ds(b * W7C, W7C)], w7_raw[:, s]).then_inc(F("w7_high").sem, 1)

        def s6_pe(pe):
            F = lambda n: f[6, n]
            MM = nc.tensor.matmul

            def scores(b, s, turn):
                pe.wait_ge(F("xn").sem, F("xn").at(b, 1))
                pe.wait_ge(F(f"rows_loaded{s}").sem, F(f"rows_loaded{s}").at(turn, 16))
                for n in range(2):
                    t = MM(bank(2 + s)[:, C * n:C * (n + 1)], xn[:, s, 0, 128 * n:128 * (n + 1)], cnat[:, s], start=True, stop=True)
                t.then_inc(F("s_psum").sem, 1)

            def body(p, b, n, s, turn, turn_b):
                if n is not None:
                    scores(n, 1 - s, turn)
                pe.wait_ge(F(f"ctx_loaded{s}").sem, F(f"ctx_loaded{s}").at(turn_b, 16))
                pe.wait_ge(F("s").sem, F("s").at(b, 1))
                pe.wait_ge(x_done.sem, b + (3 * NB - 1))
                for n in range(2):
                    t = MM(bank(4 + s)[:, 0:C], ctxT[:, s, n], sgm[:, s, n], start=(n == 0), stop=(n == 1))
                t.then_inc(F("y").sem, 1)

            pipeline(pe, lambda: scores(0, 0, 0), body, lambda p, s: None)

        c_in = [sem("c_in0"), sem("c_in1")]
        c_parts = Flag(sem("c_parts"), 4)
        c_out = [sem("c_out0"), sem("c_out1")]

        def ctx_pipeline(pool, fetch):
            rs = rstd_step(0, pool)

            def one(b, u, turn, first, last):
                rs(b, u)
                pool.wait_ge(c_in[u], turn * 16 + 16)
                plain(pool)
                if not first:
                    pool.wait_ge(c_out[u], turn * 16)
                split3(nc.gpsimd, pool, cnat[:, u], lambda n: cparts[:, u, n], cres[:], c_parts, b)
                pool.wait_ge(c_parts.sem, c_parts.at(b, 4))
                pool.dma_start(kscr[b].rearrange("r p n -> p r n"), cparts[:, u]).then_inc(c_out[u], 16)
                if not last:
                    fetch(b + 2, u)
            for u in range(2):
                one(u, u, 0, True, False)
            with pool.Fori(1, NB // 2 - 1) as i:
                for u in range(2):
                    one(i * 2 + u, u, i, False, False)
            for u in range(2):
                one(NB - 2 + u, u, NB // 2 - 1, False, True)


        @block.sync
        def _(sp):
            sp.dma_start(x[:, 0:2], a["x"][:, 0:2]).then_inc(loaded_x[0], 16)
            for t, name in ((w0x, "w0x"), (w0c, "w0c")):
                sp.dma_start(t, a[name]).then_inc(loaded_c, 16)
            s0_sp_first(sp)
            sp.wait_ge(loaded_c, LOADS_0)
            sp.dma_start(ext0[:], a["ext0"].bitcast(BF16)).then_inc(loaded_s0, 16)
            sp.dma_start(w0o, a["w0o"]).then_inc(loaded_s0, 16)
            sp.dma_start(x[:, 2:NB], a["x"][:, 2:NB]).then_inc(loaded_x[1], 16)
            sp.dma_start(arena[:, 0:10240], a["w13"]).then_inc(w_loaded[1], 16)
            for t, name in ((wr, "wr"), (iota8, "iota8"), (sel2s, "sel2s"), (sbias, "sbias"), (bkc, "bkc"), (fb, "fb")):
                sp.dma_start(t[:], a[name]).then_inc(loaded_later, 16)
            sp.dma_start(rows4[:, 0:3], a["rows4"]).then_inc(loaded_later, 16)
            sp.dma_start(sel2[:], a["sel2"].bitcast(BF16)).then_inc(loaded_later, 16)
            s0_sp(sp)
            if n_stages > 1:
                stage_over(sp, 1)
                sp.dma_start(wq_n, a["w4n"].rearrange("p (w o c) -> p w o c", w=2, o=2)).then_inc(w_loaded[4], 16)
            if n_stages > 2:
                s2_sp(sp)
                sp.dma_start(wkT, a["wkT"]).then_inc(w_loaded[3], 16)
                sp.dma_start(wvT, a["wvT"]).then_inc(w_loaded[3], 16)
                sp.dma_start(sel4, a["sel4"].bitcast(BF16)).then_inc(w_loaded[3], 16)
            if n_stages > 3:
                stage_over(sp, 3)
                sp.dma_start(factors, a["w5"]).then_inc(w_loaded[5], 16)
            if n_stages > 4:
                stage_over(sp, 4)
                s4_sp(sp)
                stage_over(sp, 5)
            if n_stages > 6:
                s6_sp(sp)
            done = sem("stored")
            for q in range(4):
                if n_stages == 8:
                    sp.wait_ge(f[7, "acc"].sem, f[7, "acc"].at(2 * q + 2, 0))
                else:
                    sp.wait_ge(*ends[n_stages - 1])
                sp.dma_start(out[:, 4 * q:4 * q + 4], x[:, 4 * q:4 * q + 4]).then_inc(done, 16)
            sp.wait_ge(done, 64)

        @block.scalar
        def _(act):
            for t, name in ((ident, "ident"), (gates, "gates"), (sel0, "sel0")):
                act.dma_start(t[:], a[name]).then_inc(loaded_c, 16)
            for t, name in ((q_const, "q_const"), (k_const, "k_const"), (ohq0, "ohq0"), (mxq0, "mxq0")):
                act.dma_start(t[:], a[name].bitcast(BF16)).then_inc(loaded_c, 16)
            act.wait_ge(loaded_c, LOADS_0)
            A = nc.scalar
            A.activation(gates[:, 0:8], gates[:, 0:8], ACT.Tanh).then_inc(gates_ready, 1)
            for s in range(2):
                A.copy(q_parts[:, s, :, 48:64], q_const[:].rearrange("p (h r) -> p h r", h=H0))
                A.copy(k_parts[:, s, :, :, 48:64], k_const[:].rearrange("p (c h r) -> p c h r", c=2, h=HK0)).then_inc(gates_ready, 1)
            give(act, [(0, "p")])
            s0_act(act)
            for s, prog in enumerate((None, lambda: glu_act(1, act), lambda: s2_act(act), lambda: s3_act(act), lambda: s4_act(act),
                                      lambda: s5_act(act), lambda: s6_act(act), lambda: glu_act(7, act))):
                if 0 < s < n_stages:
                    stage_over(act, s)
                    if s == 1:
                        act.wait_ge(loaded_later, LOADS_1)
                    prog()

        @block.vector
        def _(dve):
            V = nc.vector
            V.memset(minus_half[:], -0.5)
            V.memset(v0[:, 0], 0.0)
            V.memset(qpad[:], 0.0)
            V.memset(onesf[:], 1.0)
            V.memset(ones96[:], 1.0)
            V.memset(mxq2[:], 0.0)
            V.memset(mxq4[:], 0.0)
            V.memset(dl[:], 0.0)
            V.memset(th[:], 0.0).then_inc(zero_ready, 1)
            dve.wait_ge(zero_ready, 2)
            for h in range(HK0):
                V.memset(v0[:, :, :, 73 * h + 64:73 * h + 65], 1.0)
            give(dve, [(s, n) for s in (1, 3, 5, 7) for n in ("h", "acc", "lg")])
            dve.wait_ge(loaded_c, LOADS_0)
            dve.wait_ge(loaded_x[0], 16)
            G = prep_w
            V.tensor_copy(identb[:], ident[:])
            dve.wait_ge(gates_ready, 1)
            V.tensor_scalar(half[:, 0], gates[:], 0.5, None, ALU.mult)
            V.tensor_scalar(half[:, 1], gates[:], -0.5, None, ALU.mult)
            V.tensor_scalar(gs5[:], gates[:, 6:7], float(8.0 ** -0.5), None, ALU.mult)
            V.tensor_tensor(gg[:], gates[:, 1:2], gates[:, 8:9], ALU.mult).then_inc(G.sem, 1)
            dve.wait_ge(G.sem, 1)
            s0_dve(dve)
            if n_stages > 1:
                stage_over(dve, 1)
                dve.wait_ge(loaded_later, LOADS_1)
                if n_stages > 2:
                    for u in range(2):
                        dve.wait_ge(c_out[u], 16 * (NB // 2))
                glu_dve(1, dve)
            if n_stages > 2:
                stage_over(dve, 2)
                s2_dve(dve)
            if n_stages > 3:
                stage_over(dve, 3)
                s3_dve(dve)
            if n_stages > 4:
                stage_over(dve, 4)
                V.tensor_copy(ident_r[:], ident[:]).then_inc(G.sem, 1)
                dve.wait_ge(G.sem, 2)
                dve.wait_ge(v4_ready, 2)
                s4_dve(dve)
            if n_stages > 5:
                stage_over(dve, 5)
                V.tensor_scalar(fb[:], fb[:], gates[:, 6:7], None, ALU.mult).then_inc(G.sem, 1)
                dve.wait_ge(G.sem, 3)
                s5_dve(dve)
            if n_stages > 6:
                stage_over(dve, 6)
                s6_dve(dve)
            if n_stages > 7:
                stage_over(dve, 7)
                glu_dve(7, dve)

        @block.gpsimd
        def _(pool):
            P = nc.gpsimd
            P.memset(v0[:, 1], 0.0).then_inc(zero_ready, 1)
            pool.wait_ge(zero_ready, 2)
            if n_stages > 3:
                pool.dma_start(eb_n[:], a["eb"]).then_inc(eb_in, 16)
                P.memset(ebias[:].bitcast(F32), 0.0).then_inc(eb_split.sem, 1)
                pool.wait_ge(eb_in, 16)
                split3(P, pool, eb_n[:], lambda r: eb_p[:, r], eb_r[:], eb_split, 0)
                pool.wait_ge(eb_split.sem, 5)
                pool.dma_start(escr.rearrange("r (p n) -> p r n", p=128), eb_p[:]).then_inc(eb_out, 16)
                pool.wait_ge(eb_out, 16)
                for r in range(3):
                    pool.dma_start(ebias[32 * r:32 * r + 1], escr[r:r + 1]).then_inc(eb_loaded, 16)
            if n_stages > 2:
                def fetch(b, u):
                    pool.dma_start(cnat[:, u], a["ctx"][:, b]).then_inc(c_in[u], 16)
                fetch(0, 0)
                fetch(1, 1)
                ctx_pipeline(pool, fetch)
            for s in range(1 if n_stages > 2 else 0, n_stages):
                stage_over(pool, s)
                if s == 2:
                    s2_pool(pool)
                elif s == 4:
                    s4_pool(pool)
                    pool.wait_ge(w_loaded[5], 16)
                    fv = factors.rearrange("p (r c n) -> p r c n", r=8, c=NC)
                    P.tensor_copy(fsum, fv[:, 0]).then_inc(fsum_ready, 1)
                    for k in range(1, 8):
                        pool.wait_ge(fsum_ready, k)
                        P.tensor_tensor(fsum, fsum, fv[:, k], ALU.add).then_inc(fsum_ready, 1)
                else:
                    pool_stage(s, pool)
                if s == 3:
                    nc.gpsimd.memset(v4, 0.0).then_inc(v4_ready, 1)
                    pool.wait_ge(v4_ready, 1)
                    for g in range(4):
                        t = nc.gpsimd.memset(v4[:, :, :, 69 * g + 64:69 * g + 65], 1.0)
                    t.then_inc(v4_ready, 1)

        @block.tensor
        def _(pe):
            pe.wait_ge(loaded_c, LOADS_0)
            pe.wait_ge(prep_w.sem, 1)
            give(pe, [(1, "y")])
            s0_pe(pe)
            for s, prog in enumerate((None, lambda: glu_pe(1, pe), lambda: (s4_weights_pe(pe) if n_stages > 4 else None, s2_pe(pe)), lambda: s3_pe(pe), lambda: s4_pe(pe),
                                      lambda: s5_pe(pe), lambda: s6_pe(pe), lambda: glu_pe(7, pe))):
                if 0 < s < n_stages:
                    stage_over(pe, s)
                    if s in (1, 3):
                        pe.wait_ge(w_loaded[1], 16)
                        pe.wait_ge(loaded_later, LOADS_1)
                    if s == 3:
                        pe.wait_ge(eb_loaded, 48)
                    if s == 4:
                        pe.wait_ge(w_loaded[3], 48)
                    if s == 5:
                        pe.wait_ge(fsum_ready, 8)
                    if s == 7:
                        pe.wait_ge(f[6, "w7_low"].sem, NB)
                    prog()


LOADS_0 = 16 * (2 + 3 + 4)
LOADS_1 = 16 * 8


def layouts(inp):
    def bf16(v):
        u = np.ascontiguousarray(v, np.float32).view(np.uint32).astype(np.uint64)
        return ((u + 0x7FFF + ((u >> 16) & 1)) >> 16).astype(np.uint16)

    def back(bits):
        return (bits.astype(np.uint32) << 16).view(np.float32)

    def chunks(w):
        return np.ascontiguousarray(w.reshape(NC, 128, -1).transpose(1, 0, 2))

    d = {}
    d["x"] = np.ascontiguousarray(inp["x"].transpose(1, 0, 2))
    d["ctxT"] = np.ascontiguousarray(inp["ctx_2048"].reshape(NB, T, NC, 128).transpose(3, 0, 2, 1))
    d["ident"] = np.eye(128, dtype=np.float32)
    g = np.concatenate([inp["g_xattn"], inp["g_ffn"], inp["L1_xattn_gamma"].reshape(1)])
    d["gates"] = np.ascontiguousarray(np.broadcast_to(g, (128, 9)))
    wq = inp["L0_xattn_Wq"].reshape(2 * C, HK0, G0, D0).transpose(0, 2, 1, 3).reshape(2 * C, C)
    d["w0x"] = chunks(np.concatenate([wq[C:], inp["L0_xattn_Wk"], inp["L0_xattn_Wv"]], 1))
    d["w0c"] = chunks(np.concatenate([inp["L0_xattn_Wsk"], inp["L0_xattn_Wsv"], wq[:C]], 1))
    d["w0o"] = np.ascontiguousarray(inp["L0_xattn_Wo"].reshape(HK0, G0, D0, C).transpose(0, 2, 1, 3).reshape(64, G0, C))
    sel = np.zeros((128, 64), np.float32)
    sel[64:72] = np.repeat(np.eye(HK0), D0, 1)
    d["sel0"] = sel
    ext = np.zeros((128, HK0, sum(2 * k for k in KEYS_T)), np.float32)
    o = 0
    for qb in range(NQB):
        for c, win in ((0, W_SSM), (1, W_ATT)):
            m = KEYS_T[qb]
            for hk in range(HK0):
                for part in range(3):
                    ext[32 * part + 8 * qb + hk, hk, o:o + m] = 1.0
            delta = (QB * qb + np.arange(QB))[:, None] - np.arange(m)[None, :]
            ext[96:128, :, o:o + m] = np.where((delta >= 0) & (delta < win), 0.0, MASKED)[:, None, :]
            o += m
    d["ext0"] = bf16(ext.reshape(128, -1))
    oh = np.zeros((128, 128), np.float32)
    oh[96:128] = np.tile(np.eye(QB), (1, G0))
    d["mxq0"] = bf16(oh)
    d["ohq0"] = bf16(oh)
    slopes = np.power(np.float32(2.0), -8.0 * np.arange(H0, dtype=np.float32) / H0).astype(np.float32)
    qc = np.zeros((128, H0, R0), np.float32)
    rest = slopes.copy()
    for part in range(3):
        p = back(bf16(rest))
        qc[:, :, 48 + part] = p.reshape(HK0, G0).T.reshape(-1)
        rest = rest - p
    kc = np.zeros((128, 2, HK0, R0), np.float32)
    kc[:, :, :, 48:51] = (np.arange(T) - 64)[:, None, None, None]
    d["q_const"], d["k_const"] = bf16(qc[:, :, 48:].reshape(128, -1)), bf16(kc[..., 48:].reshape(128, -1))
    def units(gate, value, down):
        up = np.stack([gate, value], 2).reshape(-1, NC, 128, 2, 128).transpose(2, 0, 1, 3, 4)
        return up.reshape(128, -1), down.transpose(1, 0, 2).reshape(128, -1)

    up, down = units(inp["L0_ffn_w1"], inp["L0_ffn_w2"], inp["L0_ffn_w3"])
    d["w13"] = np.ascontiguousarray(np.concatenate([up, down, chunks(inp["L1_ffn_expert_w"].transpose(2, 0, 1).reshape(C, -1)).reshape(128, -1)], 1))
    w12 = inp["L3_ffn_w12"].transpose(0, 2, 1)
    s1, s2 = (inp[n].reshape(8, 128, C).transpose(0, 2, 1) for n in ("L3_ffn_sw1", "L3_ffn_sw2"))
    down = np.concatenate([inp["L3_ffn_w3"].transpose(0, 2, 1), inp["L3_ffn_sw3"].T.reshape(8, 128, C)])
    d["w7"] = np.ascontiguousarray(np.concatenate(units(np.concatenate([w12[:, :, :128], s1]), np.concatenate([w12[:, :, 128:], s2]), down), 1))
    d["wr"] = np.ascontiguousarray(np.stack([chunks(inp[n].T) for n in ("L0_ffn_router_w", "L1_ffn_gate_w", "L3_ffn_router_w")], 1))
    d["iota8"] = np.ascontiguousarray(np.broadcast_to(np.arange(8, dtype=np.float32), (128, 8)))
    d["sbias"] = np.ascontiguousarray(np.broadcast_to(inp["L3_ffn_expert_bias"], (128, 8)))
    d["eb"] = np.ascontiguousarray(inp["L1_ffn_expert_b"].reshape(128, 16))
    d["ctx"] = np.ascontiguousarray(inp["ctx_2048"].transpose(1, 0, 2))
    d["ctxT16"] = np.ascontiguousarray(inp["ctx_2048"].reshape(NB, 8, 16, 2, 128).transpose(4, 0, 3, 1, 2).reshape(128, NB, 256))
    sel = np.zeros((68, 128), np.float32)
    sel[0:4, 64:] = np.repeat(np.eye(4), 16, 1)
    sel[64:, 0:64] = np.repeat(np.eye(4), 16, 1)
    d["sel2s"] = sel
    sel = np.zeros((96, 8, 128), np.float32)
    for h in range(8):
        sel[h:24:8, h] = 1.0
    d["sel2"] = bf16(sel)
    wk = np.zeros((C, 4, 4, 32), np.float32)
    wk[..., :16] = inp["L2_xattn_wk"].T.reshape(C, 4, 4, 16)
    d["wkT"] = np.ascontiguousarray(chunks(wk.reshape(C, -1)).reshape(128, NC, 4, 128))
    bk = np.zeros((4, 4, 32), np.float32)
    bk[..., :16] = inp["L2_xattn_bk"].reshape(4, 4, 16)
    d["bkc"] = np.ascontiguousarray(bk.reshape(4, 128).T)
    d["wvT"] = chunks(inp["L2_xattn_wv"].T)
    d["rows4"] = np.ascontiguousarray(np.broadcast_to(np.stack([inp["L2_xattn_bq"], inp["L2_xattn_bv"], inp["L2_xattn_bo"]]), (128, 3, C)))
    d["w4n"] = np.ascontiguousarray(np.stack([inp[n].reshape(2, 128, C).transpose(1, 0, 2) for n in ("L2_xattn_wq", "L2_xattn_wo")], 1).reshape(128, -1))
    d["mask"] = np.ascontiguousarray(inp["mask_BxSxS2_ff0"].transpose(1, 0, 2))
    d["maskT"] = np.ascontiguousarray(inp["mask_BxSxS2_ff0"].transpose(2, 0, 1))
    sel = np.zeros((96, 16, 128), np.float32)
    for h in range(16):
        sel[h:48:16, h] = 1.0
    d["sel4"] = bf16(sel)
    d["w5"] = np.ascontiguousarray(inp["L2_ffn_factors"].reshape(8, NC, 128, C).transpose(2, 0, 1, 3).reshape(128, -1))
    d["fb"] = np.ascontiguousarray(np.broadcast_to(inp["L2_ffn_bias"], (128, C)))
    return d


def kernel(**inputs):
    import numpy as _np
    import concourse.bacc as _bacc
    from concourse import mybir as _mybir
    from concourse.bass_utils import run_bass_kernel_spmd as _run

    nc = _bacc.Bacc("TRN2", target_bir_lowering=False, num_devices=1)
    arrays, a = {}, {}
    for name, v in layouts(inputs).items():
        arrays["in_" + name] = v
        a[name] = nc.dram_tensor("in_" + name, v.shape, _mybir.dt.from_np(v.dtype), kind="ExternalInput").ap()
    out = nc.dram_tensor("out", (T, NB, C), F32, kind="ExternalOutput").ap()
    bass_program(nc, a, out)
    r = _run(nc, [arrays], core_ids=[0])
    return _np.ascontiguousarray(r.results[0]["out"].transpose(1, 0, 2))
```
